# Optimizing a Trainium2 kernel written in Bass

```python
import numpy as np
import jax
import jax.numpy as jnp

def _softmax(x, axis=-1):
    return jax.nn.softmax(x, axis=axis)

def _gelu(x):
    return jax.nn.gelu(x, approximate=True)

def _silu(x):
    return jax.nn.silu(x)

def _sigmoid(x):
    return jax.nn.sigmoid(x)

def _layernorm(x, axis=-1, eps=1e-05):
    m = jnp.mean(x, axis=axis, keepdims=True)
    v = jnp.var(x, axis=axis, keepdims=True)
    return (x - m) / jnp.sqrt(v + eps)

def _scatter_add(tgt, idx, src, axis=0):
    return tgt.at[idx].add(src)

def _segment_sum(src, seg, n):
    return jax.ops.segment_sum(src, seg, n)
kernel_name = 'mk_pixart_resid_d4_seqx_r8_16d1ff'

def setup_inputs(seed: int=0):
    np.random.seed(seed)
    _w = jnp.asarray

    def _rec_inputs():
        import jax
        import jax.numpy as jnp
        _rk = jax.random.key(seed)
        x = -0.0002928 + 1 * jax.random.normal(jax.random.fold_in(_rk, 1), (16, 56, 128), jnp.float32)
        _lenS = 56 - jax.random.randint(jax.random.fold_in(_rk, 7), (16,), 0, max(1, 56 // 4) + 1, jnp.int32)
        _lenS2 = 1500 - jax.random.randint(jax.random.fold_in(_rk, 8), (16,), 0, max(1, 1500 // 4) + 1, jnp.int32)
        cond_1024 = 0.0061147 + 1.02565 * jax.random.normal(jax.random.fold_in(_rk, 11), (16, 128), jnp.float32)
        _ctx_1024P = jax.random.normal(jax.random.fold_in(_rk, 12), (16, 16, 128), jnp.float32)
        _ctx_1024c = jax.random.dirichlet(jax.random.fold_in(_rk, 512), 0.3 * jnp.ones((16,), jnp.float32), (16, 1500))
        _ctx_1024t = jnp.einsum('bsk,bkd->bsd', _ctx_1024c, _ctx_1024P)
        _ctx_1024t = _ctx_1024t * jax.lax.rsqrt(jnp.mean(jnp.square(_ctx_1024t)) + 1e-12) * 0.953939
        ctx_1024 = 0.00086875 + 0.999764 * (_ctx_1024t + 0.3 * jax.random.normal(jax.random.fold_in(_rk, 612), (16, 1500, 128), jnp.float32))
        _validS = jnp.arange(56)[None, :] < _lenS[:, None]
        _validS2 = jnp.arange(1500)[None, :] < _lenS2[:, None]
        _causal = jnp.tril(jnp.ones((56, 56), dtype=bool))
        mask_BxS_bf0 = jnp.logical_not(jnp.ones((16, 56), dtype=bool))
        mask_BxS2_bf0 = jnp.logical_not(jnp.ones((16, 1500), dtype=bool))
        return (x, cond_1024, ctx_1024, mask_BxS_bf0, mask_BxS2_bf0)
    x, cond_1024, ctx_1024, mask_BxS_bf0, mask_BxS2_bf0 = _rec_inputs()

    def _L0_xcond_setup():
        import jax, jax.numpy as jnp
        import numpy as np
        NL, D, H, DFF = (6, 128, 16, 512)
        HD = D // H

        def _rope(x):
            L = x.shape[1]
            half = HD // 2
            inv = 1.0 / 10000.0 ** (jnp.arange(half, dtype=jnp.float32) / half)
            ang = jnp.arange(L, dtype=jnp.float32)[:, None] * inv
            cos = jnp.cos(ang)[None, :, None, :]
            sin = jnp.sin(ang)[None, :, None, :]
            x1, x2 = (x[..., :half], x[..., half:])
            return jnp.concatenate([x1 * cos - x2 * sin, x1 * sin + x2 * cos], axis=-1)

        def _ln(x, eps=1e-05):
            m = jnp.mean(x, axis=-1, keepdims=True)
            v = jnp.var(x, axis=-1, keepdims=True)
            return (x - m) * jax.lax.rsqrt(v + eps)

        def _adaln(x, emb, w, b):
            gb = emb[:, 0, :] @ w.T + b
            g, be = jnp.split(gb, 2, axis=-1)
            return _ln(x) * (1.0 + g[:, None, :]) + be[:, None, :]

        def _attn(q, k, v, mask):
            scores = jnp.einsum('bqhd,bkhd->bhqk', q, k) / np.float32(np.sqrt(HD))
            scores = jnp.where(mask[:, None, None, :], jnp.float32(-jnp.inf), scores)
            w = jax.nn.softmax(scores, axis=-1)
            return jnp.einsum('bhqk,bkhd->bqhd', w, v)
        key = jax.random.key(seed)
        ks = jax.random.split(key, 20)
        B, L, LC = (4, 128, 64)
        s = 0.02
        inp = {'x': jax.random.normal(ks[0], (B, L, D), jnp.float32), 'noise_emb': jax.random.normal(ks[1], (B, 1, D), jnp.float32), 'context': jax.random.normal(ks[2], (B, LC, D), jnp.float32), 'src_mask': jnp.zeros((B, L), bool), 'ctx_mask': jnp.zeros((B, LC), bool), 'n1_w': jax.random.normal(ks[3], (NL, 2 * D, D), jnp.float32) * s, 'n1_b': jnp.zeros((NL, 2 * D), jnp.float32), 'n2_w': jax.random.normal(ks[4], (NL, 2 * D, D), jnp.float32) * s, 'n2_b': jnp.zeros((NL, 2 * D), jnp.float32), 'n3_w': jax.random.normal(ks[5], (NL, 2 * D, D), jnp.float32) * s, 'n3_b': jnp.zeros((NL, 2 * D), jnp.float32), 'qkv_w': jax.random.normal(ks[6], (NL, 3 * D, D), jnp.float32) * s, 'so_w': jax.random.normal(ks[7], (NL, D, D), jnp.float32) * s, 'cq_w': jax.random.normal(ks[8], (NL, D, D), jnp.float32) * s, 'ck_w': jax.random.normal(ks[9], (NL, D, D), jnp.float32) * s, 'cv_w': jax.random.normal(ks[10], (NL, D, D), jnp.float32) * s, 'co_w': jax.random.normal(ks[11], (NL, D, D), jnp.float32) * s, 'f1_w': jax.random.normal(ks[12], (NL, DFF, D), jnp.float32) * s, 'f1_b': jnp.zeros((NL, DFF), jnp.float32), 'f2_w': jax.random.normal(ks[13], (NL, D, DFF), jnp.float32) * s, 'f2_b': jnp.zeros((NL, D), jnp.float32)}
        return inp
    _L0_xcond_all = _L0_xcond_setup()
    _L0_xcond_in = {k: v for k, v in _L0_xcond_all.items() if k in ('n1_w', 'n1_b', 'n2_w', 'n2_b', 'n3_w', 'n3_b', 'qkv_w', 'so_w', 'cq_w', 'ck_w', 'cv_w', 'co_w', 'f1_w', 'f1_b', 'f2_w', 'f2_b')}
    del _L0_xcond_all

    def _L0_ffn_setup():
        import jax, jax.numpy as jnp
        import numpy as np
        H = 128
        E = 64
        K = 8
        G = 8
        TOPK_GROUP = 4
        I_MOE = 64
        I_SHARED = 256
        SCALE = 2.5

        def relu2(x):
            return jnp.square(jax.nn.relu(x))

        def _route(xf, router_w, correction_bias):
            T = xf.shape[0]
            logits = xf @ router_w.T
            scores = jax.nn.sigmoid(logits)
            sfc = scores + correction_bias[None, :]
            grp = sfc.reshape(T, G, E // G)
            top2, _ = jax.lax.top_k(grp, 2)
            group_scores = top2.sum(-1)
            _, gidx = jax.lax.top_k(group_scores, TOPK_GROUP)
            gmask = jnp.zeros((T, G), sfc.dtype).at[jnp.arange(T)[:, None], gidx].set(1.0)
            emask = jnp.repeat(gmask, E // G, axis=1)
            masked = jnp.where(emask > 0, sfc, 0.0)
            _, tidx = jax.lax.top_k(masked, K)
            tw = jnp.take_along_axis(scores, tidx, axis=1)
            tw = tw / (tw.sum(-1, keepdims=True) + 1e-20)
            return (tidx, tw * SCALE)
        key = jax.random.key(seed)
        ks = jax.random.split(key, 7)
        x = jax.random.normal(ks[0], (2, 128, H), dtype=jnp.float32)
        router_w = jax.random.normal(ks[1], (E, H), dtype=jnp.float32) * 0.02
        correction_bias = jax.random.normal(ks[2], (E,), dtype=jnp.float32) * 0.01
        up_w = jax.random.normal(ks[3], (E, H, I_MOE), dtype=jnp.float32) * 0.02
        down_w = jax.random.normal(ks[4], (E, I_MOE, H), dtype=jnp.float32) * 0.02
        shared_up_w = jax.random.normal(ks[5], (H, I_SHARED), dtype=jnp.float32) * 0.02
        shared_down_w = jax.random.normal(ks[6], (I_SHARED, H), dtype=jnp.float32) * 0.02
        return {'x': x, 'router_w': router_w, 'correction_bias': correction_bias, 'up_w': up_w, 'down_w': down_w, 'shared_up_w': shared_up_w, 'shared_down_w': shared_down_w}
    _L0_ffn_all = _L0_ffn_setup()
    _L0_ffn_in = {k: v for k, v in _L0_ffn_all.items() if k in ('router_w', 'correction_bias', 'up_w', 'down_w', 'shared_up_w', 'shared_down_w')}
    del _L0_ffn_all

    def _L1_xcond_setup():
        import jax, jax.numpy as jnp
        import numpy as np
        import math
        B, S, CTX, D, H, DH = (2, 256, 32, 128, 16, 64)
        INNER = H * DH
        DFF = 4 * D

        def layernorm(x, eps=1e-05):
            m = jnp.mean(x, axis=-1, keepdims=True)
            v = jnp.var(x, axis=-1, keepdims=True)
            return (x - m) * jax.lax.rsqrt(v + eps)

        def adaln(x, t, w, b):
            emb = t @ w + b
            scale, shift = jnp.split(emb, 2, axis=-1)
            return layernorm(x) * (1.0 + scale) + shift

        def mha(xq, ctx, wq, wk, wv, wo, bo):
            b, sq, _ = xq.shape
            sk = ctx.shape[1]
            q = (xq @ wq).reshape(b, sq, H, DH).transpose(0, 2, 1, 3)
            k = (ctx @ wk).reshape(b, sk, H, DH).transpose(0, 2, 1, 3)
            v = (ctx @ wv).reshape(b, sk, H, DH).transpose(0, 2, 1, 3)
            scores = jnp.einsum('bhqd,bhkd->bhqk', q, k) / math.sqrt(DH)
            attn = jax.nn.softmax(scores, axis=-1)
            out = jnp.einsum('bhqk,bhkd->bhqd', attn, v)
            out = out.transpose(0, 2, 1, 3).reshape(b, sq, INNER)
            return out @ wo + bo

        def glu_ff(x, w1, b1, w2, b2):
            u = x @ w1 + b1
            a, gate = jnp.split(u, 2, axis=-1)
            return a * jax.nn.gelu(gate, approximate=False) @ w2 + b2
        key = jax.random.key(seed)
        ks = jax.random.split(key, 24)
        s = 1.0 / math.sqrt(D)

        def n(k, shape, scale=1.0):
            return jax.random.normal(k, shape, dtype=jnp.float32) * scale
        return {'x': n(ks[0], (B, S, D)), 't': n(ks[1], (B, 1, D)), 'context': n(ks[2], (B, CTX, D)), 'attn1_wq': n(ks[3], (D, INNER), s), 'attn1_wk': n(ks[4], (D, INNER), s), 'attn1_wv': n(ks[5], (D, INNER), s), 'attn1_wo': n(ks[6], (INNER, D), s), 'attn1_bo': n(ks[7], (D,), 0.01), 'attn2_wq': n(ks[8], (D, INNER), s), 'attn2_wk': n(ks[9], (D, INNER), s), 'attn2_wv': n(ks[10], (D, INNER), s), 'attn2_wo': n(ks[11], (INNER, D), s), 'attn2_bo': n(ks[12], (D,), 0.01), 'ff_w1': n(ks[13], (D, 2 * DFF), s), 'ff_b1': n(ks[14], (2 * DFF,), 0.01), 'ff_w2': n(ks[15], (DFF, D), 1.0 / math.sqrt(DFF)), 'ff_b2': n(ks[16], (D,), 0.01), 'norm1_w': n(ks[17], (D, 2 * D), s), 'norm1_b': n(ks[18], (2 * D,), 0.01), 'norm2_w': n(ks[19], (D, 2 * D), s), 'norm2_b': n(ks[20], (2 * D,), 0.01), 'norm3_w': n(ks[21], (D, 2 * D), s), 'norm3_b': n(ks[22], (2 * D,), 0.01)}
    _L1_xcond_all = _L1_xcond_setup()
    _L1_xcond_in = {k: v for k, v in _L1_xcond_all.items() if k in ('attn1_wq', 'attn1_wk', 'attn1_wv', 'attn1_wo', 'attn1_bo', 'attn2_wq', 'attn2_wk', 'attn2_wv', 'attn2_wo', 'attn2_bo', 'ff_w1', 'ff_b1', 'ff_w2', 'ff_b2', 'norm1_w', 'norm1_b', 'norm2_w', 'norm2_b', 'norm3_w', 'norm3_b')}
    del _L1_xcond_all

    def _L1_ffn_setup():
        import jax, jax.numpy as jnp
        import numpy as np
        key = jax.random.key(seed)
        k0, k1, k2, k3 = jax.random.split(key, 4)
        B, S, D, F, E = (8, 256, 128, 256, 8)
        x = jax.random.normal(k0, (B, S, D), dtype=jnp.float32)
        Wg = jax.random.normal(k1, (D, E), dtype=jnp.float32) * 0.02
        W1 = jax.random.normal(k2, (E, D, F), dtype=jnp.float32) * 0.02
        W2 = jax.random.normal(k3, (E, F, D), dtype=jnp.float32) * 0.02
        return {'x': x, 'Wg': Wg, 'W1': W1, 'W2': W2}
    _L1_ffn_all = _L1_ffn_setup()
    _L1_ffn_in = {k: v for k, v in _L1_ffn_all.items() if k in ('Wg', 'W1', 'W2')}
    del _L1_ffn_all

    def _L2_xcond_setup():
        import jax, jax.numpy as jnp
        import numpy as np
        DIM = 128
        DIM_HEAD = 64
        HEADS = 16
        INNER = DIM_HEAD * HEADS
        B, N1, N2 = (8, 512, 32)
        EPS = 1e-05

        def layer_norm(x, w, b):
            mu = jnp.mean(x, axis=-1, keepdims=True)
            var = jnp.var(x, axis=-1, keepdims=True)
            return (x - mu) * jax.lax.rsqrt(var + EPS) * w + b
        key = jax.random.key(seed)
        ks = jax.random.split(key, 10)
        return {'x': jax.random.normal(ks[0], (B, N1, DIM), jnp.float32), 'latents': jax.random.normal(ks[1], (B, N2, DIM), jnp.float32), 'shift': jax.random.normal(ks[2], (B, DIM), jnp.float32), 'scale': jax.random.normal(ks[3], (B, DIM), jnp.float32), 'ln1_w': jnp.ones((DIM,), jnp.float32), 'ln1_b': jnp.zeros((DIM,), jnp.float32), 'ln2_w': jnp.ones((DIM,), jnp.float32), 'ln2_b': jnp.zeros((DIM,), jnp.float32), 'Wq': jax.random.normal(ks[4], (INNER, DIM), jnp.float32) * 0.02, 'Wkv': jax.random.normal(ks[5], (2 * INNER, DIM), jnp.float32) * 0.02, 'Wo': jax.random.normal(ks[6], (DIM, INNER), jnp.float32) * 0.02}
    _L2_xcond_all = _L2_xcond_setup()
    _L2_xcond_in = {k: v for k, v in _L2_xcond_all.items() if k in ('ln1_w', 'ln1_b', 'ln2_w', 'ln2_b', 'Wq', 'Wkv', 'Wo')}
    del _L2_xcond_all

    def _L2_ffn_setup():
        import jax, jax.numpy as jnp
        import numpy as np
        B, S, H = (4, 256, 128)
        F = 512
        E = 8
        JITTER_EPS = 0.01

        def _sparse_mixer_top2(scores, jitter_eps):
            vals, idx = jax.lax.top_k(scores, 2)
            neg_inf = -jnp.inf
            m1 = vals[:, :1]
            factor1 = jnp.maximum(jnp.abs(scores), m1)
            mask1 = (m1 - scores) / factor1 > 2 * jitter_eps
            p1 = jax.nn.softmax(jnp.where(mask1, neg_inf, scores), axis=-1)
            mult1 = jnp.take_along_axis(p1, idx[:, :1], axis=-1)[:, 0]
            m2 = vals[:, 1:2]
            factor2 = jnp.maximum(jnp.abs(scores), m2)
            mask2 = (m2 - scores) / factor2 > 2 * jitter_eps
            top1_onehot = jnp.arange(scores.shape[-1])[None, :] == idx[:, :1]
            s2 = jnp.where(top1_onehot, neg_inf, scores)
            p2 = jax.nn.softmax(jnp.where(mask2, neg_inf, s2), axis=-1)
            mult2 = jnp.take_along_axis(p2, idx[:, 1:2], axis=-1)[:, 0]
            return (mult1, mult2, idx)
        key = jax.random.key(seed)
        k0, k1, k2, k3, k4 = jax.random.split(key, 5)
        hidden_states = jax.random.normal(k0, (B, S, H), dtype=jnp.float32)
        gate_w = jax.random.normal(k1, (E, H), dtype=jnp.float32) * 0.02
        w1 = jax.random.normal(k2, (E, F, H), dtype=jnp.float32) * 0.02
        w2 = jax.random.normal(k3, (E, H, F), dtype=jnp.float32) * 0.02
        w3 = jax.random.normal(k4, (E, F, H), dtype=jnp.float32) * 0.02
        return {'hidden_states': hidden_states, 'gate_w': gate_w, 'w1': w1, 'w2': w2, 'w3': w3}
    _L2_ffn_all = _L2_ffn_setup()
    _L2_ffn_in = {k: v for k, v in _L2_ffn_all.items() if k in ('gate_w', 'w1', 'w2', 'w3')}
    del _L2_ffn_all

    def _L3_xcond_setup():
        import jax, jax.numpy as jnp
        import numpy as np
        B, N, K, D, T = (16, 512, 16, 128, 3)
        EPS_ATTN = 1e-08
        LN_EPS = 1e-05

        def _ln(x, g, b):
            mu = jnp.mean(x, axis=-1, keepdims=True)
            var = jnp.mean(jnp.square(x - mu), axis=-1, keepdims=True)
            return (x - mu) * jax.lax.rsqrt(var + LN_EPS) * g + b
        key = jax.random.key(seed)
        ks = jax.random.split(key, 16)
        w = lambda k, i, o: jax.random.normal(k, (i, o), jnp.float32) * 0.02
        inp = {'x_cls': jax.random.normal(ks[0], (B, D), jnp.float32), 'x': jax.random.normal(ks[1], (B, N, D), jnp.float32), 'noise': jax.random.normal(ks[2], (B, K, D), jnp.float32), 'q_mu': jax.random.normal(ks[3], (1, 1, D), jnp.float32), 'q_logsig': jax.random.normal(ks[4], (1, 1, D), jnp.float32) * 0.02, 'lnkv_g': jnp.ones((D,), jnp.float32), 'lnkv_b': jnp.zeros((D,), jnp.float32), 'lnq_g': jnp.ones((D,), jnp.float32), 'lnq_b': jnp.zeros((D,), jnp.float32), 'lnm_g': jnp.ones((D,), jnp.float32), 'lnm_b': jnp.zeros((D,), jnp.float32), 'lnp_g': jnp.ones((D,), jnp.float32), 'lnp_b': jnp.zeros((D,), jnp.float32), 'wk': w(ks[5], D, D), 'bk': jnp.zeros((D,), jnp.float32), 'wv': w(ks[6], D, D), 'bv': jnp.zeros((D,), jnp.float32), 'wq': w(ks[7], D, D), 'bq': jnp.zeros((D,), jnp.float32), 'wu': w(ks[8], D, D), 'bu': jnp.zeros((D,), jnp.float32), 'w1': w(ks[9], D, D), 'b1': jnp.zeros((D,), jnp.float32), 'w2': w(ks[10], D, D), 'b2': jnp.zeros((D,), jnp.float32)}
        return inp
    _L3_xcond_all = _L3_xcond_setup()
    _L3_xcond_in = {k: v for k, v in _L3_xcond_all.items() if k in ('q_mu', 'q_logsig', 'lnkv_g', 'lnkv_b', 'lnq_g', 'lnq_b', 'lnm_g', 'lnm_b', 'lnp_g', 'lnp_b', 'wk', 'bk', 'wv', 'bv', 'wq', 'bq', 'wu', 'bu', 'w1', 'b1', 'w2', 'b2')}
    del _L3_xcond_all

    def _L3_ffn_setup():
        import jax, jax.numpy as jnp
        import numpy as np
        LATENT = 128
        LEAF_W = 64
        DEPTH = 4
        N_LEAVES = 2 ** DEPTH
        N_NODES = 2 ** DEPTH - 1
        B, S = (4, 256)

        def _fff_params(key, prefix):
            ks = jax.random.split(key, 4)
            d, h, l, n = (LATENT, LEAF_W, N_LEAVES, N_NODES)
            s_in = 1.0 / np.sqrt(d).astype(np.float32)
            s_h = 1.0 / np.sqrt(h).astype(np.float32)
            return {f'{prefix}_node_w': jax.random.normal(ks[0], (n, d), jnp.float32) * s_in, f'{prefix}_node_b': jax.random.normal(ks[1], (n,), jnp.float32) * s_in, f'{prefix}_w1': jax.random.normal(ks[2], (l, d, h), jnp.float32) * s_in, f'{prefix}_b1': jnp.zeros((l, h), jnp.float32), f'{prefix}_w2': jax.random.normal(ks[3], (l, h, d), jnp.float32) * s_h, f'{prefix}_b2': jnp.zeros((l, d), jnp.float32)}

        def _fff(x, node_w, node_b, w1, b1, w2, b2):
            Bx, Sx, D = x.shape
            xf = x.reshape(-1, D)
            N = xf.shape[0]
            cur = jnp.zeros((N,), jnp.int32)
            for _ in range(DEPTH):
                pw = node_w[cur]
                score = jnp.einsum('nd,nd->n', xf, pw) + node_b[cur]
                cur = 2 * cur + 1 + (score >= 0).astype(jnp.int32)
            leaf = cur - N_NODES
            sel = jax.nn.one_hot(leaf, N_LEAVES, dtype=xf.dtype)
            hidden_all = jax.nn.relu(jnp.einsum('nd,ldh->lnh', xf, w1) + b1[:, None, :])
            hidden = hidden_all * sel.T[:, :, None]
            out = jnp.einsum('lnh,lho->no', hidden, w2) + sel @ b2
            return out.reshape(Bx, Sx, D)
        key = jax.random.key(seed)
        kx, kq, kk, kv = jax.random.split(key, 4)
        inp = {'x': jax.random.normal(kx, (B, S, LATENT), jnp.float32)}
        inp.update(_fff_params(kq, 'q'))
        inp.update(_fff_params(kk, 'k'))
        inp.update(_fff_params(kv, 'v'))
        return inp
    _L3_ffn_all = _L3_ffn_setup()
    _L3_ffn_in = {k: v for k, v in _L3_ffn_all.items() if k in ('q_node_w', 'q_node_b', 'q_w1', 'q_b1', 'q_w2', 'q_b2', 'k_node_w', 'k_node_b', 'k_w1', 'k_b1', 'k_w2', 'k_b2', 'v_node_w', 'v_node_b', 'v_w1', 'v_b1', 'v_w2', 'v_b2')}
    del _L3_ffn_all
    return {'x': x, 'cond_1024': cond_1024, 'ctx_1024': ctx_1024, 'mask_BxS_bf0': mask_BxS_bf0, 'mask_BxS2_bf0': mask_BxS2_bf0, 'L0_xcond_n1_w': _L0_xcond_in['n1_w'], 'L0_xcond_n1_b': _L0_xcond_in['n1_b'], 'L0_xcond_n2_w': _L0_xcond_in['n2_w'], 'L0_xcond_n2_b': _L0_xcond_in['n2_b'], 'L0_xcond_n3_w': _L0_xcond_in['n3_w'], 'L0_xcond_n3_b': _L0_xcond_in['n3_b'], 'L0_xcond_qkv_w': _L0_xcond_in['qkv_w'], 'L0_xcond_so_w': _L0_xcond_in['so_w'], 'L0_xcond_cq_w': _L0_xcond_in['cq_w'], 'L0_xcond_ck_w': _L0_xcond_in['ck_w'], 'L0_xcond_cv_w': _L0_xcond_in['cv_w'], 'L0_xcond_co_w': _L0_xcond_in['co_w'], 'L0_xcond_f1_w': _L0_xcond_in['f1_w'], 'L0_xcond_f1_b': _L0_xcond_in['f1_b'], 'L0_xcond_f2_w': _L0_xcond_in['f2_w'], 'L0_xcond_f2_b': _L0_xcond_in['f2_b'], 'L0_ffn_router_w': _L0_ffn_in['router_w'], 'L0_ffn_correction_bias': _L0_ffn_in['correction_bias'], 'L0_ffn_up_w': _L0_ffn_in['up_w'], 'L0_ffn_down_w': _L0_ffn_in['down_w'], 'L0_ffn_shared_up_w': _L0_ffn_in['shared_up_w'], 'L0_ffn_shared_down_w': _L0_ffn_in['shared_down_w'], 'L1_xcond_attn1_wq': _L1_xcond_in['attn1_wq'], 'L1_xcond_attn1_wk': _L1_xcond_in['attn1_wk'], 'L1_xcond_attn1_wv': _L1_xcond_in['attn1_wv'], 'L1_xcond_attn1_wo': _L1_xcond_in['attn1_wo'], 'L1_xcond_attn1_bo': _L1_xcond_in['attn1_bo'], 'L1_xcond_attn2_wq': _L1_xcond_in['attn2_wq'], 'L1_xcond_attn2_wk': _L1_xcond_in['attn2_wk'], 'L1_xcond_attn2_wv': _L1_xcond_in['attn2_wv'], 'L1_xcond_attn2_wo': _L1_xcond_in['attn2_wo'], 'L1_xcond_attn2_bo': _L1_xcond_in['attn2_bo'], 'L1_xcond_ff_w1': _L1_xcond_in['ff_w1'], 'L1_xcond_ff_b1': _L1_xcond_in['ff_b1'], 'L1_xcond_ff_w2': _L1_xcond_in['ff_w2'], 'L1_xcond_ff_b2': _L1_xcond_in['ff_b2'], 'L1_xcond_norm1_w': _L1_xcond_in['norm1_w'], 'L1_xcond_norm1_b': _L1_xcond_in['norm1_b'], 'L1_xcond_norm2_w': _L1_xcond_in['norm2_w'], 'L1_xcond_norm2_b': _L1_xcond_in['norm2_b'], 'L1_xcond_norm3_w': _L1_xcond_in['norm3_w'], 'L1_xcond_norm3_b': _L1_xcond_in['norm3_b'], 'L1_ffn_Wg': _L1_ffn_in['Wg'], 'L1_ffn_W1': _L1_ffn_in['W1'], 'L1_ffn_W2': _L1_ffn_in['W2'], 'L2_xcond_ln1_w': _L2_xcond_in['ln1_w'], 'L2_xcond_ln1_b': _L2_xcond_in['ln1_b'], 'L2_xcond_ln2_w': _L2_xcond_in['ln2_w'], 'L2_xcond_ln2_b': _L2_xcond_in['ln2_b'], 'L2_xcond_Wq': _L2_xcond_in['Wq'], 'L2_xcond_Wkv': _L2_xcond_in['Wkv'], 'L2_xcond_Wo': _L2_xcond_in['Wo'], 'L2_ffn_gate_w': _L2_ffn_in['gate_w'], 'L2_ffn_w1': _L2_ffn_in['w1'], 'L2_ffn_w2': _L2_ffn_in['w2'], 'L2_ffn_w3': _L2_ffn_in['w3'], 'L3_xcond_q_mu': _L3_xcond_in['q_mu'], 'L3_xcond_q_logsig': _L3_xcond_in['q_logsig'], 'L3_xcond_lnkv_g': _L3_xcond_in['lnkv_g'], 'L3_xcond_lnkv_b': _L3_xcond_in['lnkv_b'], 'L3_xcond_lnq_g': _L3_xcond_in['lnq_g'], 'L3_xcond_lnq_b': _L3_xcond_in['lnq_b'], 'L3_xcond_lnm_g': _L3_xcond_in['lnm_g'], 'L3_xcond_lnm_b': _L3_xcond_in['lnm_b'], 'L3_xcond_lnp_g': _L3_xcond_in['lnp_g'], 'L3_xcond_lnp_b': _L3_xcond_in['lnp_b'], 'L3_xcond_wk': _L3_xcond_in['wk'], 'L3_xcond_bk': _L3_xcond_in['bk'], 'L3_xcond_wv': _L3_xcond_in['wv'], 'L3_xcond_bv': _L3_xcond_in['bv'], 'L3_xcond_wq': _L3_xcond_in['wq'], 'L3_xcond_bq': _L3_xcond_in['bq'], 'L3_xcond_wu': _L3_xcond_in['wu'], 'L3_xcond_bu': _L3_xcond_in['bu'], 'L3_xcond_w1': _L3_xcond_in['w1'], 'L3_xcond_b1': _L3_xcond_in['b1'], 'L3_xcond_w2': _L3_xcond_in['w2'], 'L3_xcond_b2': _L3_xcond_in['b2'], 'L3_ffn_q_node_w': _L3_ffn_in['q_node_w'], 'L3_ffn_q_node_b': _L3_ffn_in['q_node_b'], 'L3_ffn_q_w1': _L3_ffn_in['q_w1'], 'L3_ffn_q_b1': _L3_ffn_in['q_b1'], 'L3_ffn_q_w2': _L3_ffn_in['q_w2'], 'L3_ffn_q_b2': _L3_ffn_in['q_b2'], 'L3_ffn_k_node_w': _L3_ffn_in['k_node_w'], 'L3_ffn_k_node_b': _L3_ffn_in['k_node_b'], 'L3_ffn_k_w1': _L3_ffn_in['k_w1'], 'L3_ffn_k_b1': _L3_ffn_in['k_b1'], 'L3_ffn_k_w2': _L3_ffn_in['k_w2'], 'L3_ffn_k_b2': _L3_ffn_in['k_b2'], 'L3_ffn_v_node_w': _L3_ffn_in['v_node_w'], 'L3_ffn_v_node_b': _L3_ffn_in['v_node_b'], 'L3_ffn_v_w1': _L3_ffn_in['v_w1'], 'L3_ffn_v_b1': _L3_ffn_in['v_b1'], 'L3_ffn_v_w2': _L3_ffn_in['v_w2'], 'L3_ffn_v_b2': _L3_ffn_in['v_b2']}

def reference(x, cond_1024, ctx_1024, mask_BxS_bf0, mask_BxS2_bf0, L0_xcond_n1_w, L0_xcond_n1_b, L0_xcond_n2_w, L0_xcond_n2_b, L0_xcond_n3_w, L0_xcond_n3_b, L0_xcond_qkv_w, L0_xcond_so_w, L0_xcond_cq_w, L0_xcond_ck_w, L0_xcond_cv_w, L0_xcond_co_w, L0_xcond_f1_w, L0_xcond_f1_b, L0_xcond_f2_w, L0_xcond_f2_b, L0_ffn_router_w, L0_ffn_correction_bias, L0_ffn_up_w, L0_ffn_down_w, L0_ffn_shared_up_w, L0_ffn_shared_down_w, L1_xcond_attn1_wq, L1_xcond_attn1_wk, L1_xcond_attn1_wv, L1_xcond_attn1_wo, L1_xcond_attn1_bo, L1_xcond_attn2_wq, L1_xcond_attn2_wk, L1_xcond_attn2_wv, L1_xcond_attn2_wo, L1_xcond_attn2_bo, L1_xcond_ff_w1, L1_xcond_ff_b1, L1_xcond_ff_w2, L1_xcond_ff_b2, L1_xcond_norm1_w, L1_xcond_norm1_b, L1_xcond_norm2_w, L1_xcond_norm2_b, L1_xcond_norm3_w, L1_xcond_norm3_b, L1_ffn_Wg, L1_ffn_W1, L1_ffn_W2, L2_xcond_ln1_w, L2_xcond_ln1_b, L2_xcond_ln2_w, L2_xcond_ln2_b, L2_xcond_Wq, L2_xcond_Wkv, L2_xcond_Wo, L2_ffn_gate_w, L2_ffn_w1, L2_ffn_w2, L2_ffn_w3, L3_xcond_q_mu, L3_xcond_q_logsig, L3_xcond_lnkv_g, L3_xcond_lnkv_b, L3_xcond_lnq_g, L3_xcond_lnq_b, L3_xcond_lnm_g, L3_xcond_lnm_b, L3_xcond_lnp_g, L3_xcond_lnp_b, L3_xcond_wk, L3_xcond_bk, L3_xcond_wv, L3_xcond_bv, L3_xcond_wq, L3_xcond_bq, L3_xcond_wu, L3_xcond_bu, L3_xcond_w1, L3_xcond_b1, L3_xcond_w2, L3_xcond_b2, L3_ffn_q_node_w, L3_ffn_q_node_b, L3_ffn_q_w1, L3_ffn_q_b1, L3_ffn_q_w2, L3_ffn_q_b2, L3_ffn_k_node_w, L3_ffn_k_node_b, L3_ffn_k_w1, L3_ffn_k_b1, L3_ffn_k_w2, L3_ffn_k_b2, L3_ffn_v_node_w, L3_ffn_v_node_b, L3_ffn_v_w1, L3_ffn_v_b1, L3_ffn_v_w2, L3_ffn_v_b2):
    import jax
    import jax.numpy as jnp

    def _L0_xcond_ref(x, noise_emb, context, src_mask, ctx_mask, n1_w, n1_b, n2_w, n2_b, n3_w, n3_b, qkv_w, so_w, cq_w, ck_w, cv_w, co_w, f1_w, f1_b, f2_w, f2_b):
        import jax, jax.numpy as jnp
        import numpy as np
        NL, D, H, DFF = (6, 128, 16, 512)
        HD = D // H

        def _rope(x):
            L = x.shape[1]
            half = HD // 2
            inv = 1.0 / 10000.0 ** (jnp.arange(half, dtype=jnp.float32) / half)
            ang = jnp.arange(L, dtype=jnp.float32)[:, None] * inv
            cos = jnp.cos(ang)[None, :, None, :]
            sin = jnp.sin(ang)[None, :, None, :]
            x1, x2 = (x[..., :half], x[..., half:])
            return jnp.concatenate([x1 * cos - x2 * sin, x1 * sin + x2 * cos], axis=-1)

        def _ln(x, eps=1e-05):
            m = jnp.mean(x, axis=-1, keepdims=True)
            v = jnp.var(x, axis=-1, keepdims=True)
            return (x - m) * jax.lax.rsqrt(v + eps)

        def _adaln(x, emb, w, b):
            gb = emb[:, 0, :] @ w.T + b
            g, be = jnp.split(gb, 2, axis=-1)
            return _ln(x) * (1.0 + g[:, None, :]) + be[:, None, :]

        def _attn(q, k, v, mask):
            scores = jnp.einsum('bqhd,bkhd->bhqk', q, k) / np.float32(np.sqrt(HD))
            scores = jnp.where(mask[:, None, None, :], jnp.float32(-jnp.inf), scores)
            w = jax.nn.softmax(scores, axis=-1)
            return jnp.einsum('bhqk,bkhd->bqhd', w, v)
        B, L, _ = x.shape
        LC = context.shape[1]
        for i in range(NL):
            xn = _adaln(x, noise_emb, n1_w[i], n1_b[i])
            qkv = xn @ qkv_w[i].T
            q, k, v = jnp.split(qkv, 3, axis=-1)
            q = _rope(q.reshape(B, L, H, HD))
            k = _rope(k.reshape(B, L, H, HD))
            v = v.reshape(B, L, H, HD)
            a = _attn(q, k, v, src_mask).reshape(B, L, D) @ so_w[i].T
            x = x + a
            xn = _adaln(x, noise_emb, n2_w[i], n2_b[i])
            q = _rope((xn @ cq_w[i].T).reshape(B, L, H, HD))
            k = _rope((context @ ck_w[i].T).reshape(B, LC, H, HD))
            v = (context @ cv_w[i].T).reshape(B, LC, H, HD)
            a = _attn(q, k, v, ctx_mask).reshape(B, L, D) @ co_w[i].T
            x = x + a
            xn = _adaln(x, noise_emb, n3_w[i], n3_b[i])
            h = jax.nn.gelu(xn @ f1_w[i].T + f1_b[i], approximate=False)
            x = x + (h @ f2_w[i].T + f2_b[i])
        return x

    def _L0_ffn_ref(x, router_w, correction_bias, up_w, down_w, shared_up_w, shared_down_w):
        import jax, jax.numpy as jnp
        import numpy as np
        H = 128
        E = 64
        K = 8
        G = 8
        TOPK_GROUP = 4
        I_MOE = 64
        I_SHARED = 256
        SCALE = 2.5

        def relu2(x):
            return jnp.square(jax.nn.relu(x))

        def _route(xf, router_w, correction_bias):
            T = xf.shape[0]
            logits = xf @ router_w.T
            scores = jax.nn.sigmoid(logits)
            sfc = scores + correction_bias[None, :]
            grp = sfc.reshape(T, G, E // G)
            top2, _ = jax.lax.top_k(grp, 2)
            group_scores = top2.sum(-1)
            _, gidx = jax.lax.top_k(group_scores, TOPK_GROUP)
            gmask = jnp.zeros((T, G), sfc.dtype).at[jnp.arange(T)[:, None], gidx].set(1.0)
            emask = jnp.repeat(gmask, E // G, axis=1)
            masked = jnp.where(emask > 0, sfc, 0.0)
            _, tidx = jax.lax.top_k(masked, K)
            tw = jnp.take_along_axis(scores, tidx, axis=1)
            tw = tw / (tw.sum(-1, keepdims=True) + 1e-20)
            return (tidx, tw * SCALE)
        B, S, Hd = x.shape
        xf = x.reshape(-1, Hd)
        T = xf.shape[0]
        tidx, tw = _route(xf.astype(jnp.float32), router_w, correction_bias)
        combine = jnp.zeros((T, E), xf.dtype).at[jnp.arange(T)[:, None], tidx].add(tw.astype(xf.dtype))

        def body(acc, ew):
            wu, wd, c = ew
            return (acc + c[:, None] * (relu2(xf @ wu) @ wd), None)
        routed, _ = jax.lax.scan(body, jnp.zeros_like(xf), (up_w, down_w, combine.T))
        shared = relu2(xf @ shared_up_w) @ shared_down_w
        return (routed + shared).reshape(B, S, Hd)

    def _L1_xcond_ref(x, t, context, attn1_wq, attn1_wk, attn1_wv, attn1_wo, attn1_bo, attn2_wq, attn2_wk, attn2_wv, attn2_wo, attn2_bo, ff_w1, ff_b1, ff_w2, ff_b2, norm1_w, norm1_b, norm2_w, norm2_b, norm3_w, norm3_b):
        import jax, jax.numpy as jnp
        import numpy as np
        import math
        B, S, CTX, D, H, DH = (2, 256, 32, 128, 16, 64)
        INNER = H * DH
        DFF = 4 * D

        def layernorm(x, eps=1e-05):
            m = jnp.mean(x, axis=-1, keepdims=True)
            v = jnp.var(x, axis=-1, keepdims=True)
            return (x - m) * jax.lax.rsqrt(v + eps)

        def adaln(x, t, w, b):
            emb = t @ w + b
            scale, shift = jnp.split(emb, 2, axis=-1)
            return layernorm(x) * (1.0 + scale) + shift

        def mha(xq, ctx, wq, wk, wv, wo, bo):
            b, sq, _ = xq.shape
            sk = ctx.shape[1]
            q = (xq @ wq).reshape(b, sq, H, DH).transpose(0, 2, 1, 3)
            k = (ctx @ wk).reshape(b, sk, H, DH).transpose(0, 2, 1, 3)
            v = (ctx @ wv).reshape(b, sk, H, DH).transpose(0, 2, 1, 3)
            scores = jnp.einsum('bhqd,bhkd->bhqk', q, k) / math.sqrt(DH)
            attn = jax.nn.softmax(scores, axis=-1)
            out = jnp.einsum('bhqk,bhkd->bhqd', attn, v)
            out = out.transpose(0, 2, 1, 3).reshape(b, sq, INNER)
            return out @ wo + bo

        def glu_ff(x, w1, b1, w2, b2):
            u = x @ w1 + b1
            a, gate = jnp.split(u, 2, axis=-1)
            return a * jax.nn.gelu(gate, approximate=False) @ w2 + b2
        h1 = adaln(x, t, norm1_w, norm1_b)
        x = mha(h1, h1, attn1_wq, attn1_wk, attn1_wv, attn1_wo, attn1_bo) + x
        h2 = adaln(x, t, norm2_w, norm2_b)
        x = mha(h2, context, attn2_wq, attn2_wk, attn2_wv, attn2_wo, attn2_bo) + x
        h3 = adaln(x, t, norm3_w, norm3_b)
        x = glu_ff(h3, ff_w1, ff_b1, ff_w2, ff_b2) + x
        return x

    def _L1_ffn_ref(x, Wg, W1, W2):
        import jax, jax.numpy as jnp
        import numpy as np
        B, S, D = x.shape
        E = Wg.shape[1]
        T = B * S
        cap = max(1, T // E)
        xt = x.reshape(T, D)
        logits = xt @ Wg
        probs = jax.nn.softmax(logits, axis=-1)
        pT = probs.T
        _, top_idx = jax.lax.top_k(pT, cap)
        sel = jnp.zeros((E, T), dtype=bool).at[jnp.arange(E)[:, None], top_idx].set(True)
        masked = jnp.where(sel, pT, -jnp.inf)
        assigned = sel.any(axis=0)
        tok2exp = jnp.where(assigned, jnp.argmax(masked, axis=0), jnp.argmax(pT, axis=0))
        weights = jnp.take_along_axis(probs, tok2exp[:, None], axis=1)[:, 0]
        out = jnp.zeros_like(xt)
        for e in range(E):
            gate = jnp.where(tok2exp == e, weights, 0.0)
            h = jax.nn.gelu(xt @ W1[e], approximate=False) @ W2[e]
            out = out + gate[:, None] * h
        return out.reshape(B, S, D)

    def _L2_xcond_ref(x, latents, shift, scale, ln1_w, ln1_b, ln2_w, ln2_b, Wq, Wkv, Wo):
        import jax, jax.numpy as jnp
        import numpy as np
        DIM = 128
        DIM_HEAD = 64
        HEADS = 16
        INNER = DIM_HEAD * HEADS
        B, N1, N2 = (8, 512, 32)
        EPS = 1e-05

        def layer_norm(x, w, b):
            mu = jnp.mean(x, axis=-1, keepdims=True)
            var = jnp.var(x, axis=-1, keepdims=True)
            return (x - mu) * jax.lax.rsqrt(var + EPS) * w + b
        x = layer_norm(x, ln1_w, ln1_b)
        lat = layer_norm(latents, ln2_w, ln2_b)
        lat = lat * (1.0 + scale[:, None, :]) + shift[:, None, :]
        b, n2, _ = lat.shape
        q = jnp.einsum('bld,ed->ble', lat, Wq)
        kv_in = jnp.concatenate((x, lat), axis=-2)
        kv = jnp.einsum('bld,ed->ble', kv_in, Wkv)
        k, v = jnp.split(kv, 2, axis=-1)

        def to_heads(t):
            bsz, L, _ = t.shape
            return t.reshape(bsz, L, HEADS, DIM_HEAD).transpose(0, 2, 1, 3)
        q, k, v = (to_heads(q), to_heads(k), to_heads(v))
        attn_scale = 1.0 / np.sqrt(np.sqrt(DIM_HEAD)).astype(np.float32)
        logits = jnp.einsum('bhqd,bhkd->bhqk', q * attn_scale, k * attn_scale)
        w = jax.nn.softmax(logits.astype(jnp.float32), axis=-1).astype(logits.dtype)
        out = jnp.einsum('bhqk,bhkd->bhqd', w, v)
        out = out.transpose(0, 2, 1, 3).reshape(b, n2, INNER)
        return jnp.einsum('ble,de->bld', out, Wo)

    def _L2_ffn_ref(hidden_states, gate_w, w1, w2, w3):
        import jax, jax.numpy as jnp
        import numpy as np
        B, S, H = (4, 256, 128)
        F = 512
        E = 8
        JITTER_EPS = 0.01

        def _sparse_mixer_top2(scores, jitter_eps):
            vals, idx = jax.lax.top_k(scores, 2)
            neg_inf = -jnp.inf
            m1 = vals[:, :1]
            factor1 = jnp.maximum(jnp.abs(scores), m1)
            mask1 = (m1 - scores) / factor1 > 2 * jitter_eps
            p1 = jax.nn.softmax(jnp.where(mask1, neg_inf, scores), axis=-1)
            mult1 = jnp.take_along_axis(p1, idx[:, :1], axis=-1)[:, 0]
            m2 = vals[:, 1:2]
            factor2 = jnp.maximum(jnp.abs(scores), m2)
            mask2 = (m2 - scores) / factor2 > 2 * jitter_eps
            top1_onehot = jnp.arange(scores.shape[-1])[None, :] == idx[:, :1]
            s2 = jnp.where(top1_onehot, neg_inf, scores)
            p2 = jax.nn.softmax(jnp.where(mask2, neg_inf, s2), axis=-1)
            mult2 = jnp.take_along_axis(p2, idx[:, 1:2], axis=-1)[:, 0]
            return (mult1, mult2, idx)
        Bv, Sv, Hv = hidden_states.shape
        x = hidden_states.reshape(-1, Hv)
        scores = x @ gate_w.T
        mult1, mult2, idx = _sparse_mixer_top2(scores, JITTER_EPS)
        out = jnp.zeros_like(x)
        for e in range(E):
            w_tok = mult1 * (idx[:, 0] == e) + mult2 * (idx[:, 1] == e)
            h = jax.nn.silu(x @ w1[e].T) * (x @ w3[e].T)
            out = out + w_tok[:, None] * (h @ w2[e].T)
        return out.reshape(Bv, Sv, Hv)

    def _L3_xcond_ref(x_cls, x, noise, q_mu, q_logsig, lnkv_g, lnkv_b, lnq_g, lnq_b, lnm_g, lnm_b, lnp_g, lnp_b, wk, bk, wv, bv, wq, bq, wu, bu, w1, b1, w2, b2):
        import jax, jax.numpy as jnp
        import numpy as np
        B, N, K, D, T = (16, 512, 16, 128, 3)
        EPS_ATTN = 1e-08
        LN_EPS = 1e-05

        def _ln(x, g, b):
            mu = jnp.mean(x, axis=-1, keepdims=True)
            var = jnp.mean(jnp.square(x - mu), axis=-1, keepdims=True)
            return (x - mu) * jax.lax.rsqrt(var + LN_EPS) * g + b
        scale = D ** (-0.5)
        x_in = _ln(x, lnkv_g, lnkv_b)
        k = x_in @ wk + bk
        v = x_in @ wv + bv
        slots = q_mu + jnp.exp(q_logsig) * noise
        for _ in range(T):
            prev = slots
            q = _ln(slots, lnq_g, lnq_b) @ wq + bq
            logits = jnp.einsum('bnd,bkd->bnk', k, q) / scale
            attn = jax.nn.softmax(logits, axis=-1) + EPS_ATTN
            attn = attn / jnp.sum(attn, axis=1, keepdims=True)
            upd = jnp.einsum('bnk,bnd->bkd', attn, v)
            slots = upd @ wu + bu + prev
            h = _ln(slots, lnm_g, lnm_b) @ w1 + b1
            slots = jax.nn.gelu(h, approximate=False) @ w2 + b2 + slots
            slots = _ln(slots + x_cls[:, None, :], lnp_g, lnp_b)
        return slots

    def _L3_ffn_ref(x, q_node_w, q_node_b, q_w1, q_b1, q_w2, q_b2, k_node_w, k_node_b, k_w1, k_b1, k_w2, k_b2, v_node_w, v_node_b, v_w1, v_b1, v_w2, v_b2):
        import jax, jax.numpy as jnp
        import numpy as np
        LATENT = 128
        LEAF_W = 64
        DEPTH = 4
        N_LEAVES = 2 ** DEPTH
        N_NODES = 2 ** DEPTH - 1
        B, S = (4, 256)

        def _fff_params(key, prefix):
            ks = jax.random.split(key, 4)
            d, h, l, n = (LATENT, LEAF_W, N_LEAVES, N_NODES)
            s_in = 1.0 / np.sqrt(d).astype(np.float32)
            s_h = 1.0 / np.sqrt(h).astype(np.float32)
            return {f'{prefix}_node_w': jax.random.normal(ks[0], (n, d), jnp.float32) * s_in, f'{prefix}_node_b': jax.random.normal(ks[1], (n,), jnp.float32) * s_in, f'{prefix}_w1': jax.random.normal(ks[2], (l, d, h), jnp.float32) * s_in, f'{prefix}_b1': jnp.zeros((l, h), jnp.float32), f'{prefix}_w2': jax.random.normal(ks[3], (l, h, d), jnp.float32) * s_h, f'{prefix}_b2': jnp.zeros((l, d), jnp.float32)}

        def _fff(x, node_w, node_b, w1, b1, w2, b2):
            Bx, Sx, D = x.shape
            xf = x.reshape(-1, D)
            N = xf.shape[0]
            cur = jnp.zeros((N,), jnp.int32)
            for _ in range(DEPTH):
                pw = node_w[cur]
                score = jnp.einsum('nd,nd->n', xf, pw) + node_b[cur]
                cur = 2 * cur + 1 + (score >= 0).astype(jnp.int32)
            leaf = cur - N_NODES
            sel = jax.nn.one_hot(leaf, N_LEAVES, dtype=xf.dtype)
            hidden_all = jax.nn.relu(jnp.einsum('nd,ldh->lnh', xf, w1) + b1[:, None, :])
            hidden = hidden_all * sel.T[:, :, None]
            out = jnp.einsum('lnh,lho->no', hidden, w2) + sel @ b2
            return out.reshape(Bx, Sx, D)
        q = _fff(x, q_node_w, q_node_b, q_w1, q_b1, q_w2, q_b2)
        k = _fff(x, k_node_w, k_node_b, k_w1, k_b1, k_w2, k_b2)
        v = _fff(x, v_node_w, v_node_b, v_w1, v_b1, v_w2, v_b2)
        scale = 1.0 / np.sqrt(LATENT).astype(np.float32)
        attn = jax.nn.softmax(jnp.einsum('bqd,bkd->bqk', q, k) * scale, axis=-1)
        return jnp.einsum('bqk,bkd->bqd', attn, v)
    x = x + _L0_xcond_ref(_layernorm(x, axis=-1), cond_1024[:, None, :], ctx_1024, mask_BxS_bf0, mask_BxS2_bf0, L0_xcond_n1_w, L0_xcond_n1_b, L0_xcond_n2_w, L0_xcond_n2_b, L0_xcond_n3_w, L0_xcond_n3_b, L0_xcond_qkv_w, L0_xcond_so_w, L0_xcond_cq_w, L0_xcond_ck_w, L0_xcond_cv_w, L0_xcond_co_w, L0_xcond_f1_w, L0_xcond_f1_b, L0_xcond_f2_w, L0_xcond_f2_b)
    x = x + _L0_ffn_ref(_layernorm(x, axis=-1), L0_ffn_router_w, L0_ffn_correction_bias, L0_ffn_up_w, L0_ffn_down_w, L0_ffn_shared_up_w, L0_ffn_shared_down_w)
    x = x + _L1_xcond_ref(_layernorm(x, axis=-1), cond_1024[:, None, :], ctx_1024, L1_xcond_attn1_wq, L1_xcond_attn1_wk, L1_xcond_attn1_wv, L1_xcond_attn1_wo, L1_xcond_attn1_bo, L1_xcond_attn2_wq, L1_xcond_attn2_wk, L1_xcond_attn2_wv, L1_xcond_attn2_wo, L1_xcond_attn2_bo, L1_xcond_ff_w1, L1_xcond_ff_b1, L1_xcond_ff_w2, L1_xcond_ff_b2, L1_xcond_norm1_w, L1_xcond_norm1_b, L1_xcond_norm2_w, L1_xcond_norm2_b, L1_xcond_norm3_w, L1_xcond_norm3_b)
    x = x + _L1_ffn_ref(_layernorm(x, axis=-1), L1_ffn_Wg, L1_ffn_W1, L1_ffn_W2)
    x = x + _L2_xcond_ref(ctx_1024, _layernorm(x, axis=-1), cond_1024, cond_1024, L2_xcond_ln1_w, L2_xcond_ln1_b, L2_xcond_ln2_w, L2_xcond_ln2_b, L2_xcond_Wq, L2_xcond_Wkv, L2_xcond_Wo)
    x = x + _L2_ffn_ref(_layernorm(x, axis=-1), L2_ffn_gate_w, L2_ffn_w1, L2_ffn_w2, L2_ffn_w3)
    x = x + _L3_xcond_ref(cond_1024, ctx_1024, _layernorm(x, axis=-1), L3_xcond_q_mu, L3_xcond_q_logsig, L3_xcond_lnkv_g, L3_xcond_lnkv_b, L3_xcond_lnq_g, L3_xcond_lnq_b, L3_xcond_lnm_g, L3_xcond_lnm_b, L3_xcond_lnp_g, L3_xcond_lnp_b, L3_xcond_wk, L3_xcond_bk, L3_xcond_wv, L3_xcond_bv, L3_xcond_wq, L3_xcond_bq, L3_xcond_wu, L3_xcond_bu, L3_xcond_w1, L3_xcond_b1, L3_xcond_w2, L3_xcond_b2)
    x = x + _L3_ffn_ref(_layernorm(x, axis=-1), L3_ffn_q_node_w, L3_ffn_q_node_b, L3_ffn_q_w1, L3_ffn_q_b1, L3_ffn_q_w2, L3_ffn_q_b2, L3_ffn_k_node_w, L3_ffn_k_node_b, L3_ffn_k_w1, L3_ffn_k_b1, L3_ffn_k_w2, L3_ffn_k_b2, L3_ffn_v_node_w, L3_ffn_v_node_b, L3_ffn_v_w1, L3_ffn_v_b1, L3_ffn_v_w2, L3_ffn_v_b2)
    return x

_drawn_inputs = setup_inputs


def setup_inputs(seed=0):
    import zlib

    import numpy as np

    out = dict(_drawn_inputs(seed))
    spreads = {'L0_xcond_n1_b': (0.0, 0.8),
     'L0_xcond_n2_b': (0.0, 0.8),
     'L0_xcond_n3_b': (0.0, 0.725),
     'L0_xcond_f1_b': (0.0, 0.1),
     'L0_xcond_f2_b': (0.0, 0.1),
     'L2_xcond_ln1_w': (1.0, 0.6),
     'L2_xcond_ln1_b': (0.0, 0.8),
     'L2_xcond_ln2_w': (1.0, 0.6),
     'L2_xcond_ln2_b': (0.0, 0.8),
     'L3_xcond_lnkv_g': (1.0, 0.6),
     'L3_xcond_lnkv_b': (0.0, 0.8),
     'L3_xcond_lnq_g': (1.0, 0.6),
     'L3_xcond_lnq_b': (0.0, 2.0),
     'L3_xcond_lnm_g': (1.0, 0.6),
     'L3_xcond_lnm_b': (0.0, 0.8),
     'L3_xcond_lnp_g': (1.0, 0.2),
     'L3_xcond_lnp_b': (0.0, 0.305),
     'L3_xcond_bk': (0.0, 0.8),
     'L3_xcond_bv': (0.0, 0.8),
     'L3_xcond_bq': (0.0, 2.0),
     'L3_xcond_bu': (0.0, 0.433),
     'L3_xcond_b1': (0.0, 0.8),
     'L3_xcond_b2': (0.0, 1.317),
     'L3_ffn_q_b1': (0.0, 0.8),
     'L3_ffn_q_b2': (0.0, 2.0),
     'L3_ffn_k_b1': (0.0, 0.8),
     'L3_ffn_k_b2': (0.0, 2.0),
     'L3_ffn_v_b1': (0.0, 0.8),
     'L3_ffn_v_b2': (0.0, 0.8)}
    factors = {'L0_xcond_n1_w': 3.033,
     'L0_xcond_n2_w': 8.0,
     'L0_xcond_cq_w': 8.0,
     'L0_xcond_ck_w': 8.0,
     'L0_ffn_router_w': 8.0,
     'L0_ffn_correction_bias': 8.0,
     'L0_ffn_up_w': 8.0,
     'L0_ffn_down_w': 8.0,
     'L0_ffn_shared_up_w': 5.368,
     'L0_ffn_shared_down_w': 4.932,
     'L1_xcond_attn1_bo': 8.0,
     'L1_xcond_attn2_bo': 8.0,
     'L1_xcond_ff_b1': 8.0,
     'L1_xcond_ff_b2': 8.0,
     'L1_xcond_norm1_b': 5.267,
     'L1_xcond_norm2_b': 8.0,
     'L1_xcond_norm3_b': 8.0,
     'L1_ffn_Wg': 8.0,
     'L1_ffn_W1': 8.0,
     'L1_ffn_W2': 8.0,
     'L2_xcond_Wq': 8.0,
     'L2_xcond_Wkv': 3.951,
     'L2_xcond_Wo': 3.901,
     'L2_ffn_gate_w': 8.0,
     'L2_ffn_w1': 8.0,
     'L2_ffn_w2': 8.0,
     'L2_ffn_w3': 8.0,
     'L3_xcond_q_logsig': 8.0,
     'L3_xcond_wk': 8.0,
     'L3_xcond_wv': 8.0,
     'L3_xcond_wq': 8.0,
     'L3_xcond_wu': 7.105,
     'L3_xcond_w1': 8.0,
     'L3_xcond_w2': 8.0,
     'L3_ffn_q_node_w': 7.511,
     'L3_ffn_q_node_b': 8.0,
     'L3_ffn_q_w1': 8.0,
     'L3_ffn_q_w2': 7.433,
     'L3_ffn_k_node_w': 7.057,
     'L3_ffn_k_node_b': 8.0,
     'L3_ffn_k_w1': 8.0,
     'L3_ffn_k_w2': 7.494,
     'L3_ffn_v_node_b': 5.705}
    for name, (base, spread) in spreads.items():
        noise = np.random.default_rng([zlib.crc32(name.encode()), seed]).standard_normal(out[name].shape)
        drawn = base * np.exp(spread * noise) if base else spread * noise
        out[name] = jnp.asarray(drawn.astype(out[name].dtype))
    for name, factor in factors.items():
        out[name] = (out[name] * factor).astype(out[name].dtype)
    return out
```

```python
from contextlib import ExitStack

import numpy as np
import concourse.bass as bass
from concourse import mybir

F32, BF16, U8 = mybir.dt.float32, mybir.dt.bfloat16, mybir.dt.uint8
ALU, ACT, AX = mybir.AluOpType, mybir.ActivationFunctionType, mybir.AxisListType

B, S, D = 16, 56, 128
T = B * S
TT = T // 128
HALF = T // 2
BH = B // 2
L = 1500
KT, KN = 12, 125
H = 16
R = H * S // 128
NL = 6
NORMS = 3 * NL + 3
BANK = 512
LOW = -1e30
EPS = 1e-5
FIRST, LAST = 0, 7


class Lane:

    def __init__(self, sem):
        self.sem, self.count, self.queue, self.seen = sem, 0, [], {}

    def wait(self, after):
        for source, value in after:
            if self.seen.get(source.sem.name, 0) < value:
                self.seen[source.sem.name] = value
                self.queue.append(lambda e, s=source.sem, v=value: e.wait_ge(s, v))

    def put(self, make, after=(), signal=True):
        self.wait(after)
        if signal:
            self.count += 1
            self.queue.append(lambda e: make(e).then_inc(self.sem, 1))
        else:
            self.queue.append(make)
        return (self, self.count)

    def run(self, e):
        for step in self.queue:
            step(e)


class Arrival:

    def __init__(self, sem):
        self.sem, self.count = sem, 0


class Slot:

    def __init__(self, ap, arrival=None):
        self.ap, self.ready, self.free, self.arrival = ap, (), (), arrival


class Ring:
    def __init__(self, slots):
        self.slots, self.n = slots, -1

    def next(self):
        self.n += 1
        return self.slots[self.n % len(self.slots)]


def halves(a):
    return [a[:, 0:HALF], a[:, HALF:T]]


def spread(cols, n):
    p, m = cols.shape
    return cols.unsqueeze(2).broadcast_to([p, m, n])


def program(nc, dr, out):
    ctx = ExitStack()
    with ctx:
        names = {}

        def sb(stack, name, shape, dt=F32):
            names[name] = names.get(name, 0) + 1
            if names[name] > 1:
                name = f"{name}_{names[name]}"
            return stack.enter_context(nc.sbuf_tensor(name, shape, dt))

        def sem(name):
            return ctx.enter_context(nc.semaphore(name))

        PE, DVE, SC, PL = (Lane(sem(n)) for n in ("pe_done", "dve_done", "act_done", "pool_done"))
        SY = Lane(sem("sync_unused"))
        arrival_of = {}

        def arrival(name):
            if name not in arrival_of:
                arrival_of[name] = Arrival(sem(name))
            return arrival_of[name]

        def mm(o, lhsT, rhs, start=True, stop=True, after=(), signal=False):
            return PE.put(lambda e: e.matmul(o, lhsT, rhs, start=start, stop=stop), after, signal=signal or stop)

        def tr(o, i, after=()):
            p = i.shape[0]
            return PE.put(lambda e: e.transpose(o, i, ident[0:p, 0:p]), after)

        def tt(o, a, b, op, after=(), lane=DVE):
            return lane.put(lambda e: e.tensor_tensor(o, a, b, op), after)

        def ts(o, a, s1, s2, op0, op1=None, after=(), lane=DVE):
            if op1 is None:
                return lane.put(lambda e: e.tensor_scalar(o, a, s1, None, op0), after)
            return lane.put(lambda e: e.tensor_scalar(o, a, s1, s2, op0, op1), after)

        def stt(o, a, s, b, op0, op1, after=()):
            return DVE.put(lambda e: e.scalar_tensor_tensor(out=o, in0=a, scalar=s, in1=b, op0=op0, op1=op1), after)

        def cp(o, a, after=(), lane=DVE):
            if lane is SC:
                return act(o, a, ACT.Copy, after=after)
            return lane.put(lambda e: e.tensor_copy(o, a), after)

        def recip(o, a, after=()):
            return DVE.put(lambda e: e.reciprocal(o, a), after)

        def max8(o, a, after=()):
            return DVE.put(lambda e: e.max(o, a), after)

        def replace8(o, found, a, after=()):
            return DVE.put(lambda e: e.match_replace(o, found, a, LOW), after)

        def bn_stats(o, a, after=()):
            return DVE.put(lambda e: e.bn_stats(o, a), after)

        def bn_aggr(o, a, after=()):
            return DVE.put(lambda e: e.bn_aggr(o, a), after)

        def memset(o, value, after=(), lane=None):
            return (lane or PL).put(lambda e: e.memset(o, value), after)

        def add_max(o, a, b, largest, after=()):
            return DVE.put(lambda e: e.tensor_tensor_reduce(o, a, b, 1.0, 3 * LOW, ALU.add, ALU.max, largest), after)

        def red(o, a, op, negate=False, after=(), axis=AX.X):
            return DVE.put(lambda e: e.tensor_reduce(o, a, axis, op, negate=negate), after)

        def act(o, a, func, bias=None, scale=None, accum=None, after=()):
            kw = {}
            if bias is not None:
                kw["bias"] = bias
            if scale is not None:
                kw["scale"] = scale
            if accum is not None:
                kw["accum_out"] = accum
            return SC.put(lambda e: e.activation(o, a, func, **kw), after)

        def load(o, i, arr, after=()):
            SY.wait(after)
            arr.count += 16
            SY.queue.append(lambda e: e.dma_start(o, i).then_inc(arr.sem, 16))
            return (arr, arr.count)

        def again(arr):
            return now() + ([(arr, arr.count)] if arr.count else [])

        def now():
            return [(lane, lane.count) for lane in (PE, DVE, SC, PL) if lane.count]

        def fence():
            done = now() + [(a, a.count) for a in arrival_of.values() if a.count]
            for lane in (PE, DVE, SC, PL, SY):
                lane.wait(done)

        x = sb(ctx, "x_state", [128, T])[:, :]
        z = sb(ctx, "block_state", [128, T])[:, :]
        xn = sb(ctx, "x_normed", [128, T])[:, :]
        dev = sb(ctx, "ln_deviation", [128, T])[:, :]
        sq = sb(ctx, "ln_square", [128, T])[:, :]
        stats = sb(ctx, "ln_token_stats", [128, 2 * TT])[:, :]
        ident = sb(ctx, "ident", [128, 128])
        mean_w = sb(ctx, "mean_weights", [128, 128])[:, :]
        gb = sb(ctx, "adaln_scale_shift", [128, NORMS, 2, B])
        cond = sb(ctx, "cond", [128, B])[:, :]
        psum = ctx.enter_context(nc.psum_tensor("psum", [128, 8, BANK], F32))
        bank = [Slot(psum[:, i, :]) for i in range(8)]
        a_in, a_w, a_w2 = arrival("in_arrived"), arrival("weights_arrived"), arrival("weights2_arrived")
        a_out = arrival("out_stored")

        t0 = memset(ident[:, :], 0.0)
        t_id = PL.put(lambda e: e.affine_select(out=ident[:, :], in_=ident[:, :], compare_op=ALU.not_equal, fill=1.0,
                                                base=0, pattern=[[-1, 128]], channel_multiplier=1), [t0])
        eps_col = sb(ctx, "eps", [128, 1])[:, :]
        memset(eps_col, EPS)
        t_mw = memset(mean_w, 1.0 / D)
        load(x, dr["xT"], a_in)
        t_x = load(cond, dr["condT"], a_in)
        for lane in (PE, DVE, SC, PL):
            lane.wait([t_x, t_id, t_mw])

        def bank_free(i, tokens):
            bank[i].free = tuple(tokens)

        def layernorm(src, dst, per_batch=None, per_feature=None):
            after = now()
            s, d, q, y = (halves(a) for a in (src, dev, sq, dst))
            mean = [psum[:, c, 0:HALF] for c in range(2)]
            t = [mm(mean[c], mean_w, s[c], after=after) for c in range(2)]
            t = [tt(d[c], s[c], mean[c], ALU.subtract, after + [t[c]]) for c in range(2)]
            t = [act(q[c], d[c], ACT.Square, after=after + [t[c]]) for c in range(2)]
            for i in range(TT):
                tv = mm(psum[:, 4, i:i + 1], sq[:, i * 128:(i + 1) * 128], mean_w[:, 0:1], after=t)
            tv = act(stats[:, 0:TT], psum[:, 4, 0:TT], ACT.Sqrt, bias=eps_col, after=[tv])
            tv = recip(stats[:, TT:2 * TT], stats[:, 0:TT], [tv])
            for i in range(TT):
                g, k = i // 4, i % 4
                tr_ = mm(psum[:, 2 + g, k * 128:(k + 1) * 128], stats[:, TT + i:TT + i + 1].broadcast_to([128, 128]),
                         ident[:, :], after=[tv])
            t = []
            for g, (lo, hi) in enumerate(((0, BANK), (BANK, T))):
                t.append(tt(dst[:, lo:hi], dev[:, lo:hi], psum[:, 2 + g, 0:hi - lo], ALU.mult, [tr_] + after))
            t = [t[1], t[1]]
            if per_batch is not None:
                for c in range(2):
                    v = y[c].rearrange("p (b s) -> p b s", s=S)
                    for k, op in ((0, ALU.mult), (1, ALU.add)):
                        t[c] = tt(v, v, spread(per_batch[k][:, c * BH:(c + 1) * BH], S), op, [t[c]])
            if per_feature is not None:
                t = [ts(y[c], y[c], per_feature[0], per_feature[1], ALU.mult, ALU.add, [t[c]]) for c in range(2)]
            return t

        def linear(pieces, banks, after):
            toks = []
            for c in range(2):
                for k, (w, src) in enumerate(pieces):
                    t = mm(psum[:, banks[c], 0:HALF], w, halves(src)[c], k == 0, k == len(pieces) - 1, after)
                toks.append(t)
            return toks

        def to_tokens(src, w, ncols, bnk, after):
            for i in range(TT):
                t = mm(psum[:, bnk, i * ncols:(i + 1) * ncols], src[:, i * 128:(i + 1) * 128], w, True, True, after)
            return t

        def to_rows(src, m, dst, after):
            toks = []
            for g, lo in enumerate(range(0, TT, 4)):
                n = min(4, TT - lo)
                for i in range(n):
                    t = tr(psum[0:m, g, i * 128:(i + 1) * 128], src[:, lo + i, :], after)
                toks.append(cp(dst[:, lo * 128:(lo + n) * 128], psum[0:m, g, 0:n * 128], [t] + after))
            return toks

        def fold_heads(first, second, table, after):
            toks = []
            for g in range(H // 4):
                for k in range(4):
                    h = 4 * g + k
                    t = mm(psum[:, g, k * 128:(k + 1) * 128], first[:, h, :], second[:, h, :], after=after)
                toks.append(cp(table[:, 4 * g:4 * g + 4, :], psum[:, g, :].rearrange("p (h d) -> p h d", h=4),
                               [t] + after, lane=(DVE, SC)[g % 2]))
            return toks

        def scale_queries(fold, src, ring, make_slot):
            def chunk(pair, slot, g):
                bk = ring.next()
                for k in range(4):
                    t = mm(bk.ap[:, k * 2 * S:(k + 1) * 2 * S], fold[:, 4 * g + k, :],
                           src[:, pair * 2 * S:(pair + 1) * 2 * S], after=tuple(bk.free) + tuple(make_slot))
                o = slot.ap[:, :, 4 * g:4 * g + 4, :].rearrange("p b h q -> p h b q")
                i = bk.ap[:, 0:8 * S].rearrange("p (h b q) -> p h b q", h=4, b=2)
                t = act(o, i, ACT.Copy, scale=float(slot.scale), after=(t,) + tuple(slot.free))
                bk.free = (t,)
                return t
            return chunk

        def project_pair(pair, slot, table, dst, bk, bias_col):
            for h in range(H):
                t = mm(bk.ap[:, 0:2 * S], table[:, h, :], slot.ap[:, h, :], h == 0, h == H - 1,
                       tuple(bk.free) + tuple(slot.ready))
            slot.free = (t,)
            d = dst[:, pair * 2 * S:(pair + 1) * 2 * S]
            if bias_col is None:
                t = tt(d, bk.ap[:, 0:2 * S], d, ALU.add, [t])
            else:
                t = stt(d, bk.ap[:, 0:2 * S], bias_col, d, ALU.add, ALU.add, [t])
            bk.free = (t,)

        def self_attention(st, query, keys, values, table, dst, key_mask=None, bias_col=None):
            p_r = Ring([Slot(sb(st, f"self_p{i}", [128, R, S])[:, :, :]) for i in range(2)])
            pt_r = Ring([Slot(sb(st, f"self_pt{i}", [S, H * S])[:, :]) for i in range(2)])
            v_r = Ring([Slot(sb(st, f"self_v{i}", [S, 128])[:, :]) for i in range(3)])
            st_r = Ring([Slot(sb(st, f"self_stat{i}", [128, 3, R])) for i in range(2)])
            u_r = Ring([Slot(sb(st, f"self_u{i}", [128, H, 2 * S])[:, :, :]) for i in range(2)])
            start = tuple(now())
            for bk in bank:
                bk.free = start
            s_bank, v_bank, o_bank = Ring(bank[0:2]), bank[6], bank[7]
            kept = {}

            def scores(b):
                v = v_r.next()
                t = tr(v_bank.ap[0:S, 0:128], values[:, b * S:(b + 1) * S], v_bank.free)
                t = cp(v.ap, v_bank.ap[0:S, 0:128], (t,) + tuple(v.free), lane=SC)
                v_bank.free, v.ready = (t,), (t,)
                q, q_ready, q_slot = query(b)
                bk = s_bank.next()
                for r in range(R):
                    t = mm(bk.ap[:, r * S:(r + 1) * S], q[:, r * 128:(r + 1) * 128], keys[:, b * S:(b + 1) * S],
                           after=tuple(bk.free) + tuple(q_ready))
                q_slot.free = (t,)
                p, stt_ = p_r.next(), st_r.next()
                s3 = bk.ap[:, 0:R * S].rearrange("p (r s) -> p r s", r=R)
                if key_mask is not None:
                    m = key_mask[:, b * S:(b + 1) * S].unsqueeze(1).broadcast_to([128, R, S])
                    t = tt(p.ap, s3, m, ALU.add, (t,) + tuple(p.free))
                    s_in = p.ap
                else:
                    s_in = s3
                t = red(stt_.ap[:, 0, :], s_in, ALU.max, after=(t,) + tuple(stt_.free))
                t = tt(p.ap, s_in, spread(stt_.ap[:, 0, :], S), ALU.subtract, (t,) + tuple(p.free))
                bk.free = (t,)
                t = act(p.ap, p.ap, ACT.Exp, after=(t,))
                t = red(stt_.ap[:, 1, :], p.ap, ALU.add, after=(t,))
                t = recip(stt_.ap[:, 2, :], stt_.ap[:, 1, :], (t,))
                t = tt(p.ap, p.ap, spread(stt_.ap[:, 2, :], S), ALU.mult, (t,))
                p.ready, stt_.free = (t,), (t,)
                kept[b] = (v, p)

            def weigh(b):
                v, p = kept.pop(b)
                pt = pt_r.next()
                ev = []
                for g, lo in enumerate(range(0, R, 4)):
                    n = min(4, R - lo)
                    bk = bank[2 + g]
                    for i in range(n):
                        t = tr(bk.ap[0:S, i * 128:(i + 1) * 128], p.ap[:, lo + i, :], tuple(bk.free) + tuple(p.ready))
                    e = cp(pt.ap[:, lo * 128:(lo + n) * 128], bk.ap[0:S, 0:n * 128], (t,) + tuple(pt.free),
                           lane=(SC, DVE)[g])
                    bk.free = (e,)
                    ev.append(e)
                p.free = (t,)
                u = u_r.next() if b % 2 == 0 else u_r.slots[u_r.n % 2]
                outs = []
                for c in range(2):
                    bk = bank[4 + c]
                    t = mm(bk.ap[:, 0:HALF], v.ap, pt.ap[:, c * HALF:(c + 1) * HALF],
                           after=tuple(bk.free) + tuple(ev) + tuple(v.ready))
                    o = u.ap[:, 8 * c:8 * c + 8, (b % 2) * S:(b % 2 + 1) * S]
                    e = cp(o, bk.ap[:, 0:HALF].rearrange("p (h q) -> p h q", q=S), (t,) + tuple(u.free),
                           lane=(SC, DVE)[c])
                    bk.free = (e,)
                    outs.append(e)
                v.free, pt.free = (t,), (t,)
                if b % 2 == 0:
                    u.ready = tuple(outs)
                else:
                    u.ready += tuple(outs)
                    project_pair(b // 2, u, table, dst, o_bank, bias_col)

            for i in range(B + 1):
                if i < B:
                    scores(i)
                if i >= 1:
                    weigh(i - 1)

        def cross_attention(bufs, widths, hooks, query, keys, values, table, dst, mask=None, bias_col=None,
                            own_values=None):
            n_s = len(widths)
            width = sum(widths)
            step = widths[0]
            s_banks = psum[:, 0:n_s, 0:step]
            s_free = tuple(now())
            t_ring, u_bank, m_bank = bufs["t_ring"], bank[6], bank[7]
            tiles = KT + (1 if own_values is not None else 0)
            items = [(b, r) for b in range(B) for r in range(R)]
            st = {}
            u_r = bufs["u_ring"]

            def score(i):
                nonlocal s_free
                b, r = items[i]
                q, q_ready, q_slot = query(b)
                k, k_ready, k_slot = keys(b)
                for c in range(n_s):
                    t = mm(s_banks[:, c, :], q[:, r * 128:(r + 1) * 128], k[:, c * step:(c + 1) * step],
                           after=tuple(s_free) + tuple(q_ready) + tuple(k_ready))
                if r == R - 1:
                    q_slot.free = (t,)
                    k_slot.free = (t,)
                return t

            def softmax(i, t):
                nonlocal s_free
                b, r = items[i]
                p, stat = bufs["p_ring"].next(), bufs["stat_ring"].next()
                pv = p.ap[:, 0:width].rearrange("p (c n) -> p c n", c=n_s)
                if mask is not None:
                    m, m_ready, m_slot = mask(b)
                    t = add_max(pv, s_banks, m.rearrange("p (c n) -> p c n", c=n_s), stat.ap[:, 0:1],
                                (t,) + tuple(p.free) + tuple(stat.free) + tuple(m_ready))
                    s_free = (t,)
                    m_slot.free = (t,)
                    t = ts(stat.ap[:, 1:2], stat.ap[:, 0:1], -1.0, None, ALU.mult, after=(t,))
                    t = act(pv, pv, ACT.Exp, bias=stat.ap[:, 1:2], accum=stat.ap[:, 2:3], after=(t,))
                else:
                    t = red(stat.ap[:, 1:2], s_banks, ALU.max, negate=True, after=(t,) + tuple(stat.free), axis=AX.XY)
                    t = act(pv, s_banks, ACT.Exp, bias=stat.ap[:, 1:2], accum=stat.ap[:, 2:3],
                            after=(t,) + tuple(p.free))
                    s_free = (t,)
                st[i] = dict(p=p, stat=stat, exp=t)

            def transpose_in(i):
                s = st[i]
                pt = bufs["pt_ring"].next()
                s["pt"], s["pt_ready"] = pt, []
                s["todo"] = []
                for g, lo in enumerate(range(0, tiles, 4)):
                    n = min(4, tiles - lo)
                    bk = t_ring.next()
                    rows = KN if lo < KT else S
                    for k in range(n):
                        c0 = (lo + k) * KN
                        t = tr(bk.ap[0:rows, k * 128:(k + 1) * 128], s["p"].ap[:, c0:c0 + rows],
                               tuple(bk.free) + (s["exp"],))
                    args = (pt.ap[0:rows, lo:lo + n, :],
                            bk.ap[0:rows, 0:n * 128].rearrange("p (k r) -> p k r", k=n), (t,) + tuple(pt.free))
                    if g < 2:
                        e = cp(*args, lane=SC)
                        bk.free = (e,)
                        s["pt_ready"].append(e)
                    else:
                        e = cp(*args)
                        bk.free = (e,)
                        s["pt_ready"].append(e)
                s["p"].free = (t,)

            def weigh(i):
                b, r = items[i]
                s = st[i]
                v, v_ready, v_slot = values(b)
                for k in range(tiles):
                    after = (s["pt_ready"][k // 4],) + tuple(v_ready) + tuple(u_bank.free)
                    if k < KT:
                        t = mm(u_bank.ap[:, 0:128], s["pt"].ap[:, k, :], v[:, k, :], k == 0, k == tiles - 1, after)
                    else:
                        t = mm(u_bank.ap[:, 0:128], s["pt"].ap[0:S, k, :], own_values[:, b, :], False, True, after)
                s["pt"].free = (t,)
                if r == R - 1:
                    v_slot.free = (t,)
                s["u"] = t

            def inverse(i):
                s = st[i]
                s["inv"] = recip(s["stat"].ap[:, 3:4], s["stat"].ap[:, 2:3], (s["exp"],))

            def normalise(i):
                s = st[i]
                w = bufs["w_ring"].next()
                t = act(w.ap, u_bank.ap[:, 0:128], ACT.Copy, scale=s["stat"].ap[:, 3:4],
                        after=(s["u"], s["inv"]) + tuple(w.free))
                u_bank.free = (t,)
                s["stat"].free = (t,)
                s["w"], s["w_ready"] = w, t

            def turn(i):
                s = st[i]
                s["turned"] = tr(m_bank.ap[:, 0:128], s["w"].ap, (s["w_ready"],) + tuple(m_bank.free))
                s["w"].free = (s["turned"],)

            def gather(i):
                b, r = items[i]
                s = st.pop(i)
                if b % 2 == 0 and r == 0:
                    u_r.next()
                u = u_r.slots[u_r.n % len(u_r.slots)]
                lo, hi = r * 128, (r + 1) * 128
                first = True
                while lo < hi:
                    h, q = divmod(lo, S)
                    n = min(S - q, hi - lo)
                    if q == 0 and hi - lo >= 2 * S:
                        nh = (hi - lo) // S
                        o = u.ap[:, h:h + nh, (b % 2) * S:(b % 2 + 1) * S]
                        i_ = m_bank.ap[:, lo - r * 128:lo - r * 128 + nh * S].rearrange("p (h q) -> p h q", q=S)
                        n = nh * S
                    else:
                        o = u.ap[:, h, (b % 2) * S + q:(b % 2) * S + q + n]
                        i_ = m_bank.ap[:, lo - r * 128:lo - r * 128 + n]
                    t = cp(o, i_, (s["turned"],) + (tuple(u.free) if first else ()))
                    first = False
                    lo += n
                m_bank.free = (t,)
                u.ready = (t,)
                if b % 2 == 1 and r == R - 1:
                    project_pair(b // 2, u, table, dst, m_bank, bias_col)

            n = len(items)
            for i in range(n + 2):
                if i < n:
                    t = score(i)
                    hooks(*items[i])
                if 0 <= i - 2:
                    normalise(i - 2)
                if 1 <= i <= n:
                    inverse(i - 1)
                    if i < n and mask is not None:
                        pass
                if i < n:
                    softmax_dve_first = softmax
                if 1 <= i <= n:
                    transpose_in(i - 1)
                if i < n:
                    softmax(i, t)
                if 0 <= i - 2:
                    turn(i - 2)
                    gather(i - 2)
                if 1 <= i <= n:
                    weigh(i - 1)

        def cross_buffers(st, arena, pt_tiles, t_banks):
            w = pt_tiles * 128
            pw = L if pt_tiles == KT else L + S
            return dict(
                p_ring=Ring([Slot(arena[:, i * pw:(i + 1) * pw]) for i in range(2)]),
                pt_ring=Ring([Slot(arena[0:KN, 2 * pw + i * w:2 * pw + (i + 1) * w].rearrange(
                    "p (k r) -> p k r", k=pt_tiles)) for i in range(2)]),
                stat_ring=Ring([Slot(sb(st, f"cross_stat{i}", [128, 4])) for i in range(4)]),
                w_ring=Ring([Slot(sb(st, f"cross_w{i}", [128, 128])[:, :]) for i in range(2)]),
                u_ring=Ring([Slot(sb(st, f"cross_u{i}", [128, H, 2 * S])[:, :, :]) for i in range(2)]),
                t_ring=Ring([bank[i] for i in t_banks]),
            )

        def streamed(st, name, shape, source):
            slots = [Slot(sb(st, f"{name}{i}", shape), arrival(f"{name}{i}_arrived")) for i in range(2)]

            def fetch(b):
                s = slots[b % 2]
                s.ready = (load(s.ap[:, :] if len(shape) == 2 else s.ap[:, :, :], source(b), s.arrival,
                                tuple(s.free) + tuple(s.ready)),)

            return slots, fetch

        if FIRST == 0 or FIRST <= 2 <= LAST:
            with ExitStack() as st:
                w = sb(st, "adaln_w", [128, 2 * NORMS * 128])[:, :]
                bcol = sb(st, "adaln_b", [128, 2 * NORMS])[:, :]
                load(w, dr["adaln_w"], a_w)
                t_w = load(bcol, dr["adaln_b"], a_w)
                gbv = gb[:, :, :, :].rearrange("p n k b -> p (n k) b")
                for g in range(2):
                    for k in range(NORMS):
                        n = NORMS * g + k
                        t = mm(psum[:, g, k * B:(k + 1) * B], w[:, n * 128:(n + 1) * 128], cond, after=[t_w])
                    t = tt(gbv[:, NORMS * g:NORMS * (g + 1), :], psum[:, g, 0:NORMS * B].rearrange("p (n b) -> p n b", b=B),
                           spread(bcol[:, NORMS * g:NORMS * (g + 1)], B), ALU.add, [t, t_w])
                t = ts(gb[:, :, 0, :], gb[:, :, 0, :], 1.0, None, ALU.add, after=[t])
            fence()

        def adaln(n):
            return gb[:, n, 0, :], gb[:, n, 1, :]

        if FIRST <= 0 <= LAST:
            layernorm(x, z)
            with ExitStack() as st:
                cos = sb(st, "rope_cos", [128, L])[:, :]
                sin = sb(st, "rope_sin", [128, L])[:, :]
                block_diag = sb(st, "head_of_feature", [128, H])[:, :]
                wq = [sb(st, f"l0_w{i}", [128, 12 * 128])[:, :] for i in range(2)]
                wf2 = sb(st, "l0_f2", [128, 4, 128])[:, :, :]
                bias = sb(st, "l0_bias", [128, NL, 5])
                heads = [sb(st, f"l0_heads{i}", [8, H, 128])[:, :, :] for i in range(2)]
                fold = sb(st, "l0_fold", [128, H, 128])[:, :, :]
                arena = sb(st, "l0_arena", [128, 2 * L + 2 * KT * 128])[:, :]
                src_mask8 = sb(st, "src_mask8", [128, T], U8)[:, :]
                src_mask = sb(st, "src_mask", [128, T], BF16)[:, :]
                a_layer = [arrival(f"l0_w{i}_arrived") for i in range(2)]
                a_head, a_f2 = arrival("l0_heads_arrived"), arrival("l0_f2_arrived")
                qd_r = Ring([Slot(sb(st, f"l0_qd{i}", [128, H, S])[:, :, :]) for i in range(2)])
                load(cos, dr["rope_cos"], a_w)
                load(sin, dr["rope_sin"], a_w)
                load(block_diag, dr["head_of_feature"], a_w)
                load(bias[:, :, :], dr["l0_bias"], a_w)
                t_c = load(src_mask8, dr["src_mask"].partition_broadcast(128), a_w)
                t_m = ts(src_mask, src_mask8, LOW, None, ALU.mult, after=[t_c], lane=PL)
                for lane in (PE, DVE, SC, PL):
                    lane.wait([t_c])
                q_rot, k_rot = xn_q, xn_k = (sb(st, "l0_q", [128, T])[:, :], sb(st, "l0_k", [128, T])[:, :])
                tmp = dev

                def rope(dst, w0, w_swapped, scale, after):
                    for c in range(2):
                        bb = BH
                        t1 = mm(psum[:, c, 0:HALF], w0, halves(xn)[c], after=after)
                        t2 = mm(psum[:, 2 + c, 0:HALF], w_swapped, halves(xn)[c], after=after)
                        cs = cos[:, 0:S].unsqueeze(1).broadcast_to([128, bb, S])
                        sn = sin[:, 0:S].unsqueeze(1).broadcast_to([128, bb, S])
                        v = lambda a: a.rearrange("p (b s) -> p b s", s=S)
                        d, m = halves(dst)[c], halves(tmp)[c]
                        t1 = stt(v(d), v(psum[:, c, 0:HALF]), scale, cs, ALU.mult, ALU.mult, list(after) + [t1])
                        t2 = stt(v(m), v(psum[:, 2 + c, 0:HALF]), scale, sn, ALU.mult, ALU.mult, [t2, t1])
                        t = tt(d, d, m, ALU.add, [t2])
                    return t

                def block_queries(src, src_ready):
                    made = {}

                    def make(b):
                        s = qd_r.next()
                        q = src[:, b * S:(b + 1) * S].unsqueeze(1).broadcast_to([128, H, S])
                        t = tt(s.ap, q, spread(block_diag, S), ALU.mult, tuple(src_ready) + tuple(s.free), lane=PL)
                        made[b] = (s.ap.rearrange("p h q -> p (h q)"), (t,), s)

                    def get(b):
                        if b not in made:
                            make(b)
                        return made[b]
                    return make, get

                q_scale = float(np.float32(1.0) / np.float32(np.sqrt(8.0)))

                def fetch_weights(i):
                    return load(wq[i % 2], dr["l0_w"][i], a_layer[i % 2], again(a_layer[i % 2]))

                t_wq = fetch_weights(0)
                for i in range(NL):
                    w = wq[i % 2]
                    col = lambda k: w[:, k * 128:(k + 1) * 128]
                    load(heads[0], dr["l0_heads"][i, 0], a_head, again(a_head))
                    t_h = load(heads[1], dr["l0_heads"][i, 1], a_head)
                    layernorm(z, xn, per_batch=adaln(3 * i))
                    after = now() + [t_wq, t_h, t_m]
                    fold_heads(heads[0], heads[1], fold, after)
                    rope(q_rot, col(0), col(1), q_scale, now())
                    t = rope(k_rot, col(2), col(3), 1.0, now())
                    with ExitStack() as s2:
                        make, get = block_queries(q_rot, now())
                        self_attention(s2, get, k_rot, xn, fold, z, key_mask=src_mask)
                    load(heads[0], dr["l0_heads"][i, 2], a_head, again(a_head))
                    t_h = load(heads[1], dr["l0_heads"][i, 3], a_head)
                    layernorm(z, xn, per_batch=adaln(3 * i + 1))
                    fold_heads(heads[0], heads[1], fold, now() + [t_h])
                    rope(q_rot, col(4), col(5), q_scale, now())
                    fence()
                    with ExitStack() as s2:
                        bufs = cross_buffers(s2, arena, KT, (3, 4, 5))
                        ctx_t, fetch_t = streamed(s2, "ctx_t", [128, L], lambda b: dr["ctxT"][b])
                        ctx_v, fetch_v = streamed(s2, "ctx_v", [KN, KT, 128], lambda b: dr["ctxV"][b])
                        m8 = [Slot(sb(s2, f"ctx_mask8_{k}", [128, L], U8)[:, :], arrival(f"ctx_mask8_{k}_arrived")) for k in range(2)]
                        mb = [Slot(sb(s2, f"ctx_mask_{k}", [128, L], BF16)[:, :]) for k in range(2)]
                        k_slots = [Slot(sb(s2, f"l0_keys{k}", [128, L])[:, :]) for k in range(2)]
                        rt = Ring([Slot(sb(s2, f"rope_tmp{k}", [128, 500])[:, :]) for k in range(1)])
                        make, get = block_queries(q_rot, now())

                        def fetch(b):
                            fetch_t(b)
                            s = m8[b % 2]
                            s.ready = (load(s.ap, dr["ctx_mask"][b].partition_broadcast(128), s.arrival,
                                            tuple(s.free) + tuple(s.ready)),)

                        def key_chunk(b, c):
                            src, dst = ctx_t[b % 2], k_slots[b % 2]
                            cols = slice(c * 500, (c + 1) * 500)
                            k0, k1, tm = bufs["t_ring"].next(), bufs["t_ring"].next(), rt.next()
                            t1 = mm(k0.ap[:, 0:500], col(6), src.ap[:, cols], after=tuple(k0.free) + tuple(src.ready))
                            t2 = mm(k1.ap[:, 0:500], col(7), src.ap[:, cols], after=tuple(k1.free))
                            src.free = (t2,)
                            t1 = tt(dst.ap[:, cols], k0.ap[:, 0:500], cos[:, cols], ALU.mult, (t1,) + tuple(dst.free))
                            t2 = tt(tm.ap, k1.ap[:, 0:500], sin[:, cols], ALU.mult, (t2,) + tuple(tm.free))
                            k0.free, k1.free = (t1,), (t2,)
                            t = tt(dst.ap[:, cols], dst.ap[:, cols], tm.ap, ALU.add, (t1, t2), lane=PL)
                            tm.free = (t,)
                            dst.ready = (t,)

                        def mask_of(b):
                            s, d = m8[b % 2], mb[b % 2]
                            t = ts(d.ap, s.ap, LOW, None, ALU.mult, after=tuple(s.ready) + tuple(d.free), lane=PL)
                            s.free, d.ready = (t,), (t,)

                        def prepare(b, step):
                            if step in (1, 2, 3):
                                key_chunk(b, step - 1)
                            if step == 4:
                                make(b)
                                mask_of(b)

                        fetch(0)
                        fetch_v(0)
                        fetch(1)
                        for step in range(5):
                            prepare(0, step)

                        def hooks(b, r):
                            if b + 1 < B:
                                if r == 1:
                                    fetch_v(b + 1)
                                prepare(b + 1, r)
                            if r == 5 and b + 2 < B:
                                fetch(b + 2)

                        cross_attention(
                            bufs, [500] * 3, hooks, get,
                            lambda b: (k_slots[b % 2].ap, k_slots[b % 2].ready, k_slots[b % 2]),
                            lambda b: (ctx_v[b % 2].ap, ctx_v[b % 2].ready, ctx_v[b % 2]),
                            fold, z, mask=lambda b: (mb[b % 2].ap, mb[b % 2].ready, mb[b % 2]))
                    fence()
                    t_f2 = load(wf2, dr["l0_f2"][i], a_f2, again(a_f2))
                    layernorm(z, xn, per_batch=adaln(3 * i + 2))
                    if i + 1 < NL:
                        t_wq = fetch_weights(i + 1)
                    hid = arena[:, 0:4 * T].rearrange("p (f t) -> p f t", f=4)
                    after = now()
                    ready = []
                    for f in range(4):
                        t = linear([(col(8 + f), xn)], (2 * f % 4 + 4, 2 * f % 4 + 5), after + ready[-4:-2])
                        for c in range(2):
                            ready.append(act(halves(hid[:, f, :])[c], psum[:, 2 * f % 4 + 4 + c, 0:HALF], ACT.Gelu,
                                             bias=bias[:, i, f:f + 1], after=after + [t[c]]))
                    t = linear([(wf2[:, f, :], hid[:, f, :]) for f in range(4)], (0, 1), after + ready + [t_f2])
                    for c in range(2):
                        stt(halves(z)[c], psum[:, c, 0:HALF], bias[:, i, 4:5], halves(z)[c], ALU.add, ALU.add, [t[c]])
                    if i + 1 < NL:
                        t_wq = (a_layer[(i + 1) % 2], a_layer[(i + 1) % 2].count)
            tt(x, x, z, ALU.add, now())
            fence()

        def experts(st, items, gates, dst, extra=None):
            u_ring, g_ring = Ring(bank[2:6]), Ring(bank[6:8])
            h_ring = Ring([Slot(sb(st, f"hidden{i}", [128, 2, HALF])) for i in range(3)])
            r_ring = Ring([Slot(sb(st, f"rectified{i}", [128, 2, HALF])) for i in range(2)])
            gs_ring = Ring([Slot(sb(st, f"gate_spread{i}", [128, HALF])[:, :]) for i in range(4)])
            start = tuple(now())
            for bk in bank:
                bk.free = start
            spread_gate = {}
            n_down = [sum(len(it["downs"]) for it in items if it["c"] == c) for c in range(2)]
            done = [0, 0]
            last = [None, None]
            kept = {}

            def up(i):
                it = items[i]
                c = it["c"]
                toks, banks = [], []
                for w in it["ups"]:
                    bk = u_ring.next()
                    toks.append(mm(bk.ap[:, 0:HALF], w, halves(xn)[c], after=bk.free))
                    banks.append(bk)
                g, key = None, (it["gate"], c)
                if it["gate"] is not None:
                    if key not in spread_gate:
                        lhsT, rhs = gates(it["gate"], c)
                        bk, s = g_ring.next(), gs_ring.next()
                        t = mm(bk.ap[:, 0:HALF], lhsT, rhs, after=bk.free)
                        t = cp(s.ap, bk.ap[:, 0:HALF], (t,) + tuple(s.free), lane=SC)
                        bk.free, s.ready = (t,), (t,)
                        spread_gate[key] = s
                    g = spread_gate[key]
                h = h_ring.next()
                h.ready = it["activate"](banks, toks, g, h, r_ring.next())
                kept[i] = h

            def down(i):
                it, h = items[i], kept.pop(i)
                c = it["c"]
                for k, w in enumerate(it["downs"]):
                    done[c] += 1
                    t = mm(bank[c].ap[:, 0:HALF], w, h.ap[:, k, :], done[c] == 1,
                           done[c] == n_down[c] and extra is None, tuple(h.ready) + tuple(bank[c].free), signal=True)
                h.free = (t,)
                last[c] = t

            for i in range(len(items) + 2):
                if i < len(items):
                    up(i)
                if i >= 2:
                    down(i - 2)
            for c in range(2):
                t = last[c]
                if extra is not None:
                    t = mm(bank[c].ap[:, 0:HALF], extra[0], halves(extra[1])[c], False, True)
                last[c] = t
            return last

        def rank_first(first, src, scratch, cols, n, after):
            mx, cand = scratch
            t = red(mx, src, ALU.max, after=after)
            t = tt(cand, src, spread(mx, n), ALU.is_equal, [t])
            down_count = cols.unsqueeze(1).broadcast_to([128, TT, n])
            t = tt(cand, cand, down_count, ALU.mult, [t])
            t = red(mx, cand, ALU.max, after=[t])
            return tt(first, cand, spread(mx, n), ALU.is_equal, [t])

        if FIRST <= 1 <= LAST:
            E, G, TOPG = 64, 8, 4
            with ExitStack() as st:
                up_w = sb(st, "moe_up", [128, E * 64])[:, :]
                down_w = sb(st, "moe_down", [128, E // 2, 128])[:, :, :]
                sh_up = sb(st, "moe_shared_up", [128, 256])[:, :]
                sh_down = sb(st, "moe_shared_down", [128, 2, 128])[:, :, :]
                rw = sb(st, "moe_router", [128, E])[:, :]
                rb = sb(st, "moe_router_bias", [128, E])[:, :]
                lower = sb(st, "moe_lower_group", [128, G, G])[:, :, :]
                load(rw, dr["moe_router"], a_w2)
                load(rb, dr["moe_bias"].partition_broadcast(128), a_w2)
                t_r = load(lower, dr["moe_lower"].rearrange("a b -> (a b)").partition_broadcast(128).rearrange(
                    "p (a b) -> p a b", a=G), a_w2)
                load(up_w, dr["moe_up"], a_w)
                load(down_w, dr["moe_down"], a_w)
                load(sh_up, dr["moe_shared_up"], a_w)
                t_w = load(sh_down, dr["moe_shared_down"], a_w)
                grid = lambda name, *shape: sb(st, name, [128, TT, *shape])
                score = grid("moe_score", E)[:, :, :]
                sfc = grid("moe_biased", E)[:, :, :]
                top = grid("moe_group_top", G, 8)
                gs = grid("moe_group_score", G)[:, :, :]
                cmp_, eq = grid("moe_cmp", G, G)[:, :, :, :], grid("moe_eq", G, G)[:, :, :, :]
                keep = grid("moe_group_keep", G)[:, :, :]
                m8 = grid("moe_top8", 8)
                rep = grid("moe_replaced", E)
                tot = sb(st, "moe_total", [128, 2, TT])
                wide = sb(st, "moe_expert_rows", [E, E * 64])[:, :]
                cp(wide.rearrange("p (e i) -> p e i", e=E), spread(ident[0:E, 0:E], 64), lane=DVE)
                combT = sb(st, "moe_combine_rows", [E, T])[:, :]
                layernorm(x, xn)
                t = to_tokens(xn, rw, E, 7, now() + [t_r])
                t = act(score, psum[:, 7, 0:TT * E].rearrange("p (t e) -> p t e", t=TT), ACT.Sigmoid, after=[t])
                t = tt(sfc, score, rb.unsqueeze(1).broadcast_to([128, TT, E]), ALU.add, [t, t_r])
                for i in range(TT):
                    for g in range(G):
                        t1 = max8(top[:, i, g, :], sfc[:, i, g * 8:g * 8 + 8], [t])
                t = tt(gs, top[:, :, :, 0], top[:, :, :, 1], ALU.add, [t1])
                other = gs.unsqueeze(2).broadcast_to([128, TT, G, G])
                mine = gs.unsqueeze(3).broadcast_to([128, TT, G, G])
                t1 = tt(cmp_, other, mine, ALU.is_gt, [t])
                t2 = tt(eq, other, mine, ALU.is_equal, [t])
                for i in range(TT):
                    t3 = tt(eq[:, i, :, :], eq[:, i, :, :], lower, ALU.mult, [t2])
                t = tt(cmp_, cmp_, eq, ALU.add, [t1, t3])
                t = red(gs, cmp_, ALU.add, after=[t])
                t = ts(keep, gs, float(TOPG), None, ALU.is_lt, after=[t])
                sfg = sfc.rearrange("p t (g k) -> p (t g) k", g=G)
                t = tt(sfg, sfg, spread(keep.rearrange("p t g -> p (t g)"), E // G), ALU.mult, [t])
                for i in range(TT):
                    t1 = max8(m8[:, i, :], sfc[:, i, :], [t])
                    t1 = replace8(rep[:, i, :], m8[:, i, :], sfc[:, i, :], [t1])
                t = tt(sfc, rep[:, :, :], sfc, ALU.is_lt, [t1])
                t = tt(sfc, sfc, score, ALU.mult, [t])
                t = red(tot[:, 0, :], sfc, ALU.add, after=[t])
                t = ts(tot[:, 0, :], tot[:, 0, :], 1e-20, None, ALU.add, after=[t])
                t = recip(tot[:, 1, :], tot[:, 0, :], [t])
                t = tt(sfc, sfc, spread(tot[:, 1, :], E), ALU.mult, [t])
                t = ts(sfc, sfc, 2.5, None, ALU.mult, after=[t])
                to_rows(sfc, E, combT, [t])
                for lane in (PE,):
                    lane.wait([t_w])

                def relu2(banks, toks, g, h, r):
                    t = act(r.ap[:, 0, :], banks[0].ap[:, 0:HALF], ACT.Relu, after=(toks[0],) + tuple(r.free))
                    banks[0].free = (t,)
                    if g is None:
                        t = tt(h.ap[:, 0, :], r.ap[:, 0, :], r.ap[:, 0, :], ALU.mult, (t,) + tuple(h.free))
                    else:
                        t = tt(r.ap[:, 1, :], r.ap[:, 0, :], g.ap, ALU.mult, (t,) + tuple(g.ready))
                        g.free = (t,)
                        t = tt(h.ap[:, 0, :], r.ap[:, 1, :], r.ap[:, 0, :], ALU.mult, (t,) + tuple(h.free))
                    r.free = (t,)
                    return (t,)

                items = [dict(c=c, ups=[up_w[:, p * 128:(p + 1) * 128]], downs=[down_w[:, p, :]], gate=p, activate=relu2)
                         for p in range(E // 2) for c in range(2)]
                items += [dict(c=c, ups=[sh_up[:, p * 128:(p + 1) * 128]], downs=[sh_down[:, p, :]], gate=None,
                               activate=relu2) for p in range(2) for c in range(2)]
                last = experts(st, items, lambda p, c: (wide[:, p * 128:(p + 1) * 128], halves(combT)[c]), x)
                for c in range(2):
                    tt(halves(x)[c], bank[c].ap[:, 0:HALF], halves(x)[c], ALU.add, [last[c]])
            fence()

        HD1 = 64

        def attention_tables(st, names, tables, arr):
            bufs = [sb(st, f"by_head{i}", [HD1, H, 128])[:, :, :] for i in range(2)]
            for k, table in enumerate(tables):
                load(bufs[0], dr[names[2 * k]], arr, again(arr))
                t = load(bufs[1], dr[names[2 * k + 1]], arr)
                fold_heads(bufs[0], bufs[1], table, now() + [t])

        def pair_queries(slots, fold, src, ring):
            chunk_ = scale_queries(fold, src, ring, now())

            def chunk(pair, g):
                s = slots[pair % 2]
                t = chunk_(pair, s, g)
                s.ready = (t,) if g == 0 else s.ready + (t,)

            def get(b):
                s = slots[(b // 2) % 2]
                return s.ap[:, b % 2, :, :].rearrange("p h q -> p (h q)"), s.ready, s
            return chunk, get

        if FIRST <= 2 <= LAST:
            layernorm(x, z)
            with ExitStack() as st:
                bo = sb(st, "l1_bias", [128, 2 + 8 + 1])
                a_h = arrival("l1_heads_arrived")
                t_b = load(bo[:, :], dr["l1_bias"], a_w)
                w1 = sb(st, "l1_ff1", [128, 8 * 128])[:, :]
                w2 = sb(st, "l1_ff2", [128, 4, 128])[:, :, :]
                load(w1, dr["l1_ff1"], a_w)
                t_w = load(w2, dr["l1_ff2"], a_w)
                for lane in (PE, DVE, SC):
                    lane.wait([t_w])
                q_fold = sb(st, "l1_q_fold", [128, H, 128])[:, :, :]
                o_fold = sb(st, "l1_o_fold", [128, H, 128])[:, :, :]
                q_slots = [Slot(sb(st, f"l1_q{i}", [128, 2, H, S])) for i in range(2)]
                for s in q_slots:
                    s.scale = 1.0 / np.sqrt(HD1)
                with ExitStack() as s2:
                    attention_tables(s2, ["l1_q1", "l1_k1", "l1_v1", "l1_o1"], [q_fold, o_fold], a_h)
                    layernorm(z, xn, per_batch=adaln(3 * NL))
                    chunk, get = pair_queries(q_slots, q_fold, xn, Ring([bank[6]]))

                    def query(b):
                        if b % 2 == 0:
                            for g in range(4):
                                chunk(b // 2, g)
                        return get(b)
                    self_attention(s2, query, xn, xn, o_fold, z, bias_col=bo[:, 0:1])
                fence()
                with ExitStack() as s2:
                    with ExitStack() as s3:
                        attention_tables(s3, ["l1_q2", "l1_k2", "l1_v2", "l1_o2"], [q_fold, o_fold], a_h)
                        layernorm(z, xn, per_batch=adaln(3 * NL + 1))
                        fence()
                    arena = sb(s2, "l1_arena", [128, 2 * L + 2 * KT * 128])[:, :]
                    bufs = cross_buffers(s2, arena, KT, (3, 4, 5))
                    for bk in bank:
                        bk.free = tuple(now())
                    for s in q_slots:
                        s.free = tuple(now())
                    ctx_t, fetch_t = streamed(s2, "ctx_t", [128, L], lambda b: dr["ctxT"][b])
                    ctx_v, fetch_v = streamed(s2, "ctx_v", [KN, KT, 128], lambda b: dr["ctxV"][b])
                    chunk, get = pair_queries(q_slots, q_fold, xn, bufs["t_ring"])
                    fetch_t(0)
                    fetch_v(0)
                    for g in range(4):
                        chunk(0, g)

                    def hooks(b, r):
                        if r == 1 and b + 1 < B:
                            fetch_t(b + 1)
                            fetch_v(b + 1)
                        if b % 2 == 1 and b + 1 < B and 1 <= r <= 4:
                            chunk(b // 2 + 1, r - 1)

                    cross_attention(bufs, [500] * 3, hooks, get,
                                    lambda b: (ctx_t[b % 2].ap, ctx_t[b % 2].ready, ctx_t[b % 2]),
                                    lambda b: (ctx_v[b % 2].ap, ctx_v[b % 2].ready, ctx_v[b % 2]),
                                    o_fold, z, bias_col=bo[:, 1:2])
                fence()
                with ExitStack() as s2:
                    layernorm(z, xn, per_batch=adaln(3 * NL + 2))
                    hid = sb(s2, "l1_hidden", [128, 4, T])
                    gate = sb(s2, "l1_gate", [128, 4, T])
                    after = now()
                    ready, freed = [], []
                    for f in range(4):
                        bks = (0, 1, 2, 3) if f % 2 == 0 else (4, 5, 6, 7)
                        aft = after + freed[-2:] if f < 2 else after + freed[2 * (f - 2):2 * (f - 1)]
                        tg = linear([(w1[:, (4 + f) * 128:(5 + f) * 128], xn)], bks[0:2], aft)
                        ta = linear([(w1[:, f * 128:(f + 1) * 128], xn)], bks[2:4], aft)
                        for c in range(2):
                            g = halves(gate[:, f, :])[c]
                            t = act(g, psum[:, bks[c], 0:HALF], ACT.Gelu, bias=bo[:, 6 + f:7 + f], after=[tg[c]] + after)
                            t = stt(halves(hid[:, f, :])[c], psum[:, bks[2 + c], 0:HALF], bo[:, 2 + f:3 + f], g, ALU.add,
                                    ALU.mult, [t, ta[c]])
                            freed.append(t)
                    t = linear([(w2[:, f, :], hid[:, f, :]) for f in range(4)], (0, 1), now())
                    for c in range(2):
                        stt(halves(z)[c], psum[:, c, 0:HALF], bo[:, 10:11], halves(z)[c], ALU.add, ALU.add, [t[c]])
            tt(x, x, z, ALU.add, now())
            fence()

        if FIRST <= 3 <= LAST:
            E, CAP = 8, T // 8
            with ExitStack() as st:
                up_w = sb(st, "ec_up", [128, E * 256])[:, :]
                down_w = sb(st, "ec_down", [128, E * 2, 128])[:, :, :]
                wg = sb(st, "ec_gate_w", [128, E])[:, :]
                down_count = sb(st, "ec_index_down", [128, E])[:, :]
                load(wg, dr["ec_gate"], a_w2)
                t_r = load(down_count, dr["index_down"].partition_broadcast(128), a_w2)
                load(up_w, dr["ec_up"], a_w)
                t_w = load(down_w, dr["ec_down"], a_w)
                grid = lambda name, *shape: sb(st, name, [128, TT, *shape])
                probs, sel_t, val, cand, onehot = (grid(f"ec_{n}", E)[:, :, :] for n in
                                                   ("probs", "chosen", "value", "candidate", "expert"))
                tok = sb(st, "ec_token", [128, 3, TT])
                rows = [sb(st, f"ec_rows{i}", [E, T])[:, :] for i in range(2)]
                m8 = sb(st, "ec_top8", [E, 8])[:, :]
                gate_rows = sb(st, "ec_gate_rows", [E, T])[:, :]
                layernorm(x, xn)
                t = to_tokens(xn, wg, E, 7, now() + [t_r])
                lg = psum[:, 7, 0:TT * E].rearrange("p (t e) -> p t e", t=TT)
                t1 = red(tok[:, 0, :], lg, ALU.max, after=[t])
                t = tt(probs, lg, spread(tok[:, 0, :], E), ALU.subtract, [t1])
                t = act(probs, probs, ACT.Exp, after=[t])
                t = red(tok[:, 0, :], probs, ALU.add, after=[t])
                t = recip(tok[:, 1, :], tok[:, 0, :], [t])
                t = tt(probs, probs, spread(tok[:, 1, :], E), ALU.mult, [t])
                t = to_rows(probs, E, rows[0], [t])
                src = rows[0]
                orig = sb(st, "ec_rows_kept", [E, T])[:, :]
                t = [cp(orig, rows[0], t)]
                for k in range(CAP // 8):
                    t = [max8(m8, src, t)]
                    d = rows[(k + 1) % 2]
                    t = [replace8(d, m8, src, t)]
                    src = d
                t = tt(orig, src, orig, ALU.not_equal, t)
                for i in range(TT):
                    t1 = tr(psum[:, 6, i * E:(i + 1) * E], orig[:, i * 128:(i + 1) * 128], [t])
                t = cp(sel_t, psum[:, 6, 0:TT * E].rearrange("p (t e) -> p t e", t=TT), [t1])
                t1 = red(tok[:, 2, :], sel_t, ALU.max, after=[t])
                t = ts(val, sel_t, -LOW, LOW, ALU.mult, ALU.add, after=[t])
                t = tt(val, val, spread(tok[:, 2, :], E), ALU.mult, [t, t1])
                t = tt(val, val, probs, ALU.add, [t])
                t = rank_first(onehot, val, (tok[:, 0, :], cand), down_count, E, [t])
                t = tt(onehot, onehot, probs, ALU.mult, [t])
                to_rows(onehot, E, gate_rows, [t])
                PE.wait([t_w])

                def gelu_gated(banks, toks, g, h, r):
                    outs = []
                    for k in range(2):
                        t = act(r.ap[:, k, :], banks[k].ap[:, 0:HALF], ACT.Gelu, after=(toks[k],) + tuple(r.free))
                        banks[k].free = (t,)
                        t = tt(h.ap[:, k, :], r.ap[:, k, :], g.ap, ALU.mult, (t,) + tuple(h.free) + tuple(g.ready))
                        outs.append(t)
                    g.free, r.free = (t,), (t,)
                    return tuple(outs)

                items = [dict(c=c, ups=[up_w[:, (2 * e + f) * 128:(2 * e + f + 1) * 128] for f in range(2)],
                              downs=[down_w[:, 2 * e + f, :] for f in range(2)], gate=e, activate=gelu_gated)
                         for e in range(E) for c in range(2)]
                last = experts(st, items, lambda g, c: (ident[0:E, g:g + 1].broadcast_to([E, 128]),
                                                        halves(gate_rows)[c]), x)
                for c in range(2):
                    tt(halves(x)[c], bank[c].ap[:, 0:HALF], halves(x)[c], ALU.add, [last[c]])
            fence()

        if LAST >= 4 and FIRST <= 6:
            c_mean = sb(ctx, "context_mean", [KN, B, KT])
            c_rstd = sb(ctx, "context_rstd", [KN, B, KT])
            with ExitStack() as st:
                slots, fetch = streamed(st, "ctx_v", [KN, KT, 128], lambda b: dr["ctxV"][b])
                part = [sb(st, f"stat_part{i}", [KN, KT, 6]) for i in range(2)]
                both = sb(st, "stat_mean_var", [KN, B, KT, 2])
                fetch(0)
                for b in range(B):
                    if b + 1 < B:
                        fetch(b + 1)
                    s = slots[b % 2]
                    for k in range(KT):
                        t = bn_stats(part[b % 2][:, k, :], s.ap[:, k, :],
                                     tuple(s.ready) + ((t,) if b >= 2 and k == 0 else ()))
                    s.free = (t,)
                    for k in range(KT):
                        t = bn_aggr(both[:, b, k, :], part[b % 2][:, k, :], [t])
                t = act(c_rstd[:, :, :], both[:, :, :, 1], ACT.Sqrt, bias=eps_col[0:KN, :], after=[t])
                t = recip(c_rstd[:, :, :], c_rstd[:, :, :], [t])
                cp(c_mean[:, :, :], both[:, :, :, 0], [t])
            fence()

        def normalise_context(b, buf, w_row, b_row, after):
            for k in range(KT):
                t = ts(buf[:, k, :], buf[:, k, :], c_mean[:, b, k:k + 1], c_rstd[:, b, k:k + 1], ALU.subtract, ALU.mult,
                       after=after, lane=PL)
            t = tt(buf, buf, w_row.unsqueeze(1).broadcast_to([KN, KT, 128]), ALU.mult, [t], lane=PL)
            return tt(buf, buf, b_row.unsqueeze(1).broadcast_to([KN, KT, 128]), ALU.add, [t], lane=PL)

        if FIRST <= 4 <= LAST:
            with ExitStack() as st:
                aff = sb(st, "l2_affine", [128, 2])
                w_row = sb(st, "l2_ctx_w", [KN, 128])[:, :]
                b_row = sb(st, "l2_ctx_b", [KN, 128])[:, :]
                cond1 = sb(st, "cond_plus_1", [128, B])[:, :]
                a_h = arrival("l2_heads_arrived")
                load(aff[:, :], dr["l2_affine"], a_w)
                load(w_row, dr["l2_ln1_w"].partition_broadcast(KN), a_w)
                t_w = load(b_row, dr["l2_ln1_b"].partition_broadcast(KN), a_w)
                DVE.wait([t_w])
                PL.wait([t_w])
                ts(cond1, cond, 1.0, None, ALU.add)
                q_fold = sb(st, "l2_q_fold", [128, H, 128])[:, :, :]
                o_fold = sb(st, "l2_o_fold", [128, H, 128])[:, :, :]
                with ExitStack() as s3:
                    attention_tables(s3, ["l2_q", "l2_k", "l2_v", "l2_o"], [q_fold, o_fold], a_h)
                layernorm(x, xn)
                layernorm(xn, xn, per_feature=(aff[:, 0:1], aff[:, 1:2]))
                v = xn.rearrange("p (b s) -> p b s", s=S)
                t = tt(v, v, spread(cond1, S), ALU.mult, now())
                t = tt(v, v, spread(cond, S), ALU.add, [t])
                lat = sb(st, "l2_latents", [S, B, 128])[:, :, :]
                for g in range(4):
                    for k in range(4):
                        t1 = tr(psum[0:S, g, k * 128:(k + 1) * 128], xn[:, (4 * g + k) * S:(4 * g + k + 1) * S], [t])
                    cp(lat[:, 4 * g:4 * g + 4, :], psum[0:S, g, :].rearrange("p (k d) -> p k d", k=4), [t1])
                fence()
                arena = sb(st, "l2_arena", [128, 2 * (L + S) + 2 * (KT + 1) * 128])[:, :]
                bufs = cross_buffers(st, arena, KT + 1, (4, 5))
                q_slots = [Slot(sb(st, f"l2_q{i}", [128, 2, H, S])) for i in range(2)]
                for s in q_slots:
                    s.scale = 1.0 / np.sqrt(HD1)
                for bk in bank:
                    bk.free = tuple(now())
                ctx_v, fetch_v = streamed(st, "ctx_v", [KN, KT, 128], lambda b: dr["ctxV"][b])
                k_slots = [Slot(sb(st, f"l2_keys{i}", [128, L + S])[:, :]) for i in range(2)]
                chunk, get = pair_queries(q_slots, q_fold, xn, bufs["t_ring"])

                def norm(b):
                    s = ctx_v[b % 2]
                    s.ready = (normalise_context(b, s.ap[:, :, :], w_row, b_row, s.ready),)

                def key_chunk(b, c):
                    s, k_ = ctx_v[b % 2], k_slots[b % 2]
                    bk = bufs["t_ring"].next()
                    for k in range(4):
                        t = tr(bk.ap[:, k * KN:(k + 1) * KN], s.ap[:, 4 * c + k, :], tuple(s.ready) + tuple(bk.free))
                    e = cp(k_.ap[:, c * 500:(c + 1) * 500], bk.ap[:, 0:500], (t,) + tuple(k_.free), lane=(SC, DVE, SC)[c])
                    bk.free = (e,)
                    if c == 0:
                        k_.ready = (e, cp(k_.ap[:, L:L + S], xn[:, b * S:(b + 1) * S], tuple(k_.free), lane=PL))
                    else:
                        k_.ready += (e,)

                fetch_v(0)
                norm(0)
                for c in range(3):
                    key_chunk(0, c)
                for g in range(4):
                    chunk(0, g)

                def hooks(b, r):
                    if b + 1 < B:
                        if r == 1:
                            fetch_v(b + 1)
                            norm(b + 1)
                        if r in (4, 5, 6):
                            key_chunk(b + 1, r - 4)
                        if b % 2 == 1 and r < 4:
                            chunk(b // 2 + 1, r)

                cross_attention(bufs, [(L + S) // 4] * 4, hooks, get,
                                lambda b: (k_slots[b % 2].ap, k_slots[b % 2].ready, k_slots[b % 2]),
                                lambda b: (ctx_v[b % 2].ap, ctx_v[b % 2].ready, ctx_v[b % 2]),
                                o_fold, x, own_values=lat)
            fence()

        if FIRST <= 5 <= LAST:
            E = 8
            with ExitStack() as st:
                w1 = sb(st, "sm_w1", [128, E * 512])[:, :]
                w3 = sb(st, "sm_w3", [128, E * 512])[:, :]
                w2 = sb(st, "sm_w2", [128, E * 4, 128])[:, :, :]
                wg = sb(st, "sm_gate_w", [128, E])[:, :]
                down_count = sb(st, "sm_index_down", [128, E])[:, :]
                load(wg, dr["sm_gate"], a_w2)
                t_r = load(down_count, dr["index_down"].partition_broadcast(128), a_w2)
                load(w1, dr["sm_w1"], a_w)
                load(w3, dr["sm_w3"], a_w)
                t_w = load(w2, dr["sm_w2"], a_w)
                grid = lambda name: sb(st, name, [128, TT, E])[:, :, :]
                sco, mag, fac, cand, hot, s2_, ex, gate = (grid(f"sm_{n}") for n in (
                    "scores", "magnitude", "factor", "candidate", "onehot", "rest", "exp", "gate"))
                mx, mx2, sm_, inv = (sb(st, f"sm_token_{n}", [128, TT])[:, :] for n in ("max", "tmp", "sum", "inv"))
                gate_rows = sb(st, "sm_gate_rows", [E, T])[:, :]
                layernorm(x, xn)
                t = to_tokens(xn, wg, E, 7, now() + [t_r])
                t = cp(sco, psum[:, 7, 0:TT * E].rearrange("p (t e) -> p t e", t=TT), [t])
                t = act(mag, sco, ACT.Abs, after=[t])
                src = sco
                for k in range(2):
                    t = red(mx, src, ALU.max, after=[t])
                    t = rank_first(hot, src, (mx2, cand), down_count, E, [t])
                    t = tt(fac, mag, spread(mx, E), ALU.max, [t])
                    t = ts(fac, fac, 0.02, None, ALU.mult, after=[t])
                    t = tt(ex, spread(mx, E), sco, ALU.subtract, [t])
                    t = tt(fac, ex, fac, ALU.is_gt, [t])
                    t = ts(fac, fac, -1.0, 1.0, ALU.mult, ALU.add, after=[t])
                    t = tt(ex, src, spread(mx, E), ALU.subtract, [t])
                    t = act(ex, ex, ACT.Exp, after=[t])
                    t = tt(ex, ex, fac, ALU.mult, [t])
                    t = red(sm_, ex, ALU.add, after=[t])
                    t = recip(inv, sm_, [t])
                    if k == 0:
                        t = tt(gate, hot, spread(inv, E), ALU.mult, [t])
                        t = stt(s2_, hot, LOW, sco, ALU.mult, ALU.add, [t])
                        src = s2_
                    else:
                        t = tt(hot, hot, spread(inv, E), ALU.mult, [t])
                        t = tt(gate, gate, hot, ALU.add, [t])
                to_rows(gate, E, gate_rows, [t])
                PE.wait([t_w])

                def silu_gated(banks, toks, g, h, r):
                    t = act(r.ap[:, 0, :], banks[0].ap[:, 0:HALF], ACT.Silu, after=(toks[0],) + tuple(r.free))
                    banks[0].free = (t,)
                    t = tt(r.ap[:, 1, :], r.ap[:, 0, :], banks[1].ap[:, 0:HALF], ALU.mult, (t, toks[1]))
                    banks[1].free = (t,)
                    t = tt(h.ap[:, 0, :], r.ap[:, 1, :], g.ap, ALU.mult, (t,) + tuple(h.free) + tuple(g.ready))
                    g.free, r.free = (t,), (t,)
                    return (t,)

                items = [dict(c=c, ups=[w1[:, (4 * e + f) * 128:(4 * e + f + 1) * 128],
                                        w3[:, (4 * e + f) * 128:(4 * e + f + 1) * 128]],
                              downs=[w2[:, 4 * e + f, :]], gate=e, activate=silu_gated)
                         for e in range(E) for c in range(2) for f in range(4)]
                last = experts(st, items, lambda g, c: (ident[0:E, g:g + 1].broadcast_to([E, 128]),
                                                        halves(gate_rows)[c]), x)
                for c in range(2):
                    tt(halves(x)[c], bank[c].ap[:, 0:HALF], halves(x)[c], ALU.add, [last[c]])
            fence()

        if FIRST <= 6 <= LAST:
            with ExitStack() as st:
                xin = sb(st, "slot_context", [KN, B, KT, 128])
                wts = sb(st, "slot_w", [128, 6, 128])
                colv = sb(st, "slot_cols", [128, 14])
                w_row = sb(st, "slot_ctx_w", [KN, 128])[:, :]
                b_row = sb(st, "slot_ctx_b", [KN, 128])[:, :]
                load(wts[:, :, :], dr["slot_w"], a_w)
                load(colv[:, :], dr["slot_cols"], a_w)
                load(w_row, dr["slot_lnkv_g"].partition_broadcast(KN), a_w)
                t_w = load(b_row, dr["slot_lnkv_b"].partition_broadcast(KN), a_w)
                for lane in (PE, DVE, SC, PL):
                    lane.wait([t_w])
                cq = {n: colv[:, i:i + 1] for i, n in enumerate((
                    "mu", "logsig", "lnq_g", "lnq_b", "lnm_g", "lnm_b", "lnp_g", "lnp_b", "bk", "bv", "bq", "bu", "b1",
                    "b2"))}
                wk_t, wq, wv, wu, w1, w2 = (wts[:, i, :] for i in range(6))
                sig = sb(st, "slot_sigma", [128, 1])[:, :]
                ones = sb(st, "slot_ones", [128, 128])[:, :]
                bk_wide = cq["bk"].broadcast_to([128, 128])
                memset(ones, 1.0)
                act(sig, cq["logsig"], ACT.Exp)
                ring4 = [arrival(f"slot_ctx{i}_arrived") for i in range(4)]
                ready = {}
                for b in range(B):
                    a = ring4[b % 4]
                    t = load(xin[:, b, :, :], dr["ctxV"][b], a, [(a, a.count)] if a.count else [])
                    ready[b] = normalise_context(b, xin[:, b, :, :], w_row, b_row, [t])
                layernorm(x, z, per_feature=(sig, cq["mu"]))
                big = lambda n: sb(st, f"slot_{n}", [128, T])[:, :]
                qT, q2, cbk, upd = big("q"), big("q_folded"), big("bk_q"), big("update")
                x_t = [Slot(sb(st, f"slot_ctxT{i}", [128, L])[:, :]) for i in range(2)]
                at_ = [Slot(sb(st, f"slot_attn{i}", [KN, KT, S])[:, :, :]) for i in range(2)]
                stat = [sb(st, f"slot_stat{i}", [KN, 3, KT]) for i in range(2)]
                rden = [sb(st, f"slot_rden{i}", [128, S])[:, :] for i in range(2)]
                root = float(np.sqrt(np.float32(D)))

                def dense(dst, w, src, bias, after=None, plus=None, func=None, rhs=None):
                    after = now()
                    t = linear([(w, src)], (0, 1), after)
                    for c in range(2):
                        o, i = halves(dst)[c], psum[:, c, 0:HALF]
                        if func is not None:
                            act(o, i, func, bias=bias, after=after + [t[c]])
                        elif plus is not None:
                            stt(o, i, bias, halves(plus)[c], ALU.add, ALU.add, after + [t[c]])
                        elif bias is not None:
                            ts(o, i, bias, None, ALU.add, after=after + [t[c]])
                        else:
                            cp(o, i, after + [t[c]])

                for it in range(3):
                    layernorm(z, xn, per_feature=(cq["lnq_g"], cq["lnq_b"]))
                    dense(qT, wq, xn, cq["bq"])
                    dense(q2, wk_t, qT, None)
                    dense(cbk, bk_wide, qT, None)
                    start = tuple(now())
                    for bk in bank:
                        bk.free = start
                    xp = {}

                    def turn_ctx(b):
                        s = x_t[b % 2]
                        toks = []
                        for g in range(3):
                            bk = bank[g]
                            for k in range(4):
                                t = tr(bk.ap[:, k * KN:(k + 1) * KN], xin[:, b, 4 * g + k, :], tuple(bk.free) + (ready[b],))
                            e = cp(s.ap[:, g * 500:(g + 1) * 500], bk.ap[:, 0:500], (t,) + tuple(s.free),
                                   lane=(SC, DVE, SC)[g])
                            bk.free = (e,)
                            toks.append(e)
                        s.ready = tuple(toks)

                    def slot_softmax(b):
                        s, a, sp = x_t[b % 2], at_[b % 2], stat[b % 2]
                        for k in range(KT):
                            bk = bank[3 + k // 6]
                            t = mm(bk.ap[0:KN, (k % 6) * S:(k % 6 + 1) * S], s.ap[:, k * KN:(k + 1) * KN],
                                   q2[:, b * S:(b + 1) * S], after=tuple(s.ready) + tuple(bk.free))
                        s.free = (t,)
                        lg = psum[0:KN, 3:5, 0:6 * S].rearrange("p c (k s) -> p c k s", s=S)
                        av = a.ap.rearrange("p (c k) s -> p c k s", c=2)
                        cb = cbk[0:KN, b * S:(b + 1) * S].unsqueeze(1).unsqueeze(1).broadcast_to([KN, 2, 6, S])
                        t = tt(av, lg, cb, ALU.add, (t,) + tuple(a.free))
                        bank[3].free = bank[4].free = (t,)
                        t = red(sp[:, 0, :], a.ap, ALU.max, after=(t,))
                        t = tt(a.ap, a.ap, spread(sp[:, 0, :], S), ALU.subtract, (t,))
                        t = act(a.ap, a.ap, ACT.Exp, scale=root, after=(t,))
                        t = red(sp[:, 1, :], a.ap, ALU.add, after=(t,))
                        t = recip(sp[:, 2, :], sp[:, 1, :], (t,))
                        t = tt(a.ap, a.ap, spread(sp[:, 2, :], S), ALU.mult, (t,))
                        t = ts(a.ap, a.ap, 1e-8, None, ALU.add, after=(t,))
                        a.ready = (t,)

                    def slot_update(b):
                        a = at_[b % 2]
                        for k in range(KT):
                            t = mm(bank[5].ap[:, 0:S], xin[:, b, k, :], a.ap[:, k, :], k == 0, k == KT - 1,
                                   tuple(a.ready) + tuple(bank[5].free))
                        for k in range(KT):
                            t2 = mm(bank[6].ap[:, 0:S], ones[0:KN, :], a.ap[:, k, :], k == 0, k == KT - 1,
                                    tuple(bank[6].free))
                        a.free = (t2,)
                        t3 = recip(rden[b % 2], bank[6].ap[:, 0:S], (t2,))
                        bank[6].free = (t3,)
                        t = tt(upd[:, b * S:(b + 1) * S], bank[5].ap[:, 0:S], rden[b % 2], ALU.mult, (t, t3))
                        bank[5].free = (t,)

                    for i in range(B + 2):
                        if i < B:
                            turn_ctx(i)
                        if 1 <= i <= B:
                            slot_softmax(i - 1)
                        if i >= 2:
                            slot_update(i - 2)
                    dense(qT, wv, upd, cq["bv"])
                    dense(z, wu, qT, cq["bu"], plus=z)
                    layernorm(z, xn, per_feature=(cq["lnm_g"], cq["lnm_b"]))
                    dense(qT, w1, xn, cq["b1"], func=ACT.Gelu)
                    dense(z, w2, qT, cq["b2"], plus=z)
                    v = z.rearrange("p (b s) -> p b s", s=S)
                    tt(v, v, spread(cond, S), ALU.add, now())
                    layernorm(z, z, per_feature=(cq["lnp_g"], cq["lnp_b"]))
                tt(x, x, z, ALU.add, now())
            fence()

        if FIRST <= 7 <= LAST:
            DEPTH, LEAVES = 4, 16
            NODES = LEAVES - 1
            with ExitStack() as st:
                w1 = sb(st, "fff_w1", [128, 3, LEAVES * 64])
                w2 = sb(st, "fff_w2", [128, 3, LEAVES // 2, 128])
                b1 = sb(st, "fff_b1", [128, 3, LEAVES // 2])
                b2 = sb(st, "fff_b2", [LEAVES, 3, 128])
                nw = sb(st, "fff_node_w", [128, 3 * NODES])[:, :]
                nb = sb(st, "fff_node_b", [128, 3 * NODES])[:, :]
                load(nw, dr["fff_node_w"], a_w2)
                t_r = load(nb, dr["fff_node_b"].partition_broadcast(128), a_w2)
                load(w1[:, :, :], dr["fff_w1"], a_w)
                load(w2[:, :, :, :], dr["fff_w2"], a_w)
                load(b1[:, :, :], dr["fff_b1"], a_w)
                t_w = load(b2[:, :, :], dr["fff_b2"], a_w)
                layernorm(x, xn)
                bit = sb(st, "fff_bit", [128, TT, 3 * NODES])
                path = [sb(st, f"fff_path{d}", [128, TT, 3, 2 ** d]) for d in range(DEPTH + 1)]
                t = to_tokens(xn, nw, 3 * NODES, 7, now() + [t_r])
                t = tt(bit[:, :, :], psum[:, 7, 0:TT * 3 * NODES].rearrange("p (t n) -> p t n", t=TT),
                       nb.unsqueeze(1).broadcast_to([128, TT, 3 * NODES]), ALU.add, [t])
                t = ts(bit[:, :, :], bit[:, :, :], 0.0, None, ALU.is_ge, after=[t])
                t0 = memset(path[0][:, :, :, :], 1.0, lane=DVE)
                bits = bit[:, :, :].rearrange("p t (j n) -> p t j n", j=3)
                t = [t, t0]
                for d in range(DEPTH):
                    w = 2 ** d
                    here = bits[:, :, :, w - 1:2 * w - 1]
                    nxt = path[d + 1][:, :, :, :].rearrange("p t j (n k) -> p t j n k", k=2)
                    for j in range(3):
                        t1 = tt(nxt[:, :, j, :, 1], path[d][:, :, j, :], here[:, :, j, :], ALU.mult, t)
                    for j in range(3):
                        t2 = tt(nxt[:, :, j, :, 0], path[d][:, :, j, :], nxt[:, :, j, :, 1], ALU.subtract, [t1])
                    t = [t2]
                wide = sb(st, "fff_leaf_cols", [LEAVES, LEAVES * 64])[:, :]
                cp(wide.rearrange("p (e i) -> p e i", e=LEAVES), spread(ident[0:LEAVES, 0:LEAVES], 64))
                rows = [sb(st, f"fff_leaf_rows{j}", [LEAVES, T])[:, :] for j in range(3)]
                for j in range(3):
                    t = to_rows(path[DEPTH][:, :, j, :], LEAVES, rows[j], now())
                PE.wait([t_w])
                SC.wait([t_w])
                res = [sb(st, f"fff_{n}", [128, T])[:, :] for n in "qkv"]
                for j in range(3):
                    with ExitStack() as s2:
                        def relu_gated(p):
                            def f(banks, toks, g, h, r):
                                t = act(r.ap[:, 0, :], banks[0].ap[:, 0:HALF], ACT.Relu, bias=b1[:, j, p:p + 1],
                                        after=(toks[0],) + tuple(r.free))
                                banks[0].free = (t,)
                                t = tt(h.ap[:, 0, :], r.ap[:, 0, :], g.ap, ALU.mult, (t,) + tuple(h.free) + tuple(g.ready))
                                g.free, r.free = (t,), (t,)
                                return (t,)
                            return f
                        items = [dict(c=c, ups=[w1[:, j, p * 128:(p + 1) * 128]], downs=[w2[:, j, p, :]], gate=p,
                                      activate=relu_gated(p)) for p in range(LEAVES // 2) for c in range(2)]
                        last = experts(s2, items, lambda p, c: (wide[:, p * 128:(p + 1) * 128],
                                                                halves(rows[j])[c]), x, extra=(b2[:, j, :], rows[j]))
                        for c in range(2):
                            cp(halves(res[j])[c], bank[c].ap[:, 0:HALF], [last[c]])
                    fence()
                q, k_, v_ = res
                p = sb(st, "fff_p", [S, B, S])[:, :, :]
                pt = sb(st, "fff_pt", [S, B, S])[:, :, :]
                vt = sb(st, "fff_v_tokens", [S, B, 128])[:, :, :]
                sst = sb(st, "fff_stat", [S, 3, B])
                for b in range(B):
                    c = slice(b * S, (b + 1) * S)
                    t = mm(psum[0:S, b // 8, (b % 8) * S:(b % 8 + 1) * S], q[:, c], k_[:, c])
                for b in range(B):
                    t1 = tr(psum[0:S, 4 + b // 4, (b % 4) * 128:(b % 4 + 1) * 128], v_[:, b * S:(b + 1) * S])
                sv = psum[0:S, 0:2, 0:HALF].rearrange("p c (b s) -> p c b s", s=S)
                t = red(sst[:, 0, :].rearrange("p (c b) -> p c b", c=2), sv, ALU.max, after=[t])
                for c in range(2):
                    t = tt(p[:, 8 * c:8 * c + 8, :], sv[:, c, :, :], spread(sst[:, 0, 8 * c:8 * c + 8], S), ALU.subtract, [t])
                t = act(p, p, ACT.Exp, scale=float(1.0 / np.sqrt(np.float32(D))), after=[t])
                t = red(sst[:, 1, :], p, ALU.add, after=[t])
                t = recip(sst[:, 2, :], sst[:, 1, :], [t])
                t = tt(p, p, spread(sst[:, 2, :], S), ALU.mult, [t])
                for b in range(B):
                    t2 = tr(psum[0:S, 2 + b // 8, (b % 8) * S:(b % 8 + 1) * S], p[:, b, :], [t])
                e1 = [cp(pt[:, 8 * c:8 * c + 8, :], psum[0:S, 2 + c, 0:HALF].rearrange("p (b s) -> p b s", s=S), [t2])
                      for c in range(2)]
                e1 += [cp(vt[:, 4 * g:4 * g + 4, :], psum[0:S, 4 + g, :].rearrange("p (b d) -> p b d", b=4), [t1], lane=SC)
                       for g in range(4)]
                for b in range(B):
                    t = mm(psum[:, b // 8, (b % 8) * S:(b % 8 + 1) * S], vt[:, b, :], pt[:, b, :], after=e1)
                for c in range(2):
                    tt(halves(x)[c], psum[:, c, 0:HALF], halves(x)[c], ALU.add, [t])
            fence()

        t = load(out, x, a_out, now())
        SY.wait([t])

        block = ctx.enter_context(nc.Block())

        @block.sync
        def _(e):
            SY.run(e)

        @block.tensor
        def _(e):
            PE.run(e)

        @block.vector
        def _(e):
            DVE.run(e)

        @block.scalar
        def _(e):
            SC.run(e)

        @block.gpsimd
        def _(e):
            PL.run(e)


def rope_tables():
    half = D // H // 2
    inv = (1.0 / 10000.0 ** (np.arange(half, dtype=np.float32) / np.float32(half))).astype(np.float32)
    ang = np.arange(L, dtype=np.float32)[:, None] * inv
    c, s = np.cos(ang).T, np.sin(ang).T
    return (np.ascontiguousarray(np.tile(np.concatenate([c, c]), (H, 1)), dtype=np.float32),
            np.ascontiguousarray(np.tile(np.concatenate([-s, s]), (H, 1)), dtype=np.float32))


def swapped(w):
    n, d = w.shape
    return w.reshape(H, 2, n // H // 2, d)[:, ::-1].reshape(n, d)


def layout(v):
    c = np.ascontiguousarray
    a = {}
    a["xT"] = c(v["x"].reshape(T, D).T)
    a["condT"] = c(v["cond_1024"].T)
    ctx = v["ctx_1024"]
    a["ctxT"] = c(ctx.transpose(0, 2, 1))
    a["ctxV"] = c(ctx.reshape(B, KT, KN, D).transpose(0, 2, 1, 3))
    a["src_mask"] = c(v["mask_BxS_bf0"]).reshape(T)
    a["ctx_mask"] = c(v["mask_BxS2_bf0"])
    ws, bs = [], []
    for i in range(NL):
        for n in ("n1", "n2", "n3"):
            ws.append(v[f"L0_xcond_{n}_w"][i].T)
            bs.append(v[f"L0_xcond_{n}_b"][i])
    for n in ("norm1", "norm2", "norm3"):
        ws.append(v[f"L1_xcond_{n}_w"])
        bs.append(v[f"L1_xcond_{n}_b"])
    a["adaln_w"] = c(np.concatenate(ws, axis=1))
    a["adaln_b"] = c(np.stack(bs).reshape(2 * NORMS, 128).T)
    a["rope_cos"], a["rope_sin"] = rope_tables()
    a["head_of_feature"] = (np.arange(128)[:, None] // 8 == np.arange(H)[None, :]).astype(np.float32)
    lw, f2, hd, lb = [], [], [], []
    for i in range(NL):
        q, k, vv = (v["L0_xcond_qkv_w"][i][j * D:(j + 1) * D] for j in range(3))
        cq, ck = v["L0_xcond_cq_w"][i], v["L0_xcond_ck_w"][i]
        rows = [q, swapped(q), k, swapped(k), cq, swapped(cq), ck, swapped(ck), v["L0_xcond_f1_w"][i]]
        lw.append(np.concatenate(rows).T)
        f2.append(v["L0_xcond_f2_w"][i].T.reshape(4, 128, D).transpose(1, 0, 2))
        by_head = lambda m: m.reshape(H, 8, D).transpose(1, 0, 2)
        hd.append(np.stack([by_head(m) for m in (vv, v["L0_xcond_so_w"][i].T, v["L0_xcond_cv_w"][i],
                                                 v["L0_xcond_co_w"][i].T)]))
        lb.append(np.concatenate([v["L0_xcond_f1_b"][i], v["L0_xcond_f2_b"][i]]).reshape(5, 128).T)
    a["l0_w"], a["l0_f2"], a["l0_heads"] = c(np.stack(lw)), c(np.stack(f2)), c(np.stack(hd))
    a["l0_bias"] = c(np.stack(lb, axis=1))
    a["moe_router"] = c(v["L0_ffn_router_w"].T)
    a["moe_bias"] = c(v["L0_ffn_correction_bias"])
    a["moe_lower"] = (np.arange(8)[None, :] < np.arange(8)[:, None]).astype(np.float32)
    a["moe_up"] = c(v["L0_ffn_up_w"].transpose(1, 0, 2).reshape(D, -1))
    a["moe_down"] = c(v["L0_ffn_down_w"].reshape(32, 128, D).transpose(1, 0, 2))
    a["moe_shared_up"] = c(v["L0_ffn_shared_up_w"])
    a["moe_shared_down"] = c(v["L0_ffn_shared_down_w"].reshape(2, 128, D).transpose(1, 0, 2))
    head64 = lambda m: c(m.reshape(H, 64, D).transpose(1, 0, 2))
    for n in (1, 2):
        for k in "qkv":
            a[f"l1_{k}{n}"] = head64(v[f"L1_xcond_attn{n}_w{k}"].T)
        a[f"l1_o{n}"] = head64(v[f"L1_xcond_attn{n}_wo"])
    a["l1_ff1"] = c(v["L1_xcond_ff_w1"])
    a["l1_ff2"] = c(v["L1_xcond_ff_w2"].reshape(4, 128, D).transpose(1, 0, 2))
    a["l1_bias"] = c(np.concatenate([v["L1_xcond_attn1_bo"], v["L1_xcond_attn2_bo"], v["L1_xcond_ff_b1"],
                                     v["L1_xcond_ff_b2"]]).reshape(11, 128).T)
    a["ec_gate"] = c(v["L1_ffn_Wg"])
    a["ec_up"] = c(v["L1_ffn_W1"].transpose(1, 0, 2).reshape(D, -1))
    a["ec_down"] = c(v["L1_ffn_W2"].reshape(16, 128, D).transpose(1, 0, 2))
    a["index_down"] = np.arange(8, 0, -1).astype(np.float32)
    a["l2_affine"] = c(np.stack([v["L2_xcond_ln2_w"], v["L2_xcond_ln2_b"]], axis=1))
    a["l2_ln1_w"], a["l2_ln1_b"] = c(v["L2_xcond_ln1_w"]), c(v["L2_xcond_ln1_b"])
    a["l2_q"] = head64(v["L2_xcond_Wq"])
    a["l2_k"], a["l2_v"] = head64(v["L2_xcond_Wkv"][:H * 64]), head64(v["L2_xcond_Wkv"][H * 64:])
    a["l2_o"] = head64(v["L2_xcond_Wo"].T)
    a["sm_gate"] = c(v["L2_ffn_gate_w"].T)
    for k in ("w1", "w3"):
        a[f"sm_{k}"] = c(v[f"L2_ffn_{k}"].transpose(2, 0, 1).reshape(D, -1))
    a["sm_w2"] = c(v["L2_ffn_w2"].transpose(0, 2, 1).reshape(32, 128, D).transpose(1, 0, 2))
    w = {k: v[f"L3_xcond_{k}"] for k in ("wk", "wq", "wv", "wu", "w1", "w2")}
    a["slot_w"] = c(np.stack([w["wk"].T] + [w[k] for k in ("wq", "wv", "wu", "w1", "w2")], axis=1))
    a["slot_cols"] = c(np.stack([v[f"L3_xcond_{k}"].reshape(D) for k in (
        "q_mu", "q_logsig", "lnq_g", "lnq_b", "lnm_g", "lnm_b", "lnp_g", "lnp_b", "bk", "bv", "bq", "bu", "b1",
        "b2")], axis=1))
    a["slot_lnkv_g"], a["slot_lnkv_b"] = c(v["L3_xcond_lnkv_g"]), c(v["L3_xcond_lnkv_b"])
    three = lambda k: [v[f"L3_ffn_{j}_{k}"] for j in "qkv"]
    a["fff_node_w"] = c(np.concatenate(three("node_w")).T)
    a["fff_node_b"] = c(np.concatenate(three("node_b")))
    a["fff_w1"] = c(np.stack([m.transpose(1, 0, 2).reshape(D, -1) for m in three("w1")], axis=1))
    a["fff_w2"] = c(np.stack([m.reshape(8, 128, D).transpose(1, 0, 2) for m in three("w2")], axis=1))
    a["fff_b1"] = c(np.stack([m.reshape(8, 128).T for m in three("b1")], axis=1))
    a["fff_b2"] = c(np.stack(three("b2"), axis=1))
    return a


def kernel(**inputs):
    import concourse.bacc as bacc
    from concourse.bass_utils import run_bass_kernel_spmd

    arrays = layout({k: np.asarray(a) for k, a in inputs.items()})
    nc = bacc.Bacc("TRN2", target_bir_lowering=False, num_devices=1)
    dr = {n: nc.dram_tensor(f"in_{n}", a.shape, mybir.dt.from_np(a.dtype), kind="ExternalInput").ap()
          for n, a in arrays.items()}
    out = nc.dram_tensor("out_0", (D, T), F32, kind="ExternalOutput").ap()
    program(nc, dr, out)
    r = run_bass_kernel_spmd(nc, [{f"in_{n}": a for n, a in arrays.items()}], core_ids=[0])
    return np.ascontiguousarray(r.results[0]["out_0"].T).reshape(B, S, D)
```

```python
from contextlib import ExitStack

import numpy as np
import concourse.bass as bass
from concourse import mybir

F32, BF16, U8 = mybir.dt.float32, mybir.dt.bfloat16, mybir.dt.uint8
ALU, ACT, AX = mybir.AluOpType, mybir.ActivationFunctionType, mybir.AxisListType

B, S, D = 16, 56, 128
T = B * S
TT = T // 128
HALF = T // 2
BH = B // 2
L = 1500
KT, KN = 12, 125
H = 16
R = H * S // 128
NL = 6
NORMS = 3 * NL + 3
BANK = 512
LOW = -1e30
EPS = 1e-5
PAIRS, F2 = H // 2, 2 * D // H
K_PARTS, Q_PARTS = (0, 0, 1, 1, 0, 2), (0, 1, 0, 1, 2, 0)
ROWS = F2 * len(K_PARTS)
QC = 2 * S
OTHER_HALF = [i ^ PAIRS for i in range(32)]
KEY_STEPS = (1, 5, 8)
MAX_STEPS = {3: (0,), 4: (1,), 5: (2,), 6: (3,), 7: (4,), 8: (5,), 9: (6, 7)}
FIRST, LAST = 0, 7


class Lane:

    def __init__(self, sem):
        self.sem, self.count, self.queue, self.seen = sem, 0, [], {}

    def wait(self, after):
        for source, value in after:
            if self.seen.get(source.sem.name, 0) < value:
                self.seen[source.sem.name] = value
                self.queue.append(lambda e, s=source.sem, v=value: e.wait_ge(s, v))

    def put(self, make, after=(), signal=True):
        self.wait(after)
        if signal:
            self.count += 1
            self.queue.append(lambda e: make(e).then_inc(self.sem, 1))
        else:
            self.queue.append(make)
        return (self, self.count)

    def run(self, e):
        for step in self.queue:
            step(e)


class Arrival:

    def __init__(self, sem):
        self.sem, self.count = sem, 0


class Slot:

    def __init__(self, ap, arrival=None):
        self.ap, self.ready, self.free, self.arrival = ap, (), (), arrival


class Ring:
    def __init__(self, slots):
        self.slots, self.n = slots, -1

    def next(self):
        self.n += 1
        return self.slots[self.n % len(self.slots)]


def halves(a):
    return [a[:, 0:HALF], a[:, HALF:T]]


def spread(cols, n):
    p, m = cols.shape
    return cols.unsqueeze(2).broadcast_to([p, m, n])


def program(nc, dr, out):
    ctx = ExitStack()
    with ctx:
        names = {}

        def sb(stack, name, shape, dt=F32):
            names[name] = names.get(name, 0) + 1
            if names[name] > 1:
                name = f"{name}_{names[name]}"
            return stack.enter_context(nc.sbuf_tensor(name, shape, dt))

        def sem(name):
            return ctx.enter_context(nc.semaphore(name))

        PE, DVE, SC, PL = (Lane(sem(n)) for n in ("pe_done", "dve_done", "act_done", "pool_done"))
        SY = Lane(sem("sync_unused"))
        arrival_of = {}

        def arrival(name):
            if name not in arrival_of:
                arrival_of[name] = Arrival(sem(name))
            return arrival_of[name]

        def mm(o, lhsT, rhs, start=True, stop=True, after=(), signal=False):
            return PE.put(lambda e: e.matmul(o, lhsT, rhs, start=start, stop=stop), after, signal=signal or stop)

        def tr(o, i, after=()):
            p = i.shape[0]
            return PE.put(lambda e: e.transpose(o, i, ident[0:p, 0:p]), after)

        def tt(o, a, b, op, after=(), lane=DVE):
            return lane.put(lambda e: e.tensor_tensor(o, a, b, op), after)

        def ts(o, a, s1, s2, op0, op1=None, after=(), lane=DVE):
            if op1 is None:
                return lane.put(lambda e: e.tensor_scalar(o, a, s1, None, op0), after)
            return lane.put(lambda e: e.tensor_scalar(o, a, s1, s2, op0, op1), after)

        def stt(o, a, s, b, op0, op1, after=()):
            return DVE.put(lambda e: e.scalar_tensor_tensor(out=o, in0=a, scalar=s, in1=b, op0=op0, op1=op1), after)

        def cp(o, a, after=(), lane=DVE):
            if lane is SC:
                return act(o, a, ACT.Copy, after=after)
            return lane.put(lambda e: e.tensor_copy(o, a), after)

        def shuffle(o, a, lanes, after=()):
            return DVE.put(lambda e: e.stream_shuffle(o, a, lanes), after)

        def recip(o, a, after=()):
            return DVE.put(lambda e: e.reciprocal(o, a), after)

        def max8(o, a, after=()):
            return DVE.put(lambda e: e.max(o, a), after)

        def replace8(o, found, a, after=()):
            return DVE.put(lambda e: e.match_replace(o, found, a, LOW), after)

        def bn_stats(o, a, after=()):
            return DVE.put(lambda e: e.bn_stats(o, a), after)

        def bn_aggr(o, a, after=()):
            return DVE.put(lambda e: e.bn_aggr(o, a), after)

        def memset(o, value, after=(), lane=None):
            return (lane or PL).put(lambda e: e.memset(o, value), after)

        def add_max(o, a, b, largest, after=()):
            return DVE.put(lambda e: e.tensor_tensor_reduce(o, a, b, 1.0, 3 * LOW, ALU.add, ALU.max, largest), after)

        def red(o, a, op, negate=False, after=(), axis=AX.X):
            return DVE.put(lambda e: e.tensor_reduce(o, a, axis, op, negate=negate), after)

        def act(o, a, func, bias=None, scale=None, accum=None, after=()):
            kw = {}
            if bias is not None:
                kw["bias"] = bias
            if scale is not None:
                kw["scale"] = scale
            if accum is not None:
                kw["accum_out"] = accum
            return SC.put(lambda e: e.activation(o, a, func, **kw), after)

        def load(o, i, arr, after=()):
            SY.wait(after)
            arr.count += 16
            SY.queue.append(lambda e: e.dma_start(o, i).then_inc(arr.sem, 16))
            return (arr, arr.count)

        def again(arr):
            return now() + ([(arr, arr.count)] if arr.count else [])

        def now():
            return [(lane, lane.count) for lane in (PE, DVE, SC, PL) if lane.count]

        def fence():
            done = now() + [(a, a.count) for a in arrival_of.values() if a.count]
            for lane in (PE, DVE, SC, PL, SY):
                lane.wait(done)

        x = sb(ctx, "x_state", [128, T])[:, :]
        z = sb(ctx, "block_state", [128, T])[:, :]
        xn = sb(ctx, "x_normed", [128, T])[:, :]
        dev = sb(ctx, "ln_deviation", [128, T])[:, :]
        sq = sb(ctx, "ln_square", [128, T])[:, :]
        stats = sb(ctx, "ln_token_stats", [128, 2 * TT])[:, :]
        ident = sb(ctx, "ident", [128, 128])
        ident_b = sb(ctx, "ident_bf16", [128, 128], BF16)
        mean_w = sb(ctx, "mean_weights", [128, 128])[:, :]
        gb = sb(ctx, "adaln_scale_shift", [128, NORMS, 2, B])
        cond = sb(ctx, "cond", [128, B])[:, :]
        c_mean = sb(ctx, "context_mean", [KN, B, KT])
        c_rstd = sb(ctx, "context_rstd", [KN, B, KT])
        psum = ctx.enter_context(nc.psum_tensor("psum", [128, 8, BANK], F32))
        bank = [Slot(psum[:, i, :]) for i in range(8)]
        a_in, a_w, a_w2 = arrival("in_arrived"), arrival("weights_arrived"), arrival("weights2_arrived")
        a_out = arrival("out_stored")

        t0 = memset(ident[:, :], 0.0)
        t_id = PL.put(lambda e: e.affine_select(out=ident[:, :], in_=ident[:, :], compare_op=ALU.not_equal, fill=1.0,
                                                base=0, pattern=[[-1, 128]], channel_multiplier=1), [t0])
        eps_col = sb(ctx, "eps", [128, 1])[:, :]
        memset(eps_col, EPS)
        t_id = cp(ident_b[:, :], ident[:, :], [t_id], lane=PL)
        t_mw = memset(mean_w, 1.0 / D)
        load(x, dr["xT"], a_in)
        t_x = load(cond, dr["condT"], a_in)
        for lane in (PE, DVE, SC, PL):
            lane.wait([t_x, t_id, t_mw])

        def bank_free(i, tokens):
            bank[i].free = tuple(tokens)

        def layernorm(src, dst, per_batch=None, per_feature=None):
            after = now()
            s, d, q, y = (halves(a) for a in (src, dev, sq, dst))
            mean = [psum[:, c, 0:HALF] for c in range(2)]
            t = [mm(mean[c], mean_w, s[c], after=after) for c in range(2)]
            t = [tt(d[c], s[c], mean[c], ALU.subtract, after + [t[c]]) for c in range(2)]
            t = [act(q[c], d[c], ACT.Square, after=after + [t[c]]) for c in range(2)]
            for i in range(TT):
                tv = mm(psum[:, 4, i:i + 1], sq[:, i * 128:(i + 1) * 128], mean_w[:, 0:1], after=t)
            tv = act(stats[:, 0:TT], psum[:, 4, 0:TT], ACT.Sqrt, bias=eps_col, after=[tv])
            tv = recip(stats[:, TT:2 * TT], stats[:, 0:TT], [tv])
            for i in range(TT):
                g, k = i // 4, i % 4
                tr_ = mm(psum[:, 2 + g, k * 128:(k + 1) * 128], stats[:, TT + i:TT + i + 1].broadcast_to([128, 128]),
                         ident[:, :], after=[tv])
            t = []
            for g, (lo, hi) in enumerate(((0, BANK), (BANK, T))):
                t.append(tt(dst[:, lo:hi], dev[:, lo:hi], psum[:, 2 + g, 0:hi - lo], ALU.mult, [tr_] + after))
            t = [t[1], t[1]]
            if per_batch is not None:
                for c in range(2):
                    v = y[c].rearrange("p (b s) -> p b s", s=S)
                    for k, op in ((0, ALU.mult), (1, ALU.add)):
                        t[c] = tt(v, v, spread(per_batch[k][:, c * BH:(c + 1) * BH], S), op, [t[c]])
            if per_feature is not None:
                t = [ts(y[c], y[c], per_feature[0], per_feature[1], ALU.mult, ALU.add, [t[c]]) for c in range(2)]
            return t

        def linear(pieces, banks, after):
            toks = []
            for c in range(2):
                for k, (w, src) in enumerate(pieces):
                    t = mm(psum[:, banks[c], 0:HALF], w, halves(src)[c], k == 0, k == len(pieces) - 1, after)
                toks.append(t)
            return toks

        def to_tokens(src, w, ncols, bnk, after):
            for i in range(TT):
                t = mm(psum[:, bnk, i * ncols:(i + 1) * ncols], src[:, i * 128:(i + 1) * 128], w, True, True, after)
            return t

        def to_rows(src, m, dst, after):
            toks = []
            for g, lo in enumerate(range(0, TT, 4)):
                n = min(4, TT - lo)
                for i in range(n):
                    t = tr(psum[0:m, g, i * 128:(i + 1) * 128], src[:, lo + i, :], after)
                toks.append(cp(dst[:, lo * 128:(lo + n) * 128], psum[0:m, g, 0:n * 128], [t] + after))
            return toks

        def fold_heads(first, second, table, after):
            toks = []
            for g in range(H // 4):
                for k in range(4):
                    h = 4 * g + k
                    t = mm(psum[:, g, k * 128:(k + 1) * 128], first[:, h, :], second[:, h, :], after=after)
                toks.append(cp(table[:, 4 * g:4 * g + 4, :], psum[:, g, :].rearrange("p (h d) -> p h d", h=4),
                               [t] + after, lane=(DVE, SC)[g % 2]))
            return toks

        def scale_queries(fold, src, ring, make_slot):
            def chunk(pair, slot, g):
                bk = ring.next()
                for k in range(4):
                    t = mm(bk.ap[:, k * 2 * S:(k + 1) * 2 * S], fold[:, 4 * g + k, :],
                           src[:, pair * 2 * S:(pair + 1) * 2 * S], after=tuple(bk.free) + tuple(make_slot))
                o = slot.ap[:, :, 4 * g:4 * g + 4, :].rearrange("p b h q -> p h b q")
                i = bk.ap[:, 0:8 * S].rearrange("p (h b q) -> p h b q", h=4, b=2)
                t = act(o, i, ACT.Copy, scale=float(slot.scale), after=(t,) + tuple(slot.free))
                bk.free = (t,)
                return t
            return chunk

        def project_pair(pair, slot, table, dst, bk, bias_col):
            for h in range(H):
                t = mm(bk.ap[:, 0:2 * S], table[:, h, :], slot.ap[:, h, :], h == 0, h == H - 1,
                       tuple(bk.free) + tuple(slot.ready))
            slot.free = (t,)
            d = dst[:, pair * 2 * S:(pair + 1) * 2 * S]
            if bias_col is None:
                t = tt(d, bk.ap[:, 0:2 * S], d, ALU.add, [t])
            else:
                t = stt(d, bk.ap[:, 0:2 * S], bias_col, d, ALU.add, ALU.add, [t])
            bk.free = (t,)

        def self_attention(st, query, keys, values, table, dst, key_mask=None, bias_col=None,
                           beside=lambda i: None):
            p_r = Ring([Slot(sb(st, f"self_p{i}", [128, R, S])[:, :, :]) for i in range(3)])
            pt_r = Ring([Slot(sb(st, f"self_pt{i}", [S, H * S])[:, :]) for i in range(2)])
            v_r = Ring([Slot(sb(st, f"self_v{i}", [S, 128])[:, :]) for i in range(4)])
            st_r = Ring([Slot(sb(st, f"self_stat{i}", [128, 3, R])) for i in range(3)])
            u_r = Ring([Slot(sb(st, f"self_u{i}", [128, H, 2 * S])[:, :, :]) for i in range(2)])
            start = tuple(now())
            for bk in bank:
                bk.free = start
            s_bank, v_bank, o_bank = Ring(bank[0:2]), bank[6], bank[7]
            kept = {}
            ahead = query(0)

            def scores(b):
                nonlocal ahead
                q, q_ready, q_slot = ahead
                bk = s_bank.next()
                for r in range(R):
                    t = mm(bk.ap[:, r * S:(r + 1) * S], q[:, r * 128:(r + 1) * 128], keys[:, b * S:(b + 1) * S],
                           after=tuple(bk.free) + tuple(q_ready))
                q_slot.free = (t,)
                if b + 1 < B:
                    ahead = query(b + 1)
                p, stat = p_r.next(), st_r.next()
                s_in = bk.ap[:, 0:R * S].rearrange("p (r s) -> p r s", r=R)
                t_s = (t,)
                if key_mask is not None:
                    m = key_mask[:, b * S:(b + 1) * S].unsqueeze(1).broadcast_to([128, R, S])
                    t = tt(p.ap, s_in, m, ALU.add, t_s + tuple(p.free))
                    bk.free, s_in = (t,), p.ap
                t = red(stat.ap[:, 0, :], s_in, ALU.max, after=(t,) + tuple(stat.free))
                t = tt(p.ap, s_in, spread(stat.ap[:, 0, :], S), ALU.subtract, (t,) + tuple(p.free))
                if key_mask is None:
                    bk.free = (t,)
                p.ready = (act(p.ap, p.ap, ACT.Exp, after=(t,)),)
                kept[b] = (p, stat)

            def value_tokens(b):
                v = v_r.next()
                t = tr(v_bank.ap[0:S, 0:128], values[:, b * S:(b + 1) * S], v_bank.free)
                t = cp(v.ap, v_bank.ap[0:S, 0:128], (t,) + tuple(v.free), lane=SC)
                v_bank.free, v.ready = (t,), (t,)
                kept[b] += (v,)

            def normalise(b):
                p, stat = kept[b]
                t = red(stat.ap[:, 1, :], p.ap, ALU.add, after=p.ready)
                t = recip(stat.ap[:, 2, :], stat.ap[:, 1, :], (t,))
                t = tt(p.ap, p.ap, spread(stat.ap[:, 2, :], S), ALU.mult, (t,))
                p.ready, stat.free = (t,), (t,)

            def turn(b):
                p, stat, v = kept[b]
                pt = pt_r.next()
                ev = []
                for g, lo in enumerate(range(0, R, 4)):
                    n = min(4, R - lo)
                    bk = bank[2 + g]
                    for i in range(n):
                        t = tr(bk.ap[0:S, i * 128:(i + 1) * 128], p.ap[:, lo + i, :], tuple(bk.free) + tuple(p.ready))
                    e = cp(pt.ap[:, lo * 128:(lo + n) * 128], bk.ap[0:S, 0:n * 128], (t,) + tuple(pt.free), lane=SC)
                    bk.free = (e,)
                    ev.append(e)
                p.free, pt.ready = (t,), tuple(ev)
                kept[b] = (v, pt)

            def weigh(b):
                v, pt = kept.pop(b)
                u = u_r.next() if b % 2 == 0 else u_r.slots[u_r.n % 2]
                outs = []
                for c in range(2):
                    bk = bank[4 + c]
                    t = mm(bk.ap[:, 0:HALF], v.ap, pt.ap[:, c * HALF:(c + 1) * HALF],
                           after=tuple(bk.free) + tuple(pt.ready) + tuple(v.ready))
                    o = u.ap[:, 8 * c:8 * c + 8, (b % 2) * S:(b % 2 + 1) * S]
                    e = cp(o, bk.ap[:, 0:HALF].rearrange("p (h q) -> p h q", q=S), (t,) + tuple(u.free),
                           lane=(SC, DVE)[c])
                    bk.free = (e,)
                    outs.append(e)
                v.free, pt.free = (t,), (t,)
                u.ready = tuple(outs) if b % 2 == 0 else u.ready + tuple(outs)

            for i in range(B + 4):
                if i < B:
                    scores(i)
                if 0 <= i - 2 < B:
                    value_tokens(i - 2)
                    turn(i - 2)
                if 0 <= i - 4 < B and (i - 4) % 2 == 1:
                    project_pair((i - 4) // 2, u_r.slots[((i - 4) // 2) % 2], table, dst, o_bank, bias_col)
                if 0 <= i - 3 < B:
                    weigh(i - 3)
                beside(i)
                if 0 <= i - 1 < B:
                    normalise(i - 1)

        def cross_attention(bufs, widths, hooks, query, keys, values, table, dst, mask=None, bias_col=None,
                            own_values=None):
            n_s = len(widths)
            width = sum(widths)
            step = widths[0]
            s_banks = psum[:, 0:n_s, 0:step]
            s_free = tuple(now())
            t_ring, u_bank, m_bank = bufs["t_ring"], bank[6], bank[7]
            tiles = KT + (1 if own_values is not None else 0)
            items = [(b, r) for b in range(B) for r in range(R)]
            st = {}
            u_r = bufs["u_ring"]

            def score(i):
                nonlocal s_free
                b, r = items[i]
                q, q_ready, q_slot = query(b)
                k, k_ready, k_slot = keys(b)
                for c in range(n_s):
                    t = mm(s_banks[:, c, :], q[:, r * 128:(r + 1) * 128], k[:, c * step:(c + 1) * step],
                           after=tuple(s_free) + tuple(q_ready) + tuple(k_ready))
                if r == R - 1:
                    q_slot.free = (t,)
                    k_slot.free = (t,)
                return t

            def softmax(i, t):
                nonlocal s_free
                b, r = items[i]
                p, stat = bufs["p_ring"].next(), bufs["stat_ring"].next()
                pv = p.ap[:, 0:width].rearrange("p (c n) -> p c n", c=n_s)
                if mask is not None:
                    m, m_ready, m_slot = mask(b)
                    t = add_max(pv, s_banks, m.rearrange("p (c n) -> p c n", c=n_s), stat.ap[:, 0:1],
                                (t,) + tuple(p.free) + tuple(stat.free) + tuple(m_ready))
                    s_free = (t,)
                    m_slot.free = (t,)
                    t = ts(stat.ap[:, 1:2], stat.ap[:, 0:1], -1.0, None, ALU.mult, after=(t,))
                    t = act(pv, pv, ACT.Exp, bias=stat.ap[:, 1:2], accum=stat.ap[:, 2:3], after=(t,))
                else:
                    t = red(stat.ap[:, 1:2], s_banks, ALU.max, negate=True, after=(t,) + tuple(stat.free), axis=AX.XY)
                    t = act(pv, s_banks, ACT.Exp, bias=stat.ap[:, 1:2], accum=stat.ap[:, 2:3],
                            after=(t,) + tuple(p.free))
                    s_free = (t,)
                st[i] = dict(p=p, stat=stat, exp=t)

            def transpose_in(i):
                s = st[i]
                pt = bufs["pt_ring"].next()
                s["pt"], s["pt_ready"] = pt, []
                s["todo"] = []
                for g, lo in enumerate(range(0, tiles, 4)):
                    n = min(4, tiles - lo)
                    bk = t_ring.next()
                    rows = KN if lo < KT else S
                    for k in range(n):
                        c0 = (lo + k) * KN
                        t = tr(bk.ap[0:rows, k * 128:(k + 1) * 128], s["p"].ap[:, c0:c0 + rows],
                               tuple(bk.free) + (s["exp"],))
                    args = (pt.ap[0:rows, lo:lo + n, :],
                            bk.ap[0:rows, 0:n * 128].rearrange("p (k r) -> p k r", k=n), (t,) + tuple(pt.free))
                    if g < 2:
                        e = cp(*args, lane=SC)
                        bk.free = (e,)
                        s["pt_ready"].append(e)
                    else:
                        e = cp(*args)
                        bk.free = (e,)
                        s["pt_ready"].append(e)
                s["p"].free = (t,)

            def weigh(i):
                b, r = items[i]
                s = st[i]
                v, v_ready, v_slot = values(b)
                for k in range(tiles):
                    after = (s["pt_ready"][k // 4],) + tuple(v_ready) + tuple(u_bank.free)
                    if k < KT:
                        t = mm(u_bank.ap[:, 0:128], s["pt"].ap[:, k, :], v[:, k, :], k == 0, k == tiles - 1, after)
                    else:
                        t = mm(u_bank.ap[:, 0:128], s["pt"].ap[0:S, k, :], own_values[:, b, :], False, True, after)
                s["pt"].free = (t,)
                if r == R - 1:
                    v_slot.free = (t,)
                s["u"] = t

            def inverse(i):
                s = st[i]
                s["inv"] = recip(s["stat"].ap[:, 3:4], s["stat"].ap[:, 2:3], (s["exp"],))

            def normalise(i):
                s = st[i]
                w = bufs["w_ring"].next()
                t = act(w.ap, u_bank.ap[:, 0:128], ACT.Copy, scale=s["stat"].ap[:, 3:4],
                        after=(s["u"], s["inv"]) + tuple(w.free))
                u_bank.free = (t,)
                s["stat"].free = (t,)
                s["w"], s["w_ready"] = w, t

            def turn(i):
                s = st[i]
                s["turned"] = tr(m_bank.ap[:, 0:128], s["w"].ap, (s["w_ready"],) + tuple(m_bank.free))
                s["w"].free = (s["turned"],)

            def gather(i):
                b, r = items[i]
                s = st.pop(i)
                if b % 2 == 0 and r == 0:
                    u_r.next()
                u = u_r.slots[u_r.n % len(u_r.slots)]
                lo, hi = r * 128, (r + 1) * 128
                first = True
                while lo < hi:
                    h, q = divmod(lo, S)
                    n = min(S - q, hi - lo)
                    if q == 0 and hi - lo >= 2 * S:
                        nh = (hi - lo) // S
                        o = u.ap[:, h:h + nh, (b % 2) * S:(b % 2 + 1) * S]
                        i_ = m_bank.ap[:, lo - r * 128:lo - r * 128 + nh * S].rearrange("p (h q) -> p h q", q=S)
                        n = nh * S
                    else:
                        o = u.ap[:, h, (b % 2) * S + q:(b % 2) * S + q + n]
                        i_ = m_bank.ap[:, lo - r * 128:lo - r * 128 + n]
                    t = cp(o, i_, (s["turned"],) + (tuple(u.free) if first else ()))
                    first = False
                    lo += n
                m_bank.free = (t,)
                u.ready = (t,)
                if b % 2 == 1 and r == R - 1:
                    project_pair(b // 2, u, table, dst, m_bank, bias_col)

            n = len(items)
            for i in range(n + 2):
                if i < n:
                    t = score(i)
                    hooks(*items[i])
                if 0 <= i - 2:
                    normalise(i - 2)
                if 1 <= i <= n:
                    inverse(i - 1)
                    if i < n and mask is not None:
                        pass
                if i < n:
                    softmax_dve_first = softmax
                if 1 <= i <= n:
                    transpose_in(i - 1)
                if i < n:
                    softmax(i, t)
                if 0 <= i - 2:
                    turn(i - 2)
                    gather(i - 2)
                if 1 <= i <= n:
                    weigh(i - 1)

        def split_keys(st, q_rot, cos, sin, parity, mask_rows):
            k_stack = [Slot(sb(st, f"key_stack{i}", [ROWS + 4, PAIRS, L], BF16), arrival(f"key_stack{i}_arrived"))
                       for i in range(2)]
            q_stack = [Slot(sb(st, f"query_stack{i}", [ROWS + 4, PAIRS * QC], BF16),
                            arrival(f"query_stack{i}_arrived")) for i in range(2)]
            k_part = Slot(sb(st, "key_parts", [128, 3, L], BF16))
            q_part = Slot(sb(st, "query_parts", [128, 3, QC], BF16))
            q_tmp = Slot(sb(st, "query_block", [128, 2, QC]))
            tm = Slot(sb(st, "key_temp", [128, 2, 500]))
            ctx_t, fetch_t = streamed(st, "ctx_t", [128, L], lambda b: dr["ctxT"][b])
            start = tuple(now())
            ones_rows = sb(st, "ones_rows", [3, L], BF16)[:, :]
            t_ones = memset(ones_rows, 1.0, start, DVE)
            for s in k_stack:
                s.ready = (load(s.ap[ROWS + 1:ROWS + 4, :, :], ones_rows.unsqueeze(1).broadcast_to([3, PAIRS, L]),
                                s.arrival, (t_ones,)),)
            for s in q_stack:
                s.free = (memset(s.ap[ROWS:ROWS + 1, :], 1.0, start, DVE),)

            def split(out3, full, rest, after, first_free):
                hi = cp(out3[0], full, tuple(after) + tuple(first_free), lane=SC)
                yield
                t = tt(rest, full, out3[0], ALU.subtract, (hi,))
                mid = cp(out3[1], rest, (t,), lane=SC)
                yield
                lo = tt(out3[2], rest, out3[1], ALU.subtract, (mid,))
                yield (hi, mid, lo)

            def key_chunk(b, c, w_key, work, rest_for=0):
                src = ctx_t[b % 2]
                cols = slice(c * 500, (c + 1) * 500)
                bk = work.next()
                t = mm(bk.ap[:, 0:500], w_key, src.ap[:, cols], after=tuple(bk.free) + tuple(src.ready))
                src.free = (t,)
                full, rest = tm.ap[:, 0, :], tm.ap[:, 1, :]
                t2 = shuffle(rest, bk.ap[:, 0:500], OTHER_HALF, (t,) + tuple(tm.free))
                t1 = tt(full, bk.ap[:, 0:500], cos[:, cols], ALU.mult, (t,) + tuple(tm.free))
                bk.free = (t1,)
                t2 = tt(rest, rest, sin[:, cols], ALU.mult, (t2,), lane=PL)
                t = tt(full, full, rest, ALU.add, (t1, t2), lane=PL)
                for _ in range(1 + rest_for):
                    yield
                first_free = k_part.free
                for done in split([k_part.ap[:, i, cols] for i in range(3)], full, rest, (t,), first_free):
                    if done:
                        tm.free = (done[2],)
                        k_part.ready = done if c == 0 else tuple(k_part.ready) + done
                    yield

            def stack_keys(b):
                s = k_stack[b % 2]
                after = tuple(s.free) + tuple(s.ready) + tuple(k_part.ready)
                for i, part in enumerate(K_PARTS):
                    t = load(s.ap[F2 * i:F2 * i + F2, :, :], k_part.ap[:, part, :], s.arrival, after)
                t = load(s.ap[ROWS:ROWS + 1, :, :], mask_rows[b:b + 1, :].unsqueeze(1).broadcast_to([1, PAIRS, L]),
                         s.arrival, after)
                s.ready, k_part.free = (t,), (t,)

            def split_queries(b, after):
                q = q_rot[:, b * S:(b + 1) * S].unsqueeze(1).broadcast_to([128, 2, S])
                t = tt(q_tmp.ap[:, 0, :].rearrange("p (h q) -> p h q", h=2), q, spread(parity, S), ALU.mult, tuple(after) + tuple(q_tmp.free),
                       lane=PL)
                yield
                for done in split([q_part.ap[:, i, :] for i in range(3)], q_tmp.ap[:, 0, :], q_tmp.ap[:, 1, :], (t,),
                                  q_part.free):
                    if done:
                        q_part.ready, q_tmp.free = done, (done[2],)
                    yield

            def stack_queries(b):
                s = q_stack[b % 2]
                after = tuple(s.free) + tuple(s.ready) + tuple(q_part.ready)
                for i, part in enumerate(Q_PARTS):
                    t = load(s.ap[F2 * i:F2 * i + F2, :].rearrange("j (p c) -> j p c", p=PAIRS), q_part.ap[:, part, :],
                             s.arrival, after)
                s.ready, q_part.free = (t,), (t,)

            return k_stack, q_stack, fetch_t, key_chunk, stack_keys, split_queries, stack_queries

        def split_cross_attention(st, shared, w_key, table, dst):
            k_stack, q_stack, fetch_t, key_chunk, stack_keys, split_queries, stack_queries = shared
            p_ring = Ring([Slot(sb(st, f"weights{i}", [KN, 2, HALF])) for i in range(3)])
            largest = sb(st, "row_max", [QC, PAIRS, 3])
            neg = sb(st, "neg_max", [QC, 2, PAIRS])
            m_part = sb(st, "neg_max_parts", [QC, PAIRS, 4], BF16)
            inv = sb(st, "inverse_sum", [QC, PAIRS])
            w_slot = Slot(sb(st, "normed_out", [QC, PAIRS, 128]))
            u_r = Ring([Slot(sb(st, f"split_u{i}", [128, H, QC])[:, :, :]) for i in range(1)])
            ctx_v = [Slot(sb(st, f"ctx_v_ones{i}", [KN, KT, 129]), arrival(f"ctx_v{i}_arrived")) for i in range(2)]
            start = tuple(now())
            for bk in bank:
                bk.free = start
            s_free = start
            acc_free = start
            work = Ring(bank[5:8])
            for s in ctx_v:
                s.free = (memset(s.ap[:, :, 128:129], 1.0, start, DVE),)
            t_one = memset(m_part[:, :, 0:1], 1.0, start, DVE)

            def acc(p):
                return psum[0:QC, 2 + p // 3, (p % 3) * 129:(p % 3) * 129 + 129]

            def fetch_v(b):
                s = ctx_v[b % 2]
                s.ready = (load(s.ap[:, :, 0:128], dr["ctxV"][b], s.arrival, tuple(s.free) + tuple(s.ready)),)

            def row_max(b, p):
                q, k = q_stack[b % 2], k_stack[b % 2]
                for c in range(3):
                    bk = work.next()
                    t = mm(bk.ap[0:QC, 0:500], q.ap[0:ROWS + 1, p * QC:(p + 1) * QC],
                           k.ap[0:ROWS + 1, p, c * 500:(c + 1) * 500],
                           after=tuple(bk.free) + tuple(q.ready) + tuple(k.ready))
                    t = red(largest[:, p, c:c + 1], bk.ap[0:QC, 0:500], ALU.max, after=(t,))
                    bk.free = (t,)
                return t

            def max_parts(t):
                nonlocal t_parts
                t = red(neg[:, 0, :], largest[:, :, :], ALU.max, negate=True, after=(t,))
                t = cp(m_part[:, :, 1], neg[:, 0, :], (t, t_one))
                t = tt(neg[:, 1, :], neg[:, 0, :], m_part[:, :, 1], ALU.subtract, (t,))
                t = cp(m_part[:, :, 2], neg[:, 1, :], (t,))
                t_parts = tt(m_part[:, :, 3], neg[:, 1, :], m_part[:, :, 2], ALU.subtract, (t,))

            t_parts = None

            def max_rows(b):
                q = q_stack[b % 2]
                bk = work.next()
                rows = bk.ap[0:4, 0:PAIRS * QC // 2].bitcast(BF16)
                for p in range(PAIRS):
                    t2 = PE.put(transposed(rows[:, p * QC:(p + 1) * QC], m_part[:, p, :], ident_b[0:QC, 0:QC]),
                                (t_parts,) + tuple(bk.free))
                t = cp(q.ap[ROWS:ROWS + 4, :], rows, (t2,))
                bk.free = (t,)
                q.ready = tuple(q.ready) + (t,)

            def transposed(o, i, idn):
                return lambda e: e.transpose(o, i, idn)

            def exponentials(b, k):
                nonlocal s_free
                q, ks, s = q_stack[b % 2], k_stack[b % 2], p_ring.next()
                for p in range(PAIRS):
                    t = mm(psum[0:KN, p // 4, (p % 4) * QC:(p % 4 + 1) * QC], ks.ap[:, p, k * KN:(k + 1) * KN],
                           q.ap[:, p * QC:(p + 1) * QC], after=tuple(s_free) + tuple(q.ready) + tuple(ks.ready))
                t = act(s.ap[:, :, :], psum[0:KN, 0:2, 0:HALF], ACT.Exp, after=(t,) + tuple(s.free))
                s_free = (t,)
                s.ready = (t,)
                if k == KT - 1:
                    q.free, ks.free = (t,), (t,)
                return s

            def weigh(b, k, s):
                nonlocal acc_done
                v = ctx_v[b % 2]
                for p in range(PAIRS):
                    w = s.ap[:, p // 4, (p % 4) * QC:(p % 4 + 1) * QC]
                    acc_done = PE.put(accumulating(acc(p), w, v.ap[:, k, :], k == 0 and p % 3 == 0, k == KT - 1),
                                      tuple(s.ready) + tuple(v.ready) + (tuple(acc_free) if k == 0 else ()))
                s.free = (acc_done,)
                if k == KT - 1:
                    v.free = (acc_done,)

            def accumulating(o, w, v, first, last):
                return lambda e: e.matmul(o, w, v, start=first, stop=last, skip_group_check=True)

            acc_done = None

            def normalise(b):
                nonlocal acc_free
                t1 = recip(inv[:, 0:6].rearrange("p (g i) -> p g i", g=2),
                           psum[0:QC, 2:4, 0:387].rearrange("p g (i c) -> p g i c", c=129)[:, :, :, 128], (acc_done,))
                t1 = recip(inv[:, 6:8], psum[0:QC, 4, 0:258].rearrange("p (i c) -> p i c", c=129)[:, :, 128], (acc_done,))
                toks = []
                for p in range(PAIRS):
                    o, i = w_slot.ap[:, p, :], acc(p)[:, 0:128]
                    after = (t1,) + tuple(w_slot.free)
                    if p < 3:
                        toks.append(act(o, i, ACT.Copy, scale=inv[:, p:p + 1], after=after))
                    else:
                        toks.append(ts(o, i, inv[:, p:p + 1], None, ALU.mult, after=after))
                acc_free = w_slot.ready = tuple(toks)

            def turn(b):
                if b % 2 == 0:
                    u_r.next()
                u = u_r.slots[u_r.n % len(u_r.slots)]
                outs = []
                for g in range(2):
                    bk = work.next()
                    for i in range(4):
                        t = tr(bk.ap[:, i * QC:(i + 1) * QC], w_slot.ap[:, 4 * g + i, :],
                               tuple(w_slot.ready) + tuple(bk.free))
                    e = cp(u.ap[:, 8 * g:8 * g + 8, (b % 2) * S:(b % 2 + 1) * S],
                           bk.ap[:, 0:4 * QC].rearrange("p (h q) -> p h q", q=S), (t,) + tuple(u.free),
                           lane=(SC, DVE)[g])
                    bk.free = (e,)
                    outs.append(e)
                w_slot.free = (t,)
                u.ready = tuple(outs) if b % 2 == 0 else tuple(u.ready) + tuple(outs)

            fetch_v(0)
            for b in (0, 1):
                for step in split_queries(b, start):
                    pass
                stack_queries(b)
            for p in range(PAIRS):
                t = row_max(0, p)
            max_parts(t)
            max_rows(0)
            weights = None
            open_steps = []
            for b in range(B + 1):
                for k in range(KT if b < B else 3):
                    if b < B:
                        if k == 0 and 0 < b < B - 1:
                            stack_keys(b + 1)
                            stack_queries(b + 1)
                        made = exponentials(b, k)
                    open_steps = [g for g in open_steps if next(g, "end") != "end"]
                    if b + 2 < B and k in KEY_STEPS:
                        open_steps.append(key_chunk(b + 2, KEY_STEPS.index(k), w_key, work,
                                                    rest_for=1 if k == KEY_STEPS[0] else 0))
                        next(open_steps[-1])
                    if b + 1 < B and k == KT - 1:
                        max_rows(b + 1)
                    if weights is not None:
                        weigh(*weights)
                    weights = (b, k, made) if b < B else None
                    if b > 0:
                        if k == 0:
                            normalise(b - 1)
                        if k == 1:
                            turn(b - 1)
                        if k == 2 and b % 2 == 0:
                            project_pair(b // 2 - 1, u_r.slots[u_r.n % len(u_r.slots)], table, dst, work.next(), None)
                    if k == 1 and b + 1 < B:
                        fetch_v(b + 1)
                    if k == 9 and b + 3 < B:
                        fetch_t(b + 3)
                    if b + 1 < B:
                        for p in MAX_STEPS.get(k, ()):
                            t_max = row_max(b + 1, p)
                            if p == PAIRS - 1:
                                max_parts(t_max)
                    if b + 2 < B and k == 3:
                        open_steps.append(split_queries(b + 2, ()))
                        next(open_steps[-1])

        def cross_buffers(st, arena, pt_tiles, t_banks):
            w = pt_tiles * 128
            pw = L if pt_tiles == KT else L + S
            return dict(
                p_ring=Ring([Slot(arena[:, i * pw:(i + 1) * pw]) for i in range(2)]),
                pt_ring=Ring([Slot(arena[0:KN, 2 * pw + i * w:2 * pw + (i + 1) * w].rearrange(
                    "p (k r) -> p k r", k=pt_tiles)) for i in range(2)]),
                stat_ring=Ring([Slot(sb(st, f"cross_stat{i}", [128, 4])) for i in range(4)]),
                w_ring=Ring([Slot(sb(st, f"cross_w{i}", [128, 128])[:, :]) for i in range(2)]),
                u_ring=Ring([Slot(sb(st, f"cross_u{i}", [128, H, 2 * S])[:, :, :]) for i in range(2)]),
                t_ring=Ring([bank[i] for i in t_banks]),
            )

        def streamed(st, name, shape, source):
            slots = [Slot(sb(st, f"{name}{i}", shape), arrival(f"{name}{i}_arrived")) for i in range(2)]

            def fetch(b):
                s = slots[b % 2]
                s.ready = (load(s.ap[:, :] if len(shape) == 2 else s.ap[:, :, :], source(b), s.arrival,
                                tuple(s.free) + tuple(s.ready)),)

            return slots, fetch

        if FIRST == 0 or FIRST <= 2 <= LAST:
            with ExitStack() as st:
                w = sb(st, "adaln_w", [128, 2 * NORMS * 128])[:, :]
                bcol = sb(st, "adaln_b", [128, 2 * NORMS])[:, :]
                load(w, dr["adaln_w"], a_w)
                t_w = load(bcol, dr["adaln_b"], a_w)
                gbv = gb[:, :, :, :].rearrange("p n k b -> p (n k) b")
                for g in range(2):
                    for k in range(NORMS):
                        n = NORMS * g + k
                        t = mm(psum[:, g, k * B:(k + 1) * B], w[:, n * 128:(n + 1) * 128], cond, after=[t_w])
                    t = tt(gbv[:, NORMS * g:NORMS * (g + 1), :], psum[:, g, 0:NORMS * B].rearrange("p (n b) -> p n b", b=B),
                           spread(bcol[:, NORMS * g:NORMS * (g + 1)], B), ALU.add, [t, t_w])
                t = ts(gb[:, :, 0, :], gb[:, :, 0, :], 1.0, None, ALU.add, after=[t])
            fence()

        def adaln(n):
            return gb[:, n, 0, :], gb[:, n, 1, :]

        if FIRST <= 0 <= LAST:
            layernorm(x, z)
            with ExitStack() as st:
                cos = sb(st, "rope_cos", [128, L])[:, :]
                sin = sb(st, "rope_sin", [128, L])[:, :]
                block_diag = sb(st, "head_of_feature", [128, H])[:, :]
                wq = sb(st, "l0_w", [128, 12 * 128])[:, :]
                wf2 = sb(st, "l0_f2", [128, 4, 128])[:, :, :]
                bias = sb(st, "l0_bias", [128, NL, 5])
                fold = sb(st, "l0_fold", [128, H, 128])[:, :, :]
                parity = sb(st, "head_parity", [128, 2])[:, :]
                mask_rows = sb(st, "ctx_mask_rows", [B, L], BF16)[:, :]
                src_mask = sb(st, "src_mask", [128, T], BF16)[:, :]
                a_layer, a_head, a_f2 = arrival("l0_w_arrived"), arrival("l0_heads_arrived"), arrival("l0_f2_arrived")
                q_rot = sb(st, "l0_q", [128, T])[:, :]
                load(cos, dr["rope_cos"], a_w)
                load(sin, dr["rope_sin"], a_w)
                load(block_diag, dr["head_of_feature"], a_w)
                load(parity, dr["head_parity"], a_w)
                with ExitStack() as s2:
                    src_mask8 = sb(s2, "src_mask8", [128, T], U8)[:, :]
                    ctx_mask8 = sb(s2, "ctx_mask8", [B, L], U8)[:, :]
                    load(ctx_mask8, dr["ctx_mask"], a_w)
                    load(bias[:, :, :], dr["l0_bias"], a_w)
                    t_c = load(src_mask8, dr["src_mask"].partition_broadcast(128), a_w)
                    ts(src_mask, src_mask8, LOW, None, ALU.mult, after=[t_c], lane=PL)
                    t_m = ts(mask_rows, ctx_mask8, LOW, None, ALU.mult, after=[t_c], lane=PL)
                    for lane in (PE, DVE, SC, PL, SY):
                        lane.wait([t_c, t_m])
                tmp = dev

                def rope(dst, w0, w_swapped, scale, after):
                    for c in range(2):
                        t1 = mm(psum[:, c, 0:HALF], w0, halves(xn)[c], after=after)
                        t2 = mm(psum[:, 2 + c, 0:HALF], w_swapped, halves(xn)[c], after=after)
                        cs = cos[:, 0:S].unsqueeze(1).broadcast_to([128, BH, S])
                        sn = sin[:, 0:S].unsqueeze(1).broadcast_to([128, BH, S])
                        v = lambda a: a.rearrange("p (b s) -> p b s", s=S)
                        d, m = halves(dst)[c], halves(tmp)[c]
                        t1 = stt(v(d), v(psum[:, c, 0:HALF]), scale, cs, ALU.mult, ALU.mult, list(after) + [t1])
                        t2 = stt(v(m), v(psum[:, 2 + c, 0:HALF]), scale, sn, ALU.mult, ALU.mult, [t2, t1])
                        t = tt(d, d, m, ALU.add, [t2])
                    return t

                def block_queries(ring, src):
                    after = tuple(now())

                    def get(b):
                        s = ring.next()
                        q = src[:, b * S:(b + 1) * S].unsqueeze(1).broadcast_to([128, H, S])
                        t = tt(s.ap, q, spread(block_diag, S), ALU.mult, after + tuple(s.free), lane=PL)
                        return s.ap.rearrange("p h q -> p (h q)"), (t,), s
                    return get

                q_scale = float(np.float32(1.0) / np.float32(np.sqrt(8.0)))
                col = lambda k: wq[:, k * 128:(k + 1) * 128]

                def fold_layer(i, k):
                    with ExitStack() as s3:
                        heads = [sb(s3, f"l0_heads{j}", [8, H, 128])[:, :, :] for j in range(2)]
                        load(heads[0], dr["l0_heads"][i, k], a_head, again(a_head))
                        t = load(heads[1], dr["l0_heads"][i, k + 1], a_head)
                        fold_heads(heads[0], heads[1], fold, now() + [t])

                shared = split_keys(st, q_rot, cos, sin, parity, mask_rows)
                fetch_t, key_chunk, stack_keys = shared[2:5]
                open_steps = []

                def first_keys(i):
                    open_steps[:] = [g for g in open_steps if next(g, "end") != "end"]
                    if i in (9, 18):
                        stack_keys(i // 9 - 1)
                    if i < 18 and i % 3 == 0:
                        open_steps.append(key_chunk(i // 9, i // 3 % 3, col(6), Ring(bank[6:8])))
                        next(open_steps[-1])
                    if i == 7:
                        fetch_t(2)

                for i in range(NL):
                    fetch_t(0)
                    fetch_t(1)
                    t_wq = load(wq, dr["l0_w"][i], a_layer, again(a_layer))
                    fold_layer(i, 0)
                    layernorm(z, xn, per_batch=adaln(3 * i))
                    rope(q_rot, col(0), col(1), q_scale, now() + [t_wq])
                    with ExitStack() as s2:
                        k_rot = sb(s2, "l0_k", [128, T])[:, :]
                        qd_r = Ring([Slot(sb(s2, f"l0_qd{j}", [128, H, S])[:, :, :]) for j in range(2)])
                        fence()
                        rope(k_rot, col(2), col(3), 1.0, now())
                        self_attention(s2, block_queries(qd_r, q_rot), k_rot, xn, fold, z, key_mask=src_mask,
                                       beside=first_keys)
                    fence()
                    fold_layer(i, 2)
                    layernorm(z, xn, per_batch=adaln(3 * i + 1))
                    rope(q_rot, col(4), col(5), q_scale, now())
                    fence()
                    with ExitStack() as s2:
                        split_cross_attention(s2, shared, col(6), fold, z)
                    fence()
                    t_f2 = load(wf2, dr["l0_f2"][i], a_f2, again(a_f2))
                    layernorm(z, xn, per_batch=adaln(3 * i + 2))
                    with ExitStack() as s2:
                        hid = sb(s2, "l0_hidden", [128, 4, T])
                        after = now()
                        ready = []
                        for f in range(4):
                            bk = (4, 6)[f % 2]
                            t = linear([(col(8 + f), xn)], (bk, bk + 1), after + ready[-4:-2])
                            for c in range(2):
                                ready.append(act(halves(hid[:, f, :])[c], psum[:, bk + c, 0:HALF], ACT.Gelu,
                                                 bias=bias[:, i, f:f + 1], after=after + [t[c]]))
                        t = linear([(wf2[:, f, :], hid[:, f, :]) for f in range(4)], (0, 1), after + ready + [t_f2])
                        for c in range(2):
                            stt(halves(z)[c], psum[:, c, 0:HALF], bias[:, i, 4:5], halves(z)[c], ALU.add, ALU.add,
                                [t[c]])
                    fence()
            tt(x, x, z, ALU.add, now())
            fence()

        def experts(st, items, gates, dst, extra=None):
            u_ring, g_ring = Ring(bank[2:6]), Ring(bank[6:8])
            h_ring = Ring([Slot(sb(st, f"hidden{i}", [128, 2, HALF])) for i in range(3)])
            r_ring = Ring([Slot(sb(st, f"rectified{i}", [128, 2, HALF])) for i in range(2)])
            gs_ring = Ring([Slot(sb(st, f"gate_spread{i}", [128, HALF])[:, :]) for i in range(4)])
            start = tuple(now())
            for bk in bank:
                bk.free = start
            spread_gate = {}
            n_down = [sum(len(it["downs"]) for it in items if it["c"] == c) for c in range(2)]
            done = [0, 0]
            last = [None, None]
            kept = {}

            def up(i):
                it = items[i]
                c = it["c"]
                toks, banks = [], []
                for w in it["ups"]:
                    bk = u_ring.next()
                    toks.append(mm(bk.ap[:, 0:HALF], w, halves(xn)[c], after=bk.free))
                    banks.append(bk)
                g, key = None, (it["gate"], c)
                if it["gate"] is not None:
                    if key not in spread_gate:
                        lhsT, rhs = gates(it["gate"], c)
                        bk, s = g_ring.next(), gs_ring.next()
                        t = mm(bk.ap[:, 0:HALF], lhsT, rhs, after=bk.free)
                        t = cp(s.ap, bk.ap[:, 0:HALF], (t,) + tuple(s.free), lane=SC)
                        bk.free, s.ready = (t,), (t,)
                        spread_gate[key] = s
                    g = spread_gate[key]
                h = h_ring.next()
                h.ready = it["activate"](banks, toks, g, h, r_ring.next())
                kept[i] = h

            def down(i):
                it, h = items[i], kept.pop(i)
                c = it["c"]
                for k, w in enumerate(it["downs"]):
                    done[c] += 1
                    t = mm(bank[c].ap[:, 0:HALF], w, h.ap[:, k, :], done[c] == 1,
                           done[c] == n_down[c] and extra is None, tuple(h.ready) + tuple(bank[c].free), signal=True)
                h.free = (t,)
                last[c] = t

            for i in range(len(items) + 2):
                if i < len(items):
                    up(i)
                if i >= 2:
                    down(i - 2)
            for c in range(2):
                t = last[c]
                if extra is not None:
                    t = mm(bank[c].ap[:, 0:HALF], extra[0], halves(extra[1])[c], False, True)
                last[c] = t
            return last

        def rank_first(first, src, scratch, cols, n, after):
            mx, cand = scratch
            t = red(mx, src, ALU.max, after=after)
            t = tt(cand, src, spread(mx, n), ALU.is_equal, [t])
            down_count = cols.unsqueeze(1).broadcast_to([128, TT, n])
            t = tt(cand, cand, down_count, ALU.mult, [t])
            t = red(mx, cand, ALU.max, after=[t])
            return tt(first, cand, spread(mx, n), ALU.is_equal, [t])

        if FIRST <= 1 <= LAST:
            E, G, TOPG = 64, 8, 4
            with ExitStack() as st:
                up_w = sb(st, "moe_up", [128, E * 64])[:, :]
                down_w = sb(st, "moe_down", [128, E // 2, 128])[:, :, :]
                sh_up = sb(st, "moe_shared_up", [128, 256])[:, :]
                sh_down = sb(st, "moe_shared_down", [128, 2, 128])[:, :, :]
                rw = sb(st, "moe_router", [128, E])[:, :]
                rb = sb(st, "moe_router_bias", [128, E])[:, :]
                lower = sb(st, "moe_lower_group", [128, G, G])[:, :, :]
                load(rw, dr["moe_router"], a_w2)
                load(rb, dr["moe_bias"].partition_broadcast(128), a_w2)
                t_r = load(lower, dr["moe_lower"].rearrange("a b -> (a b)").partition_broadcast(128).rearrange(
                    "p (a b) -> p a b", a=G), a_w2)
                load(up_w, dr["moe_up"], a_w)
                load(down_w, dr["moe_down"], a_w)
                load(sh_up, dr["moe_shared_up"], a_w)
                t_w = load(sh_down, dr["moe_shared_down"], a_w)
                grid = lambda name, *shape: sb(st, name, [128, TT, *shape])
                score = grid("moe_score", E)[:, :, :]
                sfc = grid("moe_biased", E)[:, :, :]
                top = grid("moe_group_top", G, 8)
                gs = grid("moe_group_score", G)[:, :, :]
                cmp_, eq = grid("moe_cmp", G, G)[:, :, :, :], grid("moe_eq", G, G)[:, :, :, :]
                keep = grid("moe_group_keep", G)[:, :, :]
                m8 = grid("moe_top8", 8)
                rep = grid("moe_replaced", E)
                tot = sb(st, "moe_total", [128, 2, TT])
                wide = sb(st, "moe_expert_rows", [E, E * 64])[:, :]
                cp(wide.rearrange("p (e i) -> p e i", e=E), spread(ident[0:E, 0:E], 64), lane=DVE)
                combT = sb(st, "moe_combine_rows", [E, T])[:, :]
                layernorm(x, xn)
                t = to_tokens(xn, rw, E, 7, now() + [t_r])
                t = act(score, psum[:, 7, 0:TT * E].rearrange("p (t e) -> p t e", t=TT), ACT.Sigmoid, after=[t])
                t = tt(sfc, score, rb.unsqueeze(1).broadcast_to([128, TT, E]), ALU.add, [t, t_r])
                for i in range(TT):
                    for g in range(G):
                        t1 = max8(top[:, i, g, :], sfc[:, i, g * 8:g * 8 + 8], [t])
                t = tt(gs, top[:, :, :, 0], top[:, :, :, 1], ALU.add, [t1])
                other = gs.unsqueeze(2).broadcast_to([128, TT, G, G])
                mine = gs.unsqueeze(3).broadcast_to([128, TT, G, G])
                t1 = tt(cmp_, other, mine, ALU.is_gt, [t])
                t2 = tt(eq, other, mine, ALU.is_equal, [t])
                for i in range(TT):
                    t3 = tt(eq[:, i, :, :], eq[:, i, :, :], lower, ALU.mult, [t2])
                t = tt(cmp_, cmp_, eq, ALU.add, [t1, t3])
                t = red(gs, cmp_, ALU.add, after=[t])
                t = ts(keep, gs, float(TOPG), None, ALU.is_lt, after=[t])
                sfg = sfc.rearrange("p t (g k) -> p (t g) k", g=G)
                t = tt(sfg, sfg, spread(keep.rearrange("p t g -> p (t g)"), E // G), ALU.mult, [t])
                for i in range(TT):
                    t1 = max8(m8[:, i, :], sfc[:, i, :], [t])
                    t1 = replace8(rep[:, i, :], m8[:, i, :], sfc[:, i, :], [t1])
                t = tt(sfc, rep[:, :, :], sfc, ALU.is_lt, [t1])
                t = tt(sfc, sfc, score, ALU.mult, [t])
                t = red(tot[:, 0, :], sfc, ALU.add, after=[t])
                t = ts(tot[:, 0, :], tot[:, 0, :], 1e-20, None, ALU.add, after=[t])
                t = recip(tot[:, 1, :], tot[:, 0, :], [t])
                t = tt(sfc, sfc, spread(tot[:, 1, :], E), ALU.mult, [t])
                t = ts(sfc, sfc, 2.5, None, ALU.mult, after=[t])
                to_rows(sfc, E, combT, [t])
                for lane in (PE,):
                    lane.wait([t_w])

                def relu2(banks, toks, g, h, r):
                    t = act(r.ap[:, 0, :], banks[0].ap[:, 0:HALF], ACT.Relu, after=(toks[0],) + tuple(r.free))
                    banks[0].free = (t,)
                    if g is None:
                        t = tt(h.ap[:, 0, :], r.ap[:, 0, :], r.ap[:, 0, :], ALU.mult, (t,) + tuple(h.free))
                    else:
                        t = tt(r.ap[:, 1, :], r.ap[:, 0, :], g.ap, ALU.mult, (t,) + tuple(g.ready))
                        g.free = (t,)
                        t = tt(h.ap[:, 0, :], r.ap[:, 1, :], r.ap[:, 0, :], ALU.mult, (t,) + tuple(h.free))
                    r.free = (t,)
                    return (t,)

                items = [dict(c=c, ups=[up_w[:, p * 128:(p + 1) * 128]], downs=[down_w[:, p, :]], gate=p, activate=relu2)
                         for p in range(E // 2) for c in range(2)]
                items += [dict(c=c, ups=[sh_up[:, p * 128:(p + 1) * 128]], downs=[sh_down[:, p, :]], gate=None,
                               activate=relu2) for p in range(2) for c in range(2)]
                last = experts(st, items, lambda p, c: (wide[:, p * 128:(p + 1) * 128], halves(combT)[c]), x)
                for c in range(2):
                    tt(halves(x)[c], bank[c].ap[:, 0:HALF], halves(x)[c], ALU.add, [last[c]])
            fence()

        HD1 = 64

        def attention_tables(st, names, tables, arr):
            bufs = [sb(st, f"by_head{i}", [HD1, H, 128])[:, :, :] for i in range(2)]
            for k, table in enumerate(tables):
                load(bufs[0], dr[names[2 * k]], arr, again(arr))
                t = load(bufs[1], dr[names[2 * k + 1]], arr)
                fold_heads(bufs[0], bufs[1], table, now() + [t])

        def pair_queries(slots, fold, src, ring):
            chunk_ = scale_queries(fold, src, ring, now())

            def chunk(pair, g):
                s = slots[pair % 2]
                t = chunk_(pair, s, g)
                s.ready = (t,) if g == 0 else s.ready + (t,)

            def get(b):
                s = slots[(b // 2) % 2]
                return s.ap[:, b % 2, :, :].rearrange("p h q -> p (h q)"), s.ready, s
            return chunk, get

        if FIRST <= 2 <= LAST:
            layernorm(x, z)
            with ExitStack() as st:
                bo = sb(st, "l1_bias", [128, 2 + 8 + 1])
                a_h = arrival("l1_heads_arrived")
                t_b = load(bo[:, :], dr["l1_bias"], a_w)
                w1 = sb(st, "l1_ff1", [128, 8 * 128])[:, :]
                w2 = sb(st, "l1_ff2", [128, 4, 128])[:, :, :]
                load(w1, dr["l1_ff1"], a_w)
                t_w = load(w2, dr["l1_ff2"], a_w)
                for lane in (PE, DVE, SC):
                    lane.wait([t_w])
                q_fold = sb(st, "l1_q_fold", [128, H, 128])[:, :, :]
                o_fold = sb(st, "l1_o_fold", [128, H, 128])[:, :, :]
                q_slots = [Slot(sb(st, f"l1_q{i}", [128, 2, H, S])) for i in range(2)]
                for s in q_slots:
                    s.scale = 1.0 / np.sqrt(HD1)
                with ExitStack() as s2:
                    attention_tables(s2, ["l1_q1", "l1_k1", "l1_v1", "l1_o1"], [q_fold, o_fold], a_h)
                    layernorm(z, xn, per_batch=adaln(3 * NL))
                    chunk, get = pair_queries(q_slots, q_fold, xn, Ring([bank[6]]))

                    def query(b):
                        if b % 2 == 0:
                            for g in range(4):
                                chunk(b // 2, g)
                        return get(b)
                    self_attention(s2, query, xn, xn, o_fold, z, bias_col=bo[:, 0:1])
                fence()
                with ExitStack() as s2:
                    with ExitStack() as s3:
                        attention_tables(s3, ["l1_q2", "l1_k2", "l1_v2", "l1_o2"], [q_fold, o_fold], a_h)
                        layernorm(z, xn, per_batch=adaln(3 * NL + 1))
                        fence()
                    arena = sb(s2, "l1_arena", [128, 2 * L + 2 * KT * 128])[:, :]
                    bufs = cross_buffers(s2, arena, KT, (3, 4, 5))
                    for bk in bank:
                        bk.free = tuple(now())
                    for s in q_slots:
                        s.free = tuple(now())
                    ctx_t, fetch_t = streamed(s2, "ctx_t", [128, L], lambda b: dr["ctxT"][b])
                    ctx_v, fetch_v = streamed(s2, "ctx_v", [KN, KT, 128], lambda b: dr["ctxV"][b])
                    chunk, get = pair_queries(q_slots, q_fold, xn, bufs["t_ring"])
                    fetch_t(0)
                    fetch_v(0)
                    for g in range(4):
                        chunk(0, g)
                    part = [sb(s2, f"stat_part{i}", [KN, KT, 6]) for i in range(2)]
                    both = sb(s2, "stat_mean_var", [KN, B, KT, 2])
                    part_read = {}

                    def statistics(b, r):
                        if r == R - 1:
                            return
                        s = ctx_v[b % 2]
                        for k in (2 * r, 2 * r + 1):
                            t = bn_stats(part[b % 2][:, k, :], s.ap[:, k, :],
                                         tuple(s.ready) + ((part_read[b - 2],) if b >= 2 else ()))
                        stats_read[b] = t
                        for k in (2 * r, 2 * r + 1):
                            t = bn_aggr(both[:, b, k, :], part[b % 2][:, k, :], [t])
                        part_read[b] = t

                    stats_read, v_read = {}, [()]

                    def hooks(b, r):
                        if b > 0 and r == 0:
                            v_read[0] = (stats_read[b - 1],)
                        statistics(b, r)
                        if r == 1 and b + 1 < B:
                            fetch_t(b + 1)
                            s = ctx_v[(b + 1) % 2]
                            s.free = tuple(s.free) + tuple(v_read[0])
                            fetch_v(b + 1)
                        if b % 2 == 1 and b + 1 < B and 1 <= r <= 4:
                            chunk(b // 2 + 1, r - 1)

                    cross_attention(bufs, [500] * 3, hooks, get,
                                    lambda b: (ctx_t[b % 2].ap, ctx_t[b % 2].ready, ctx_t[b % 2]),
                                    lambda b: (ctx_v[b % 2].ap, ctx_v[b % 2].ready, ctx_v[b % 2]),
                                    o_fold, z, bias_col=bo[:, 1:2])
                    t = act(c_rstd[:, :, :], both[:, :, :, 1], ACT.Sqrt, bias=eps_col[0:KN, :], after=now())
                    recip(c_rstd[:, :, :], c_rstd[:, :, :], [t])
                    cp(c_mean[:, :, :], both[:, :, :, 0], now())
                fence()
                with ExitStack() as s2:
                    layernorm(z, xn, per_batch=adaln(3 * NL + 2))
                    hid = sb(s2, "l1_hidden", [128, 4, T])
                    gate = sb(s2, "l1_gate", [128, 4, T])
                    after = now()
                    ready, freed = [], []
                    for f in range(4):
                        bks = (0, 1, 2, 3) if f % 2 == 0 else (4, 5, 6, 7)
                        aft = after + freed[-2:] if f < 2 else after + freed[2 * (f - 2):2 * (f - 1)]
                        tg = linear([(w1[:, (4 + f) * 128:(5 + f) * 128], xn)], bks[0:2], aft)
                        ta = linear([(w1[:, f * 128:(f + 1) * 128], xn)], bks[2:4], aft)
                        for c in range(2):
                            g = halves(gate[:, f, :])[c]
                            t = act(g, psum[:, bks[c], 0:HALF], ACT.Gelu, bias=bo[:, 6 + f:7 + f], after=[tg[c]] + after)
                            t = stt(halves(hid[:, f, :])[c], psum[:, bks[2 + c], 0:HALF], bo[:, 2 + f:3 + f], g, ALU.add,
                                    ALU.mult, [t, ta[c]])
                            freed.append(t)
                    t = linear([(w2[:, f, :], hid[:, f, :]) for f in range(4)], (0, 1), now())
                    for c in range(2):
                        stt(halves(z)[c], psum[:, c, 0:HALF], bo[:, 10:11], halves(z)[c], ALU.add, ALU.add, [t[c]])
            tt(x, x, z, ALU.add, now())
            fence()

        if FIRST <= 3 <= LAST:
            E, CAP = 8, T // 8
            with ExitStack() as st:
                up_w = sb(st, "ec_up", [128, E * 256])[:, :]
                down_w = sb(st, "ec_down", [128, E * 2, 128])[:, :, :]
                wg = sb(st, "ec_gate_w", [128, E])[:, :]
                down_count = sb(st, "ec_index_down", [128, E])[:, :]
                load(wg, dr["ec_gate"], a_w2)
                t_r = load(down_count, dr["index_down"].partition_broadcast(128), a_w2)
                load(up_w, dr["ec_up"], a_w)
                t_w = load(down_w, dr["ec_down"], a_w)
                grid = lambda name, *shape: sb(st, name, [128, TT, *shape])
                probs, sel_t, val, cand, onehot = (grid(f"ec_{n}", E)[:, :, :] for n in
                                                   ("probs", "chosen", "value", "candidate", "expert"))
                tok = sb(st, "ec_token", [128, 3, TT])
                rows = [sb(st, f"ec_rows{i}", [E, T])[:, :] for i in range(2)]
                m8 = sb(st, "ec_top8", [E, 8])[:, :]
                gate_rows = sb(st, "ec_gate_rows", [E, T])[:, :]
                layernorm(x, xn)
                t = to_tokens(xn, wg, E, 7, now() + [t_r])
                lg = psum[:, 7, 0:TT * E].rearrange("p (t e) -> p t e", t=TT)
                t1 = red(tok[:, 0, :], lg, ALU.max, after=[t])
                t = tt(probs, lg, spread(tok[:, 0, :], E), ALU.subtract, [t1])
                t = act(probs, probs, ACT.Exp, after=[t])
                t = red(tok[:, 0, :], probs, ALU.add, after=[t])
                t = recip(tok[:, 1, :], tok[:, 0, :], [t])
                t = tt(probs, probs, spread(tok[:, 1, :], E), ALU.mult, [t])
                t = to_rows(probs, E, rows[0], [t])
                src = rows[0]
                orig = sb(st, "ec_rows_kept", [E, T])[:, :]
                t = [cp(orig, rows[0], t)]
                for k in range(CAP // 8):
                    t = [max8(m8, src, t)]
                    d = rows[(k + 1) % 2]
                    t = [replace8(d, m8, src, t)]
                    src = d
                t = tt(orig, src, orig, ALU.not_equal, t)
                for i in range(TT):
                    t1 = tr(psum[:, 6, i * E:(i + 1) * E], orig[:, i * 128:(i + 1) * 128], [t])
                t = cp(sel_t, psum[:, 6, 0:TT * E].rearrange("p (t e) -> p t e", t=TT), [t1])
                t1 = red(tok[:, 2, :], sel_t, ALU.max, after=[t])
                t = ts(val, sel_t, -LOW, LOW, ALU.mult, ALU.add, after=[t])
                t = tt(val, val, spread(tok[:, 2, :], E), ALU.mult, [t, t1])
                t = tt(val, val, probs, ALU.add, [t])
                t = rank_first(onehot, val, (tok[:, 0, :], cand), down_count, E, [t])
                t = tt(onehot, onehot, probs, ALU.mult, [t])
                to_rows(onehot, E, gate_rows, [t])
                PE.wait([t_w])

                def gelu_gated(banks, toks, g, h, r):
                    outs = []
                    for k in range(2):
                        t = act(r.ap[:, k, :], banks[k].ap[:, 0:HALF], ACT.Gelu, after=(toks[k],) + tuple(r.free))
                        banks[k].free = (t,)
                        t = tt(h.ap[:, k, :], r.ap[:, k, :], g.ap, ALU.mult, (t,) + tuple(h.free) + tuple(g.ready))
                        outs.append(t)
                    g.free, r.free = (t,), (t,)
                    return tuple(outs)

                items = [dict(c=c, ups=[up_w[:, (2 * e + f) * 128:(2 * e + f + 1) * 128] for f in range(2)],
                              downs=[down_w[:, 2 * e + f, :] for f in range(2)], gate=e, activate=gelu_gated)
                         for e in range(E) for c in range(2)]
                last = experts(st, items, lambda g, c: (ident[0:E, g:g + 1].broadcast_to([E, 128]),
                                                        halves(gate_rows)[c]), x)
                for c in range(2):
                    tt(halves(x)[c], bank[c].ap[:, 0:HALF], halves(x)[c], ALU.add, [last[c]])
            fence()

        if LAST >= 4 and 3 <= FIRST <= 6:
            with ExitStack() as st:
                slots, fetch = streamed(st, "ctx_v", [KN, KT, 128], lambda b: dr["ctxV"][b])
                part = [sb(st, f"stat_part{i}", [KN, KT, 6]) for i in range(2)]
                both = sb(st, "stat_mean_var", [KN, B, KT, 2])
                fetch(0)
                for b in range(B):
                    if b + 1 < B:
                        fetch(b + 1)
                    s = slots[b % 2]
                    for k in range(KT):
                        t = bn_stats(part[b % 2][:, k, :], s.ap[:, k, :],
                                     tuple(s.ready) + ((t,) if b >= 2 and k == 0 else ()))
                    s.free = (t,)
                    for k in range(KT):
                        t = bn_aggr(both[:, b, k, :], part[b % 2][:, k, :], [t])
                t = act(c_rstd[:, :, :], both[:, :, :, 1], ACT.Sqrt, bias=eps_col[0:KN, :], after=[t])
                t = recip(c_rstd[:, :, :], c_rstd[:, :, :], [t])
                cp(c_mean[:, :, :], both[:, :, :, 0], [t])
            fence()

        def normalise_context(b, buf, w_row, b_row, after, lane=PL):
            for k in range(KT):
                t = ts(buf[:, k, :], buf[:, k, :], c_mean[:, b, k:k + 1], c_rstd[:, b, k:k + 1], ALU.subtract, ALU.mult,
                       after=after)
            t = tt(buf, buf, w_row.unsqueeze(1).broadcast_to([KN, KT, 128]), ALU.mult, [t], lane=lane)
            return tt(buf, buf, b_row.unsqueeze(1).broadcast_to([KN, KT, 128]), ALU.add, [t], lane=PL)

        if FIRST <= 4 <= LAST:
            with ExitStack() as st:
                aff = sb(st, "l2_affine", [128, 2])
                w_row = sb(st, "l2_ctx_w", [KN, 128])[:, :]
                b_row = sb(st, "l2_ctx_b", [KN, 128])[:, :]
                cond1 = sb(st, "cond_plus_1", [128, B])[:, :]
                a_h = arrival("l2_heads_arrived")
                load(aff[:, :], dr["l2_affine"], a_w)
                load(w_row, dr["l2_ln1_w"].partition_broadcast(KN), a_w)
                t_w = load(b_row, dr["l2_ln1_b"].partition_broadcast(KN), a_w)
                DVE.wait([t_w])
                PL.wait([t_w])
                ts(cond1, cond, 1.0, None, ALU.add)
                q_fold = sb(st, "l2_q_fold", [128, H, 128])[:, :, :]
                o_fold = sb(st, "l2_o_fold", [128, H, 128])[:, :, :]
                with ExitStack() as s3:
                    attention_tables(s3, ["l2_q", "l2_k", "l2_v", "l2_o"], [q_fold, o_fold], a_h)
                layernorm(x, xn)
                layernorm(xn, xn, per_feature=(aff[:, 0:1], aff[:, 1:2]))
                v = xn.rearrange("p (b s) -> p b s", s=S)
                t = tt(v, v, spread(cond1, S), ALU.mult, now())
                t = tt(v, v, spread(cond, S), ALU.add, [t])
                lat = sb(st, "l2_latents", [S, B, 128])[:, :, :]
                for g in range(4):
                    for k in range(4):
                        t1 = tr(psum[0:S, g, k * 128:(k + 1) * 128], xn[:, (4 * g + k) * S:(4 * g + k + 1) * S], [t])
                    cp(lat[:, 4 * g:4 * g + 4, :], psum[0:S, g, :].rearrange("p (k d) -> p k d", k=4), [t1])
                fence()
                arena = sb(st, "l2_arena", [128, 2 * (L + S) + 2 * (KT + 1) * 128])[:, :]
                bufs = cross_buffers(st, arena, KT + 1, (4, 5))
                q_slots = [Slot(sb(st, f"l2_q{i}", [128, 2, H, S])) for i in range(2)]
                for s in q_slots:
                    s.scale = 1.0 / np.sqrt(HD1)
                for bk in bank:
                    bk.free = tuple(now())
                ctx_v, fetch_v = streamed(st, "ctx_v", [KN, KT, 128], lambda b: dr["ctxV"][b])
                k_slots = [Slot(sb(st, f"l2_keys{i}", [128, L + S])[:, :]) for i in range(2)]
                chunk, get = pair_queries(q_slots, q_fold, xn, bufs["t_ring"])

                def norm(b):
                    s = ctx_v[b % 2]
                    s.ready = (normalise_context(b, s.ap[:, :, :], w_row, b_row, s.ready),)

                def key_chunk(b, c):
                    s, k_ = ctx_v[b % 2], k_slots[b % 2]
                    bk = bufs["t_ring"].next()
                    for k in range(4):
                        t = tr(bk.ap[:, k * KN:(k + 1) * KN], s.ap[:, 4 * c + k, :], tuple(s.ready) + tuple(bk.free))
                    e = cp(k_.ap[:, c * 500:(c + 1) * 500], bk.ap[:, 0:500], (t,) + tuple(k_.free), lane=(SC, DVE, SC)[c])
                    bk.free = (e,)
                    if c == 0:
                        k_.ready = (e, cp(k_.ap[:, L:L + S], xn[:, b * S:(b + 1) * S], tuple(k_.free), lane=PL))
                    else:
                        k_.ready += (e,)

                fetch_v(0)
                norm(0)
                for c in range(3):
                    key_chunk(0, c)
                for g in range(4):
                    chunk(0, g)

                def hooks(b, r):
                    if b + 1 < B:
                        if r == 1:
                            fetch_v(b + 1)
                            norm(b + 1)
                        if r in (4, 5, 6):
                            key_chunk(b + 1, r - 4)
                        if b % 2 == 1 and r < 4:
                            chunk(b // 2 + 1, r)

                cross_attention(bufs, [(L + S) // 4] * 4, hooks, get,
                                lambda b: (k_slots[b % 2].ap, k_slots[b % 2].ready, k_slots[b % 2]),
                                lambda b: (ctx_v[b % 2].ap, ctx_v[b % 2].ready, ctx_v[b % 2]),
                                o_fold, x, own_values=lat)
            fence()

        if FIRST <= 5 <= LAST:
            E = 8
            with ExitStack() as st:
                w1 = sb(st, "sm_w1", [128, E * 512])[:, :]
                w3 = sb(st, "sm_w3", [128, E * 512])[:, :]
                w2 = sb(st, "sm_w2", [128, E * 4, 128])[:, :, :]
                wg = sb(st, "sm_gate_w", [128, E])[:, :]
                down_count = sb(st, "sm_index_down", [128, E])[:, :]
                load(wg, dr["sm_gate"], a_w2)
                t_r = load(down_count, dr["index_down"].partition_broadcast(128), a_w2)
                load(w1, dr["sm_w1"], a_w)
                load(w3, dr["sm_w3"], a_w)
                t_w = load(w2, dr["sm_w2"], a_w)
                grid = lambda name: sb(st, name, [128, TT, E])[:, :, :]
                sco, mag, fac, cand, hot, s2_, ex, gate = (grid(f"sm_{n}") for n in (
                    "scores", "magnitude", "factor", "candidate", "onehot", "rest", "exp", "gate"))
                mx, mx2, sm_, inv = (sb(st, f"sm_token_{n}", [128, TT])[:, :] for n in ("max", "tmp", "sum", "inv"))
                gate_rows = sb(st, "sm_gate_rows", [E, T])[:, :]
                layernorm(x, xn)
                t = to_tokens(xn, wg, E, 7, now() + [t_r])
                t = cp(sco, psum[:, 7, 0:TT * E].rearrange("p (t e) -> p t e", t=TT), [t])
                t = act(mag, sco, ACT.Abs, after=[t])
                src = sco
                for k in range(2):
                    t = red(mx, src, ALU.max, after=[t])
                    t = rank_first(hot, src, (mx2, cand), down_count, E, [t])
                    t = tt(fac, mag, spread(mx, E), ALU.max, [t])
                    t = ts(fac, fac, 0.02, None, ALU.mult, after=[t])
                    t = tt(ex, spread(mx, E), sco, ALU.subtract, [t])
                    t = tt(fac, ex, fac, ALU.is_gt, [t])
                    t = ts(fac, fac, -1.0, 1.0, ALU.mult, ALU.add, after=[t])
                    t = tt(ex, src, spread(mx, E), ALU.subtract, [t])
                    t = act(ex, ex, ACT.Exp, after=[t])
                    t = tt(ex, ex, fac, ALU.mult, [t])
                    t = red(sm_, ex, ALU.add, after=[t])
                    t = recip(inv, sm_, [t])
                    if k == 0:
                        t = tt(gate, hot, spread(inv, E), ALU.mult, [t])
                        t = stt(s2_, hot, LOW, sco, ALU.mult, ALU.add, [t])
                        src = s2_
                    else:
                        t = tt(hot, hot, spread(inv, E), ALU.mult, [t])
                        t = tt(gate, gate, hot, ALU.add, [t])
                to_rows(gate, E, gate_rows, [t])
                PE.wait([t_w])

                def silu_gated(banks, toks, g, h, r):
                    t = act(r.ap[:, 0, :], banks[0].ap[:, 0:HALF], ACT.Silu, after=(toks[0],) + tuple(r.free))
                    banks[0].free = (t,)
                    t = tt(r.ap[:, 1, :], r.ap[:, 0, :], banks[1].ap[:, 0:HALF], ALU.mult, (t, toks[1]))
                    banks[1].free = (t,)
                    t = tt(h.ap[:, 0, :], r.ap[:, 1, :], g.ap, ALU.mult, (t,) + tuple(h.free) + tuple(g.ready))
                    g.free, r.free = (t,), (t,)
                    return (t,)

                items = [dict(c=c, ups=[w1[:, (4 * e + f) * 128:(4 * e + f + 1) * 128],
                                        w3[:, (4 * e + f) * 128:(4 * e + f + 1) * 128]],
                              downs=[w2[:, 4 * e + f, :]], gate=e, activate=silu_gated)
                         for e in range(E) for c in range(2) for f in range(4)]
                last = experts(st, items, lambda g, c: (ident[0:E, g:g + 1].broadcast_to([E, 128]),
                                                        halves(gate_rows)[c]), x)
                for c in range(2):
                    tt(halves(x)[c], bank[c].ap[:, 0:HALF], halves(x)[c], ALU.add, [last[c]])
            fence()

        if FIRST <= 6 <= LAST:
            with ExitStack() as st:
                xin = sb(st, "slot_context", [KN, B, KT, 128])
                wts = sb(st, "slot_w", [128, 6, 128])
                colv = sb(st, "slot_cols", [128, 14])
                w_row = sb(st, "slot_ctx_w", [KN, 128])[:, :]
                b_row = sb(st, "slot_ctx_b", [KN, 128])[:, :]
                load(wts[:, :, :], dr["slot_w"], a_w)
                load(colv[:, :], dr["slot_cols"], a_w)
                load(w_row, dr["slot_lnkv_g"].partition_broadcast(KN), a_w)
                t_w = load(b_row, dr["slot_lnkv_b"].partition_broadcast(KN), a_w)
                for lane in (PE, DVE, SC, PL):
                    lane.wait([t_w])
                cq = {n: colv[:, i:i + 1] for i, n in enumerate((
                    "mu", "logsig", "lnq_g", "lnq_b", "lnm_g", "lnm_b", "lnp_g", "lnp_b", "bk", "bv", "bq", "bu", "b1",
                    "b2"))}
                wk_t, wq, wv, wu, w1, w2 = (wts[:, i, :] for i in range(6))
                sig = sb(st, "slot_sigma", [128, 1])[:, :]
                ones = sb(st, "slot_ones", [128, 128])[:, :]
                bk_wide = cq["bk"].broadcast_to([128, 128])
                memset(ones, 1.0)
                act(sig, cq["logsig"], ACT.Exp)
                ring4 = [arrival(f"slot_ctx{i}_arrived") for i in range(4)]
                ready, landed = {}, {}
                for b in range(B):
                    a = ring4[b % 4]
                    landed[b] = load(xin[:, b, :, :], dr["ctxV"][b], a, [(a, a.count)] if a.count else [])

                def norm_ctx(b):
                    ready[b] = normalise_context(b, xin[:, b, :, :], w_row, b_row, [landed[b]], lane=DVE)

                for b in range(3):
                    norm_ctx(b)
                layernorm(x, z, per_feature=(sig, cq["mu"]))
                big = lambda n: sb(st, f"slot_{n}", [128, T])[:, :]
                qT, q2, cbk, upd = big("q"), big("q_folded"), big("bk_q"), big("update")
                x_t = [Slot(sb(st, f"slot_ctxT{i}", [128, L])[:, :]) for i in range(2)]
                at_ = [Slot(sb(st, f"slot_attn{i}", [KN, KT, S])[:, :, :]) for i in range(2)]
                stat = [sb(st, f"slot_stat{i}", [KN, 3, KT]) for i in range(2)]
                rden = [sb(st, f"slot_rden{i}", [128, S])[:, :] for i in range(2)]
                root = float(np.sqrt(np.float32(D)))

                def dense(dst, w, src, bias, after=None, plus=None, func=None, rhs=None):
                    after = now()
                    t = linear([(w, src)], (0, 1), after)
                    for c in range(2):
                        o, i = halves(dst)[c], psum[:, c, 0:HALF]
                        if func is not None:
                            act(o, i, func, bias=bias, after=after + [t[c]])
                        elif plus is not None:
                            stt(o, i, bias, halves(plus)[c], ALU.add, ALU.add, after + [t[c]])
                        elif bias is not None:
                            ts(o, i, bias, None, ALU.add, after=after + [t[c]])
                        else:
                            cp(o, i, after + [t[c]])

                for it in range(3):
                    layernorm(z, xn, per_feature=(cq["lnq_g"], cq["lnq_b"]))
                    dense(qT, wq, xn, cq["bq"])
                    dense(q2, wk_t, qT, None)
                    dense(cbk, bk_wide, qT, None)
                    start = tuple(now())
                    for bk in bank:
                        bk.free = start
                    xp = {}

                    def turn_ctx(b):
                        s = x_t[b % 2]
                        toks = []
                        for g in range(3):
                            bk = bank[g]
                            for k in range(4):
                                t = tr(bk.ap[:, k * KN:(k + 1) * KN], xin[:, b, 4 * g + k, :], tuple(bk.free) + (ready[b],))
                            e = cp(s.ap[:, g * 500:(g + 1) * 500], bk.ap[:, 0:500], (t,) + tuple(s.free),
                                   lane=(SC, DVE, SC)[g])
                            bk.free = (e,)
                            toks.append(e)
                        s.ready = tuple(toks)

                    def slot_softmax(b):
                        s, a, sp = x_t[b % 2], at_[b % 2], stat[b % 2]
                        for k in range(KT):
                            bk = bank[3 + k // 6]
                            t = mm(bk.ap[0:KN, (k % 6) * S:(k % 6 + 1) * S], s.ap[:, k * KN:(k + 1) * KN],
                                   q2[:, b * S:(b + 1) * S], after=tuple(s.ready) + tuple(bk.free))
                        s.free = (t,)
                        lg = psum[0:KN, 3:5, 0:6 * S].rearrange("p c (k s) -> p c k s", s=S)
                        av = a.ap.rearrange("p (c k) s -> p c k s", c=2)
                        cb = cbk[0:KN, b * S:(b + 1) * S].unsqueeze(1).unsqueeze(1).broadcast_to([KN, 2, 6, S])
                        t = tt(av, lg, cb, ALU.add, (t,) + tuple(a.free))
                        bank[3].free = bank[4].free = (t,)
                        t = red(sp[:, 0, :], a.ap, ALU.max, after=(t,))
                        t = tt(a.ap, a.ap, spread(sp[:, 0, :], S), ALU.subtract, (t,))
                        t = act(a.ap, a.ap, ACT.Exp, scale=root, after=(t,))
                        t = red(sp[:, 1, :], a.ap, ALU.add, after=(t,))
                        t = recip(sp[:, 2, :], sp[:, 1, :], (t,))
                        t = tt(a.ap, a.ap, spread(sp[:, 2, :], S), ALU.mult, (t,))
                        t = ts(a.ap, a.ap, 1e-8, None, ALU.add, after=(t,))
                        a.ready = (t,)

                    def slot_update(b):
                        a = at_[b % 2]
                        for k in range(KT):
                            t = mm(bank[5].ap[:, 0:S], xin[:, b, k, :], a.ap[:, k, :], k == 0, k == KT - 1,
                                   tuple(a.ready) + tuple(bank[5].free))
                        for k in range(KT):
                            t2 = mm(bank[6].ap[:, 0:S], ones[0:KN, :], a.ap[:, k, :], k == 0, k == KT - 1,
                                    tuple(bank[6].free))
                        a.free = (t2,)
                        t3 = recip(rden[b % 2], bank[6].ap[:, 0:S], (t2,))
                        bank[6].free = (t3,)
                        t = tt(upd[:, b * S:(b + 1) * S], bank[5].ap[:, 0:S], rden[b % 2], ALU.mult, (t, t3))
                        bank[5].free = (t,)

                    for i in range(B + 2):
                        if i < B:
                            turn_ctx(i)
                        if it == 0 and 3 <= i + 3 < B:
                            norm_ctx(i + 3)
                        if 1 <= i <= B:
                            slot_softmax(i - 1)
                        if i >= 2:
                            slot_update(i - 2)
                    dense(qT, wv, upd, cq["bv"])
                    dense(z, wu, qT, cq["bu"], plus=z)
                    layernorm(z, xn, per_feature=(cq["lnm_g"], cq["lnm_b"]))
                    dense(qT, w1, xn, cq["b1"], func=ACT.Gelu)
                    dense(z, w2, qT, cq["b2"], plus=z)
                    v = z.rearrange("p (b s) -> p b s", s=S)
                    tt(v, v, spread(cond, S), ALU.add, now())
                    layernorm(z, z, per_feature=(cq["lnp_g"], cq["lnp_b"]))
                tt(x, x, z, ALU.add, now())
            fence()

        if FIRST <= 7 <= LAST:
            DEPTH, LEAVES = 4, 16
            NODES = LEAVES - 1
            with ExitStack() as st:
                w1 = sb(st, "fff_w1", [128, 3, LEAVES * 64])
                w2 = sb(st, "fff_w2", [128, 3, LEAVES // 2, 128])
                b1 = sb(st, "fff_b1", [128, 3, LEAVES // 2])
                b2 = sb(st, "fff_b2", [LEAVES, 3, 128])
                nw = sb(st, "fff_node_w", [128, 3 * NODES])[:, :]
                nb = sb(st, "fff_node_b", [128, 3 * NODES])[:, :]
                load(nw, dr["fff_node_w"], a_w2)
                t_r = load(nb, dr["fff_node_b"].partition_broadcast(128), a_w2)
                load(w1[:, :, :], dr["fff_w1"], a_w)
                load(w2[:, :, :, :], dr["fff_w2"], a_w)
                load(b1[:, :, :], dr["fff_b1"], a_w)
                t_w = load(b2[:, :, :], dr["fff_b2"], a_w)
                layernorm(x, xn)
                bit = sb(st, "fff_bit", [128, TT, 3 * NODES])
                path = [sb(st, f"fff_path{d}", [128, TT, 3, 2 ** d]) for d in range(DEPTH + 1)]
                t = to_tokens(xn, nw, 3 * NODES, 7, now() + [t_r])
                t = tt(bit[:, :, :], psum[:, 7, 0:TT * 3 * NODES].rearrange("p (t n) -> p t n", t=TT),
                       nb.unsqueeze(1).broadcast_to([128, TT, 3 * NODES]), ALU.add, [t])
                t = ts(bit[:, :, :], bit[:, :, :], 0.0, None, ALU.is_ge, after=[t])
                t0 = memset(path[0][:, :, :, :], 1.0, lane=DVE)
                bits = bit[:, :, :].rearrange("p t (j n) -> p t j n", j=3)
                t = [t, t0]
                for d in range(DEPTH):
                    w = 2 ** d
                    here = bits[:, :, :, w - 1:2 * w - 1]
                    nxt = path[d + 1][:, :, :, :].rearrange("p t j (n k) -> p t j n k", k=2)
                    for j in range(3):
                        t1 = tt(nxt[:, :, j, :, 1], path[d][:, :, j, :], here[:, :, j, :], ALU.mult, t)
                    for j in range(3):
                        t2 = tt(nxt[:, :, j, :, 0], path[d][:, :, j, :], nxt[:, :, j, :, 1], ALU.subtract, [t1])
                    t = [t2]
                wide = sb(st, "fff_leaf_cols", [LEAVES, LEAVES * 64])[:, :]
                cp(wide.rearrange("p (e i) -> p e i", e=LEAVES), spread(ident[0:LEAVES, 0:LEAVES], 64))
                rows = [sb(st, f"fff_leaf_rows{j}", [LEAVES, T])[:, :] for j in range(3)]
                for j in range(3):
                    t = to_rows(path[DEPTH][:, :, j, :], LEAVES, rows[j], now())
                PE.wait([t_w])
                SC.wait([t_w])
                res = [sb(st, f"fff_{n}", [128, T])[:, :] for n in "qkv"]
                for j in range(3):
                    with ExitStack() as s2:
                        def relu_gated(p):
                            def f(banks, toks, g, h, r):
                                t = act(r.ap[:, 0, :], banks[0].ap[:, 0:HALF], ACT.Relu, bias=b1[:, j, p:p + 1],
                                        after=(toks[0],) + tuple(r.free))
                                banks[0].free = (t,)
                                t = tt(h.ap[:, 0, :], r.ap[:, 0, :], g.ap, ALU.mult, (t,) + tuple(h.free) + tuple(g.ready))
                                g.free, r.free = (t,), (t,)
                                return (t,)
                            return f
                        items = [dict(c=c, ups=[w1[:, j, p * 128:(p + 1) * 128]], downs=[w2[:, j, p, :]], gate=p,
                                      activate=relu_gated(p)) for p in range(LEAVES // 2) for c in range(2)]
                        last = experts(s2, items, lambda p, c: (wide[:, p * 128:(p + 1) * 128],
                                                                halves(rows[j])[c]), x, extra=(b2[:, j, :], rows[j]))
                        for c in range(2):
                            cp(halves(res[j])[c], bank[c].ap[:, 0:HALF], [last[c]])
                    fence()
                q, k_, v_ = res
                p = sb(st, "fff_p", [S, B, S])[:, :, :]
                pt = sb(st, "fff_pt", [S, B, S])[:, :, :]
                vt = sb(st, "fff_v_tokens", [S, B, 128])[:, :, :]
                sst = sb(st, "fff_stat", [S, 3, B])
                for b in range(B):
                    c = slice(b * S, (b + 1) * S)
                    t = mm(psum[0:S, b // 8, (b % 8) * S:(b % 8 + 1) * S], q[:, c], k_[:, c])
                for b in range(B):
                    t1 = tr(psum[0:S, 4 + b // 4, (b % 4) * 128:(b % 4 + 1) * 128], v_[:, b * S:(b + 1) * S])
                sv = psum[0:S, 0:2, 0:HALF].rearrange("p c (b s) -> p c b s", s=S)
                t = red(sst[:, 0, :].rearrange("p (c b) -> p c b", c=2), sv, ALU.max, after=[t])
                for c in range(2):
                    t = tt(p[:, 8 * c:8 * c + 8, :], sv[:, c, :, :], spread(sst[:, 0, 8 * c:8 * c + 8], S), ALU.subtract, [t])
                t = act(p, p, ACT.Exp, scale=float(1.0 / np.sqrt(np.float32(D))), after=[t])
                t = red(sst[:, 1, :], p, ALU.add, after=[t])
                t = recip(sst[:, 2, :], sst[:, 1, :], [t])
                t = tt(p, p, spread(sst[:, 2, :], S), ALU.mult, [t])
                for b in range(B):
                    t2 = tr(psum[0:S, 2 + b // 8, (b % 8) * S:(b % 8 + 1) * S], p[:, b, :], [t])
                e1 = [cp(pt[:, 8 * c:8 * c + 8, :], psum[0:S, 2 + c, 0:HALF].rearrange("p (b s) -> p b s", s=S), [t2])
                      for c in range(2)]
                e1 += [cp(vt[:, 4 * g:4 * g + 4, :], psum[0:S, 4 + g, :].rearrange("p (b d) -> p b d", b=4), [t1], lane=SC)
                       for g in range(4)]
                for b in range(B):
                    t = mm(psum[:, b // 8, (b % 8) * S:(b % 8 + 1) * S], vt[:, b, :], pt[:, b, :], after=e1)
                for c in range(2):
                    tt(halves(x)[c], psum[:, c, 0:HALF], halves(x)[c], ALU.add, [t])
            fence()

        t = load(out, x, a_out, now())
        SY.wait([t])

        block = ctx.enter_context(nc.Block())

        @block.sync
        def _(e):
            SY.run(e)

        @block.tensor
        def _(e):
            PE.run(e)

        @block.vector
        def _(e):
            DVE.run(e)

        @block.scalar
        def _(e):
            SC.run(e)

        @block.gpsimd
        def _(e):
            PL.run(e)


PAIR_ORDER = np.arange(D).reshape(H // 2, 2, 2, D // H // 2).transpose(1, 3, 2, 0).reshape(D)


def rope_tables():
    half = D // H // 2
    inv = (1.0 / 10000.0 ** (np.arange(half, dtype=np.float32) / np.float32(half))).astype(np.float32)
    ang = np.arange(L, dtype=np.float32)[:, None] * inv
    c, s = np.cos(ang).T, np.sin(ang).T
    return (np.ascontiguousarray(np.tile(np.concatenate([c, c]), (H, 1))[PAIR_ORDER], dtype=np.float32),
            np.ascontiguousarray(np.tile(np.concatenate([-s, s]), (H, 1))[PAIR_ORDER], dtype=np.float32))


def swapped(w):
    n, d = w.shape
    return w.reshape(H, 2, n // H // 2, d)[:, ::-1].reshape(n, d)


def layout(v):
    c = np.ascontiguousarray
    a = {}
    a["xT"] = c(v["x"].reshape(T, D).T)
    a["condT"] = c(v["cond_1024"].T)
    ctx = v["ctx_1024"]
    a["ctxT"] = c(ctx.transpose(0, 2, 1))
    a["ctxV"] = c(ctx.reshape(B, KT, KN, D).transpose(0, 2, 1, 3))
    a["src_mask"] = c(v["mask_BxS_bf0"]).reshape(T)
    a["ctx_mask"] = c(v["mask_BxS2_bf0"])
    ws, bs = [], []
    for i in range(NL):
        for n in ("n1", "n2", "n3"):
            ws.append(v[f"L0_xcond_{n}_w"][i].T)
            bs.append(v[f"L0_xcond_{n}_b"][i])
    for n in ("norm1", "norm2", "norm3"):
        ws.append(v[f"L1_xcond_{n}_w"])
        bs.append(v[f"L1_xcond_{n}_b"])
    a["adaln_w"] = c(np.concatenate(ws, axis=1))
    a["adaln_b"] = c(np.stack(bs).reshape(2 * NORMS, 128).T)
    a["rope_cos"], a["rope_sin"] = rope_tables()
    a["head_of_feature"] = (PAIR_ORDER[:, None] // 8 == np.arange(H)[None, :]).astype(np.float32)
    a["head_parity"] = ((PAIR_ORDER[:, None] // 8) % 2 == np.arange(2)[None, :]).astype(np.float32)
    lw, f2, hd, lb = [], [], [], []
    for i in range(NL):
        q, k, vv = (v["L0_xcond_qkv_w"][i][j * D:(j + 1) * D] for j in range(3))
        cq, ck = v["L0_xcond_cq_w"][i], v["L0_xcond_ck_w"][i]
        rows = [m[PAIR_ORDER] for w in (q, k, cq, ck) for m in (w, swapped(w))] + [v["L0_xcond_f1_w"][i]]
        lw.append(np.concatenate(rows).T)
        f2.append(v["L0_xcond_f2_w"][i].T.reshape(4, 128, D).transpose(1, 0, 2))
        by_head = lambda m: m.reshape(H, 8, D).transpose(1, 0, 2)
        hd.append(np.stack([by_head(m) for m in (vv, v["L0_xcond_so_w"][i].T, v["L0_xcond_cv_w"][i],
                                                 v["L0_xcond_co_w"][i].T)]))
        lb.append(np.concatenate([v["L0_xcond_f1_b"][i], v["L0_xcond_f2_b"][i]]).reshape(5, 128).T)
    a["l0_w"], a["l0_f2"], a["l0_heads"] = c(np.stack(lw)), c(np.stack(f2)), c(np.stack(hd))
    a["l0_bias"] = c(np.stack(lb, axis=1))
    a["moe_router"] = c(v["L0_ffn_router_w"].T)
    a["moe_bias"] = c(v["L0_ffn_correction_bias"])
    a["moe_lower"] = (np.arange(8)[None, :] < np.arange(8)[:, None]).astype(np.float32)
    a["moe_up"] = c(v["L0_ffn_up_w"].transpose(1, 0, 2).reshape(D, -1))
    a["moe_down"] = c(v["L0_ffn_down_w"].reshape(32, 128, D).transpose(1, 0, 2))
    a["moe_shared_up"] = c(v["L0_ffn_shared_up_w"])
    a["moe_shared_down"] = c(v["L0_ffn_shared_down_w"].reshape(2, 128, D).transpose(1, 0, 2))
    head64 = lambda m: c(m.reshape(H, 64, D).transpose(1, 0, 2))
    for n in (1, 2):
        for k in "qkv":
            a[f"l1_{k}{n}"] = head64(v[f"L1_xcond_attn{n}_w{k}"].T)
        a[f"l1_o{n}"] = head64(v[f"L1_xcond_attn{n}_wo"])
    a["l1_ff1"] = c(v["L1_xcond_ff_w1"])
    a["l1_ff2"] = c(v["L1_xcond_ff_w2"].reshape(4, 128, D).transpose(1, 0, 2))
    a["l1_bias"] = c(np.concatenate([v["L1_xcond_attn1_bo"], v["L1_xcond_attn2_bo"], v["L1_xcond_ff_b1"],
                                     v["L1_xcond_ff_b2"]]).reshape(11, 128).T)
    a["ec_gate"] = c(v["L1_ffn_Wg"])
    a["ec_up"] = c(v["L1_ffn_W1"].transpose(1, 0, 2).reshape(D, -1))
    a["ec_down"] = c(v["L1_ffn_W2"].reshape(16, 128, D).transpose(1, 0, 2))
    a["index_down"] = np.arange(8, 0, -1).astype(np.float32)
    a["l2_affine"] = c(np.stack([v["L2_xcond_ln2_w"], v["L2_xcond_ln2_b"]], axis=1))
    a["l2_ln1_w"], a["l2_ln1_b"] = c(v["L2_xcond_ln1_w"]), c(v["L2_xcond_ln1_b"])
    a["l2_q"] = head64(v["L2_xcond_Wq"])
    a["l2_k"], a["l2_v"] = head64(v["L2_xcond_Wkv"][:H * 64]), head64(v["L2_xcond_Wkv"][H * 64:])
    a["l2_o"] = head64(v["L2_xcond_Wo"].T)
    a["sm_gate"] = c(v["L2_ffn_gate_w"].T)
    for k in ("w1", "w3"):
        a[f"sm_{k}"] = c(v[f"L2_ffn_{k}"].transpose(2, 0, 1).reshape(D, -1))
    a["sm_w2"] = c(v["L2_ffn_w2"].transpose(0, 2, 1).reshape(32, 128, D).transpose(1, 0, 2))
    w = {k: v[f"L3_xcond_{k}"] for k in ("wk", "wq", "wv", "wu", "w1", "w2")}
    a["slot_w"] = c(np.stack([w["wk"].T] + [w[k] for k in ("wq", "wv", "wu", "w1", "w2")], axis=1))
    a["slot_cols"] = c(np.stack([v[f"L3_xcond_{k}"].reshape(D) for k in (
        "q_mu", "q_logsig", "lnq_g", "lnq_b", "lnm_g", "lnm_b", "lnp_g", "lnp_b", "bk", "bv", "bq", "bu", "b1",
        "b2")], axis=1))
    a["slot_lnkv_g"], a["slot_lnkv_b"] = c(v["L3_xcond_lnkv_g"]), c(v["L3_xcond_lnkv_b"])
    three = lambda k: [v[f"L3_ffn_{j}_{k}"] for j in "qkv"]
    a["fff_node_w"] = c(np.concatenate(three("node_w")).T)
    a["fff_node_b"] = c(np.concatenate(three("node_b")))
    a["fff_w1"] = c(np.stack([m.transpose(1, 0, 2).reshape(D, -1) for m in three("w1")], axis=1))
    a["fff_w2"] = c(np.stack([m.reshape(8, 128, D).transpose(1, 0, 2) for m in three("w2")], axis=1))
    a["fff_b1"] = c(np.stack([m.reshape(8, 128).T for m in three("b1")], axis=1))
    a["fff_b2"] = c(np.stack(three("b2"), axis=1))
    return a


def kernel(**inputs):
    import concourse.bacc as bacc
    from concourse.bass_utils import run_bass_kernel_spmd

    arrays = layout({k: np.asarray(a) for k, a in inputs.items()})
    nc = bacc.Bacc("TRN2", target_bir_lowering=False, num_devices=1)
    dr = {n: nc.dram_tensor(f"in_{n}", a.shape, mybir.dt.from_np(a.dtype), kind="ExternalInput").ap()
          for n, a in arrays.items()}
    out = nc.dram_tensor("out_0", (D, T), F32, kind="ExternalOutput").ap()
    program(nc, dr, out)
    r = run_bass_kernel_spmd(nc, [{f"in_{n}": a for n, a in arrays.items()}], core_ids=[0])
    return np.ascontiguousarray(r.results[0]["out_0"].T).reshape(B, S, D)
```

```python
from contextlib import ExitStack

import numpy as np
import concourse.bass as bass
from concourse import mybir

F32, BF16, U8 = mybir.dt.float32, mybir.dt.bfloat16, mybir.dt.uint8
ALU, ACT, AX = mybir.AluOpType, mybir.ActivationFunctionType, mybir.AxisListType

B, S, D = 16, 56, 128
T = B * S
TT = T // 128
HALF = T // 2
BH = B // 2
L = 1500
KT, KN = 12, 125
H = 16
R = H * S // 128
NL = 6
NORMS = 3 * NL + 3
BANK = 512
LOW = -1e30
EPS = 1e-5
PAIRS, F2 = H // 2, 2 * D // H
K_PARTS, Q_PARTS = (0, 0, 1, 1, 0, 2), (0, 1, 0, 1, 2, 0)
ROWS = F2 * len(K_PARTS)
QC = 2 * S
OTHER_HALF = [i ^ PAIRS for i in range(32)]
KEY_STEPS = (1, 5, 8)
MAX_STEPS = {k: (k - 2,) for k in range(2, 2 + PAIRS)}
SIDE_STEPS = (0, 5, 10, 11)
FIRST, LAST = 0, 7


class Lane:

    def __init__(self, sem):
        self.sem, self.count, self.queue, self.seen = sem, 0, [], {}

    def wait(self, after):
        for source, value in after:
            if self.seen.get(source.sem.name, 0) < value:
                self.seen[source.sem.name] = value
                self.queue.append(lambda e, s=source.sem, v=value: e.wait_ge(s, v))

    def put(self, make, after=(), signal=True):
        self.wait(after)
        if signal:
            self.count += 1
            self.queue.append(lambda e: make(e).then_inc(self.sem, 1))
        else:
            self.queue.append(make)
        return (self, self.count)

    def run(self, e):
        for step in self.queue:
            step(e)


class Arrival:

    def __init__(self, sem):
        self.sem, self.count, self.ready = sem, 0, None


class Slot:

    def __init__(self, ap, arrival=None):
        self.ap, self.ready, self.free, self.arrival = ap, (), (), arrival


class Ring:
    def __init__(self, slots):
        self.slots, self.n = slots, -1

    def next(self):
        self.n += 1
        return self.slots[self.n % len(self.slots)]


def halves(a):
    return [a[:, 0:HALF], a[:, HALF:T]]


def finish(steps):
    for _ in steps:
        pass


def spread(cols, n):
    p, m = cols.shape
    return cols.unsqueeze(2).broadcast_to([p, m, n])


def program(nc, dr, out):
    ctx = ExitStack()
    with ctx:
        names = {}

        def sb(stack, name, shape, dt=F32):
            names[name] = names.get(name, 0) + 1
            if names[name] > 1:
                name = f"{name}_{names[name]}"
            return stack.enter_context(nc.sbuf_tensor(name, shape, dt))

        def sem(name):
            return ctx.enter_context(nc.semaphore(name))

        PE, DVE, SC, PL = (Lane(sem(n)) for n in ("pe_done", "dve_done", "act_done", "pool_done"))
        SY = Lane(None)
        arrival_of = {}

        def arrival(name):
            if name not in arrival_of:
                arrival_of[name] = Arrival(sem(name))
            return arrival_of[name]

        def mm(o, lhsT, rhs, start=True, stop=True, after=(), signal=False):
            return PE.put(lambda e: e.matmul(o, lhsT, rhs, start=start, stop=stop), after, signal=signal or stop)

        def tr(o, i, after=()):
            p = i.shape[0]
            return PE.put(lambda e: e.transpose(o, i, ident[0:p, 0:p]), after)

        def tt(o, a, b, op, after=(), lane=DVE):
            return lane.put(lambda e: e.tensor_tensor(o, a, b, op), after)

        def ts(o, a, s1, s2, op0, op1=None, after=(), lane=DVE):
            if op1 is None:
                return lane.put(lambda e: e.tensor_scalar(o, a, s1, None, op0), after)
            return lane.put(lambda e: e.tensor_scalar(o, a, s1, s2, op0, op1), after)

        def stt(o, a, s, b, op0, op1, after=()):
            return DVE.put(lambda e: e.scalar_tensor_tensor(out=o, in0=a, scalar=s, in1=b, op0=op0, op1=op1), after)

        def cp(o, a, after=(), lane=DVE):
            if lane is SC:
                return act(o, a, ACT.Copy, after=after)
            return lane.put(lambda e: e.tensor_copy(o, a), after)

        def shuffle(o, a, lanes, after=()):
            return DVE.put(lambda e: e.stream_shuffle(o, a, lanes), after)

        def recip(o, a, after=()):
            return DVE.put(lambda e: e.reciprocal(o, a), after)

        def max8(o, a, after=()):
            return DVE.put(lambda e: e.max(o, a), after)

        def replace8(o, found, a, after=()):
            return DVE.put(lambda e: e.match_replace(o, found, a, LOW), after)

        def bn_stats(o, a, after=()):
            return DVE.put(lambda e: e.bn_stats(o, a), after)

        def bn_aggr(o, a, after=()):
            return DVE.put(lambda e: e.bn_aggr(o, a), after)

        def memset(o, value, after=(), lane=None):
            return (lane or PL).put(lambda e: e.memset(o, value), after)

        def red(o, a, op, negate=False, after=(), axis=AX.X):
            return DVE.put(lambda e: e.tensor_reduce(o, a, axis, op, negate=negate), after)

        def act(o, a, func, bias=None, scale=None, accum=None, after=()):
            kw = {}
            if bias is not None:
                kw["bias"] = bias
            if scale is not None:
                kw["scale"] = scale
            if accum is not None:
                kw["accum_out"] = accum
            return SC.put(lambda e: e.activation(o, a, func, **kw), after)

        def load(o, i, arr, after=()):
            SY.wait(after)
            arr.count += 16
            SY.queue.append(lambda e: e.dma_start(o, i).then_inc(arr.sem, 16))
            return (arr, arr.count)

        def again(arr):
            return now() + ([(arr, arr.count)] if arr.count else [])

        def now():
            return [(lane, lane.count) for lane in (PE, DVE, SC, PL) if lane.count]

        def fence():
            done = now() + [(a, a.count) for a in arrival_of.values() if a.count]
            for lane in (PE, DVE, SC, PL, SY):
                lane.wait(done)

        x = sb(ctx, "x_state", [128, T])[:, :]
        z = sb(ctx, "block_state", [128, T])[:, :]
        xn = sb(ctx, "x_normed", [128, T])[:, :]
        dev = sb(ctx, "ln_deviation", [128, T])[:, :]
        sq = sb(ctx, "ln_square", [128, T])[:, :]
        stats = sb(ctx, "ln_token_stats", [128, 16])[:, :]
        ident = sb(ctx, "ident", [128, 128])
        ident_b = sb(ctx, "ident_bf16", [128, 128], BF16)
        mean_w = sb(ctx, "mean_weights", [128, 128])[:, :]
        gb = sb(ctx, "adaln_scale_shift", [128, NORMS, 2, B])
        cond = sb(ctx, "cond", [128, B])[:, :]
        c_mean = sb(ctx, "context_mean", [KN, B, KT])
        c_rstd = sb(ctx, "context_rstd", [KN, B, KT])
        psum = ctx.enter_context(nc.psum_tensor("psum", [128, 8, BANK], F32))
        bank = [Slot(psum[:, i, :]) for i in range(8)]
        a_in, a_w, a_w2 = arrival("in_arrived"), arrival("weights_arrived"), arrival("weights2_arrived")
        a_out = arrival("out_stored")

        t0 = memset(ident[:, :], 0.0)
        t_id = PL.put(lambda e: e.affine_select(out=ident[:, :], in_=ident[:, :], compare_op=ALU.not_equal, fill=1.0,
                                                base=0, pattern=[[-1, 128]], channel_multiplier=1), [t0])
        eps_col = sb(ctx, "eps", [128, 1])[:, :]
        memset(eps_col, EPS)
        t_id = cp(ident_b[:, :], ident[:, :], [t_id], lane=PL)
        t_mw = memset(mean_w, 1.0 / D)
        load(x, dr["xT"], a_in)
        t_x = load(cond, dr["condT"], a_in)
        for lane in (PE, DVE, SC, PL):
            lane.wait([t_x, t_id, t_mw])

        def layernorm(src, dst, per_batch=None, per_feature=None):
            after = now()
            s, d, q, y = (halves(a) for a in (src, dev, sq, dst))
            mean = [psum[:, c, 0:HALF] for c in range(2)]
            t = [mm(mean[c], mean_w, s[c], after=after) for c in range(2)]
            t = [tt(d[c], s[c], mean[c], ALU.subtract, after + [t[c]]) for c in range(2)]
            t = [act(q[c], d[c], ACT.Square, after=after + [t[c]]) for c in range(2)]
            for i in range(TT):
                tv = mm(psum[:, 4, i:i + 1], sq[:, i * 128:(i + 1) * 128], mean_w[:, 0:1], after=t)
            tv = act(stats[:, 0:TT], psum[:, 4, 0:TT], ACT.Sqrt, bias=eps_col, after=[tv])
            tv = recip(stats[:, TT:2 * TT], stats[:, 0:TT], [tv])
            spread_out = [None, None]
            for i in range(TT):
                g, k = i // 4, i % 4
                spread_out[g] = mm(psum[:, 2 + g, k * 128:(k + 1) * 128],
                                   stats[:, TT + i:TT + i + 1].broadcast_to([128, 128]), ident[:, :], after=[tv])
            t = []
            for g, (lo, hi) in enumerate(((0, BANK), (BANK, T))):
                t.append(tt(dst[:, lo:hi], dev[:, lo:hi], psum[:, 2 + g, 0:hi - lo], ALU.mult, [spread_out[g]] + after))
            if per_batch is not None:
                for c in range(2):
                    v = y[c].rearrange("p (b s) -> p b s", s=S)
                    for k, op in ((0, ALU.mult), (1, ALU.add)):
                        t[c] = tt(v, v, spread(per_batch[k][:, c * BH:(c + 1) * BH], S), op, [t[c]])
            if per_feature is not None:
                t = [ts(y[c], y[c], per_feature[0], per_feature[1], ALU.mult, ALU.add, [t[c]]) for c in range(2)]
            return t

        def linear(pieces, banks, after):
            toks = []
            for c in range(2):
                for k, (w, src) in enumerate(pieces):
                    t = mm(psum[:, banks[c], 0:HALF], w, halves(src)[c], k == 0, k == len(pieces) - 1, after)
                toks.append(t)
            return toks

        def to_tokens(src, w, ncols, bnk, after):
            for i in range(TT):
                t = mm(psum[:, bnk, i * ncols:(i + 1) * ncols], src[:, i * 128:(i + 1) * 128], w, True, True, after)
            return t

        def to_rows(src, m, dst, after):
            toks = []
            for g, lo in enumerate(range(0, TT, 4)):
                n = min(4, TT - lo)
                for i in range(n):
                    t = tr(psum[0:m, g, i * 128:(i + 1) * 128], src[:, lo + i, :], after)
                toks.append(cp(dst[:, lo * 128:(lo + n) * 128], psum[0:m, g, 0:n * 128], [t] + after))
            return toks

        def fold_heads(first, second, table, after):
            toks = []
            for g in range(H // 4):
                for k in range(4):
                    h = 4 * g + k
                    t = mm(psum[:, g, k * 128:(k + 1) * 128], first[:, h, :], second[:, h, :], after=after)
                toks.append(cp(table[:, 4 * g:4 * g + 4, :], psum[:, g, :].rearrange("p (h d) -> p h d", h=4),
                               [t] + after, lane=(DVE, SC)[g % 2]))
            return toks

        def scale_queries(fold, src, ring, ready):
            def chunk(pair, slot, g):
                bk = ring.next()
                for k in range(4):
                    t = mm(bk.ap[:, k * 2 * S:(k + 1) * 2 * S], fold[:, 4 * g + k, :],
                           src[:, pair * 2 * S:(pair + 1) * 2 * S], after=tuple(bk.free) + tuple(ready))
                o = slot.ap[:, :, 4 * g:4 * g + 4, :].rearrange("p b h q -> p h b q")
                i = bk.ap[:, 0:8 * S].rearrange("p (h b q) -> p h b q", h=4, b=2)
                t = act(o, i, ACT.Copy, scale=float(slot.scale), after=(t,) + tuple(slot.free))
                bk.free = (t,)
                return t
            return chunk

        def project_pair(pair, slot, table, dst, bk, bias_col):
            for h in range(H):
                t = mm(bk.ap[:, 0:2 * S], table.ap[:, h, :], slot.ap[:, h, :], h == 0, h == H - 1,
                       tuple(bk.free) + tuple(slot.ready) + tuple(table.ready))
            slot.free = (t,)
            d = dst[:, pair * 2 * S:(pair + 1) * 2 * S]
            if bias_col is None:
                t = tt(d, bk.ap[:, 0:2 * S], d, ALU.add, [t])
            else:
                t = stt(d, bk.ap[:, 0:2 * S], bias_col, d, ALU.add, ALU.add, [t])
            bk.free = (t,)

        def self_attention(st, query, keys, values, table, dst, key_mask=None, bias_col=None,
                           beside=lambda i: None):
            p_r = Ring([Slot(sb(st, f"self_p{i}", [128, R, S])[:, :, :]) for i in range(3)])
            pt_r = Ring([Slot(sb(st, f"self_pt{i}", [S, H * S])[:, :]) for i in range(2)])
            v_r = Ring([Slot(sb(st, f"self_v{i}", [S, 128])[:, :]) for i in range(4)])
            st_r = Ring([Slot(sb(st, f"self_stat{i}", [128, 3, R])) for i in range(3)])
            u_r = Ring([Slot(sb(st, f"self_u{i}", [128, H, 2 * S])[:, :, :]) for i in range(2)])
            start = tuple(now())
            for bk in bank:
                bk.free = start
            s_bank, v_bank, o_bank = Ring(bank[0:2]), bank[6], bank[7]
            kept = {}
            ahead = query(0)

            def scores(b):
                nonlocal ahead
                q, q_ready, q_slot = ahead
                bk = s_bank.next()
                for r in range(R):
                    t = mm(bk.ap[:, r * S:(r + 1) * S], q[:, r * 128:(r + 1) * 128], keys[:, b * S:(b + 1) * S],
                           after=tuple(bk.free) + tuple(q_ready))
                q_slot.free = (t,)
                if b + 1 < B:
                    ahead = query(b + 1)
                p, stat = p_r.next(), st_r.next()
                s_in = bk.ap[:, 0:R * S].rearrange("p (r s) -> p r s", r=R)
                t_s = (t,)
                if key_mask is not None:
                    m = key_mask[:, b * S:(b + 1) * S].unsqueeze(1).broadcast_to([128, R, S])
                    t = tt(p.ap, s_in, m, ALU.add, t_s + tuple(p.free))
                    bk.free, s_in = (t,), p.ap
                t = red(stat.ap[:, 0, :], s_in, ALU.max, after=(t,) + tuple(stat.free))
                t = tt(p.ap, s_in, spread(stat.ap[:, 0, :], S), ALU.subtract, (t,) + tuple(p.free))
                if key_mask is None:
                    bk.free = (t,)
                p.ready = (act(p.ap, p.ap, ACT.Exp, after=(t,)),)
                kept[b] = (p, stat)

            def value_tokens(b):
                v = v_r.next()
                t = tr(v_bank.ap[0:S, 0:128], values[:, b * S:(b + 1) * S], v_bank.free)
                t = cp(v.ap, v_bank.ap[0:S, 0:128], (t,) + tuple(v.free), lane=SC)
                v_bank.free, v.ready = (t,), (t,)
                kept[b] += (v,)

            def normalise(b):
                p, stat = kept[b]
                t = red(stat.ap[:, 1, :], p.ap, ALU.add, after=p.ready)
                t = recip(stat.ap[:, 2, :], stat.ap[:, 1, :], (t,))
                t = tt(p.ap, p.ap, spread(stat.ap[:, 2, :], S), ALU.mult, (t,))
                p.ready, stat.free = (t,), (t,)

            def turn(b):
                p, stat, v = kept[b]
                pt = pt_r.next()
                ev = []
                for g, lo in enumerate(range(0, R, 4)):
                    n = min(4, R - lo)
                    bk = bank[2 + g]
                    for i in range(n):
                        t = tr(bk.ap[0:S, i * 128:(i + 1) * 128], p.ap[:, lo + i, :], tuple(bk.free) + tuple(p.ready))
                    e = cp(pt.ap[:, lo * 128:(lo + n) * 128], bk.ap[0:S, 0:n * 128], (t,) + tuple(pt.free), lane=SC)
                    bk.free = (e,)
                    ev.append(e)
                p.free, pt.ready = (t,), tuple(ev)
                kept[b] = (v, pt)

            def weigh(b):
                v, pt = kept.pop(b)
                u = u_r.next() if b % 2 == 0 else u_r.slots[u_r.n % 2]
                outs = []
                for c in range(2):
                    bk = bank[4 + c]
                    t = mm(bk.ap[:, 0:HALF], v.ap, pt.ap[:, c * HALF:(c + 1) * HALF],
                           after=tuple(bk.free) + tuple(pt.ready) + tuple(v.ready))
                    o = u.ap[:, 8 * c:8 * c + 8, (b % 2) * S:(b % 2 + 1) * S]
                    e = cp(o, bk.ap[:, 0:HALF].rearrange("p (h q) -> p h q", q=S), (t,) + tuple(u.free),
                           lane=(SC, DVE)[c])
                    bk.free = (e,)
                    outs.append(e)
                v.free, pt.free = (t,), (t,)
                u.ready = tuple(outs) if b % 2 == 0 else u.ready + tuple(outs)

            for i in range(B + 4):
                if 0 <= i - 1 < B:
                    normalise(i - 1)
                if i < B:
                    scores(i)
                if 0 <= i - 2 < B:
                    value_tokens(i - 2)
                    turn(i - 2)
                if 0 <= i - 4 < B and (i - 4) % 2 == 1:
                    project_pair((i - 4) // 2, u_r.slots[((i - 4) // 2) % 2], table, dst, o_bank, bias_col)
                if 0 <= i - 3 < B:
                    weigh(i - 3)
                beside(i)

        def cross_attention(bufs, widths, hooks, query, keys, values, table, dst, bias_col=None,
                            own_values=None):
            n_s = len(widths)
            width = sum(widths)
            step = widths[0]
            s_banks = psum[:, 0:n_s, 0:step]
            s_free = tuple(now())
            t_ring, u_bank, m_bank = bufs["t_ring"], bank[6], bank[7]
            tiles = KT + (1 if own_values is not None else 0)
            items = [(b, r) for b in range(B) for r in range(R)]
            st = {}
            u_r = bufs["u_ring"]

            def score(i):
                nonlocal s_free
                b, r = items[i]
                q, q_ready, q_slot = query(b)
                k, k_ready, k_slot = keys(b)
                for c in range(n_s):
                    t = mm(s_banks[:, c, :], q[:, r * 128:(r + 1) * 128], k[:, c * step:(c + 1) * step],
                           after=tuple(s_free) + tuple(q_ready) + tuple(k_ready))
                if r == R - 1:
                    q_slot.free = (t,)
                    k_slot.free = (t,)
                return t

            def largest(i, t):
                p, stat = bufs["p_ring"].next(), bufs["stat_ring"].next()
                t = red(stat.ap[:, 1:2], s_banks, ALU.max, negate=True, after=(t,) + tuple(stat.free), axis=AX.XY)
                st[i] = dict(p=p, stat=stat, max=t)

            def exponentials(i):
                nonlocal s_free
                s = st[i]
                t = act(s["p"].ap[:, 0:width].rearrange("p (c n) -> p c n", c=n_s), s_banks, ACT.Exp,
                        bias=s["stat"].ap[:, 1:2], accum=s["stat"].ap[:, 2:3], after=(s["max"],) + tuple(s["p"].free))
                s["exp"], s_free = t, (t,)

            lag = len(t_ring.slots) - 1

            def weigh(i, between):
                s, pt = st[i], bufs["pt_ring"].next()
                v, v_ready, v_slot = values(items[i][0])
                copied = []

                def products(g):
                    for k in range(4 * g, min(4 * g + 4, tiles)):
                        after = (copied[g],) + tuple(v_ready) + tuple(u_bank.free)
                        if k < KT:
                            t = mm(u_bank.ap[:, 0:128], pt.ap[:, k, :], v[:, k, :], k == 0, k == tiles - 1, after)
                        else:
                            t = mm(u_bank.ap[:, 0:128], pt.ap[0:S, k, :], own_values[:, items[i][0], :], False, True,
                                   after)
                    return t

                for g, lo in enumerate(range(0, tiles, 4)):
                    n = min(4, tiles - lo)
                    bk = t_ring.next()
                    rows = KN if lo < KT else S
                    for k in range(n):
                        c0 = (lo + k) * KN
                        t = tr(bk.ap[0:rows, k * 128:(k + 1) * 128], s["p"].ap[:, c0:c0 + rows],
                               tuple(bk.free) + (s["exp"],))
                    e = cp(pt.ap[0:rows, lo:lo + n, :], bk.ap[0:rows, 0:n * 128].rearrange("p (k r) -> p k r", k=n),
                           (t,) + tuple(pt.free), lane=SC if g < 2 else DVE)
                    bk.free = (e,)
                    copied.append(e)
                    if g >= lag:
                        products(g - lag)
                s["p"].free = (t,)
                between()
                for k in range(max(0, g - lag + 1), g + 1):
                    s["u"] = products(k)
                pt.free = (s["u"],)
                if items[i][1] == R - 1:
                    v_slot.free = (s["u"],)

            def inverse(i):
                s = st[i]
                s["inv"] = recip(s["stat"].ap[:, 3:4], s["stat"].ap[:, 2:3], (s["exp"],))

            def normalise(i):
                s = st[i]
                w = bufs["w_ring"].next()
                t = act(w.ap, u_bank.ap[:, 0:128], ACT.Copy, scale=s["stat"].ap[:, 3:4],
                        after=(s["u"], s["inv"]) + tuple(w.free))
                u_bank.free = (t,)
                s["stat"].free = (t,)
                s["w"], s["w_ready"] = w, t

            def turn(i):
                s = st[i]
                s["turned"] = tr(m_bank.ap[:, 0:128], s["w"].ap, (s["w_ready"],) + tuple(m_bank.free))
                s["w"].free = (s["turned"],)

            def gather(i):
                b, r = items[i]
                s = st.pop(i)
                if b % 2 == 0 and r == 0:
                    u_r.next()
                u = u_r.slots[u_r.n % len(u_r.slots)]
                lo, hi = r * 128, (r + 1) * 128
                first = True
                while lo < hi:
                    h, q = divmod(lo, S)
                    n = min(S - q, hi - lo)
                    if q == 0 and hi - lo >= 2 * S:
                        nh = (hi - lo) // S
                        o = u.ap[:, h:h + nh, (b % 2) * S:(b % 2 + 1) * S]
                        i_ = m_bank.ap[:, lo - r * 128:lo - r * 128 + nh * S].rearrange("p (h q) -> p h q", q=S)
                        n = nh * S
                    else:
                        o = u.ap[:, h, (b % 2) * S + q:(b % 2) * S + q + n]
                        i_ = m_bank.ap[:, lo - r * 128:lo - r * 128 + n]
                    t = cp(o, i_, (s["turned"],) + (tuple(u.free) if first else ()))
                    first = False
                    lo += n
                m_bank.free = (t,)
                u.ready = (t,)
                if b % 2 == 1 and r == R - 1:
                    project_pair(b // 2, u, Slot(table), dst, m_bank, bias_col)

            n = len(items)
            for i in range(n + 2):
                if i < n:
                    t = score(i)
                    hooks(*items[i])
                if 0 <= i - 2:
                    normalise(i - 2)
                if 1 <= i <= n:
                    inverse(i - 1)
                if i < n:
                    largest(i, t)
                if 1 <= i <= n:
                    weigh(i - 1, between=lambda: turn(i - 2) if i >= 2 else None)
                if i < n:
                    exponentials(i)
                if i == n + 1:
                    turn(i - 2)
                if i >= 2:
                    gather(i - 2)

        def split_keys(st, q_rot, cos, sin, parity, mask_rows):
            k_stack = [Slot(sb(st, f"key_stack{i}", [ROWS + 4, PAIRS, L], BF16), arrival(f"key_stack{i}_arrived"))
                       for i in range(2)]
            q_stack = [Slot(sb(st, f"query_stack{i}", [ROWS + 4, PAIRS * QC], BF16),
                            arrival(f"query_stack{i}_arrived")) for i in range(2)]
            k_part = Slot(sb(st, "key_parts", [128, 3, L], BF16))
            q_part = Slot(sb(st, "query_parts", [128, 3, QC], BF16))
            q_tmp = Slot(sb(st, "query_block", [128, 2, QC]))
            tm = Slot(sb(st, "key_temp", [128, 2, 500]))
            ctx_t, fetch_t = streamed(st, "ctx_t", [128, L], lambda b: dr["ctxT"][b])
            start = tuple(now())
            ones_rows = k_part.ap[0:3, 0, :]
            t_ones = memset(ones_rows, 1.0, start, DVE)
            for s in k_stack:
                s.ready = (load(s.ap[ROWS + 1:ROWS + 4, :, :], ones_rows.unsqueeze(1).broadcast_to([3, PAIRS, L]),
                                s.arrival, (t_ones,)),)
            k_part.free = k_stack[0].ready + k_stack[1].ready
            for s in q_stack:
                s.free = (memset(s.ap[ROWS:ROWS + 1, :], 1.0, start, DVE),)

            def split(out3, full, rest, after, first_free):
                hi = cp(out3[0], full, tuple(after) + tuple(first_free), lane=SC)
                yield
                t = tt(rest, full, out3[0], ALU.subtract, (hi,))
                mid = cp(out3[1], rest, (t,), lane=SC)
                yield
                lo = tt(out3[2], rest, out3[1], ALU.subtract, (mid,))
                yield (hi, mid, lo)

            def key_chunk(b, c, w_key, work, pause=0, t_w=None):
                src = ctx_t[b % 2]
                cols = slice(c * 500, (c + 1) * 500)
                bk = work.next()
                t = mm(bk.ap[:, 0:500], w_key, src.ap[:, cols],
                       after=tuple(bk.free) + tuple(src.ready) + ((t_w,) if t_w else ()))
                src.free = (t,)
                full, rest = tm.ap[:, 0, :], tm.ap[:, 1, :]
                t2 = shuffle(rest, bk.ap[:, 0:500], OTHER_HALF, (t,) + tuple(tm.free))
                t1 = tt(full, bk.ap[:, 0:500], cos[:, cols], ALU.mult, (t,) + tuple(tm.free))
                bk.free = (t1,)
                t2 = tt(rest, rest, sin[:, cols], ALU.mult, (t2,), lane=PL)
                t = tt(full, full, rest, ALU.add, (t1, t2), lane=PL)
                for _ in range(1 + pause):
                    yield
                first_free = k_part.free
                for done in split([k_part.ap[:, i, cols] for i in range(3)], full, rest, (t,), first_free):
                    if done:
                        tm.free = (done[2],)
                        k_part.ready = done if c == 0 else tuple(k_part.ready) + done
                    yield

            def stack_keys(b):
                s = k_stack[b % 2]
                after = tuple(s.free) + tuple(s.ready) + tuple(k_part.ready)
                for i, part in enumerate(K_PARTS):
                    t = load(s.ap[F2 * i:F2 * i + F2, :, :], k_part.ap[:, part, :], s.arrival, after)
                t = load(s.ap[ROWS:ROWS + 1, :, :], mask_rows[b:b + 1, :].unsqueeze(1).broadcast_to([1, PAIRS, L]),
                         s.arrival, after)
                s.ready, k_part.free = (t,), (t,)

            def split_queries(b, after):
                q = q_rot[:, b * S:(b + 1) * S].unsqueeze(1).broadcast_to([128, 2, S])
                t = tt(q_tmp.ap[:, 0, :].rearrange("p (h q) -> p h q", h=2), q, spread(parity, S), ALU.mult,
                       tuple(after) + tuple(q_tmp.free))
                yield
                for done in split([q_part.ap[:, i, :] for i in range(3)], q_tmp.ap[:, 0, :], q_tmp.ap[:, 1, :], (t,),
                                  q_part.free):
                    if done:
                        q_part.ready, q_tmp.free = done, (done[2],)
                    yield

            def stack_queries(b):
                s = q_stack[b % 2]
                after = tuple(s.free) + tuple(s.ready) + tuple(q_part.ready)
                for i, part in enumerate(Q_PARTS):
                    t = load(s.ap[F2 * i:F2 * i + F2, :].rearrange("j (p c) -> j p c", p=PAIRS), q_part.ap[:, part, :],
                             s.arrival, after)
                s.ready, q_part.free = (t,), (t,)

            return k_stack, q_stack, fetch_t, key_chunk, stack_keys, split_queries, stack_queries

        def split_cross_attention(st, shared, w_key, table, dst, side, rope_done, halves_done):
            k_stack, q_stack, fetch_t, key_chunk, stack_keys, split_queries, stack_queries = shared
            p_ring = Ring([Slot(sb(st, f"weights{i}", [KN, 2, HALF])) for i in range(3)])
            largest = sb(st, "row_max", [QC, PAIRS, 3])
            neg = sb(st, "neg_max", [QC, 2, PAIRS])
            m_part = sb(st, "neg_max_parts", [QC, PAIRS, 4], BF16)
            inv = sb(st, "inverse_sum", [QC, PAIRS])
            w_slot = Slot(sb(st, "normed_out", [QC, PAIRS, 128]))
            u_r = Ring([Slot(sb(st, f"split_u{i}", [128, H, QC])[:, :, :]) for i in range(1)])
            ctx_v = [Slot(sb(st, f"ctx_v_ones{i}", [KN, KT, 129]), arrival(f"ctx_v{i}_arrived")) for i in range(2)]
            start = tuple(now())
            for bk in bank:
                bk.free = start
            s_free = start
            acc_free = start
            work = Ring(bank[5:8])
            for s in ctx_v:
                s.free = (memset(s.ap[:, :, 128:129], 1.0, start, DVE),)
            t_one = memset(m_part[:, :, 0:1], 1.0, start, DVE)

            def acc(p):
                return psum[0:QC, 2 + p // 3, (p % 3) * 129:(p % 3) * 129 + 129]

            def fetch_v(b):
                s = ctx_v[b % 2]
                s.ready = (load(s.ap[:, :, 0:128], dr["ctxV"][b], s.arrival, tuple(s.free) + tuple(s.ready)),)

            def row_max(b, p):
                q, k = q_stack[b % 2], k_stack[b % 2]
                for c in range(3):
                    bk = work.next()
                    t = mm(bk.ap[0:QC, 0:500], q.ap[0:ROWS + 1, p * QC:(p + 1) * QC],
                           k.ap[0:ROWS + 1, p, c * 500:(c + 1) * 500],
                           after=tuple(bk.free) + tuple(q.ready) + tuple(k.ready))
                    t = red(largest[:, p, c:c + 1], bk.ap[0:QC, 0:500], ALU.max, after=(t,))
                    bk.free = (t,)
                return t

            def max_parts(t):
                nonlocal t_parts
                t = red(neg[:, 0, :], largest[:, :, :], ALU.max, negate=True, after=(t,))
                t = cp(m_part[:, :, 1], neg[:, 0, :], (t, t_one))
                t = tt(neg[:, 1, :], neg[:, 0, :], m_part[:, :, 1], ALU.subtract, (t,))
                t = cp(m_part[:, :, 2], neg[:, 1, :], (t,))
                t_parts = tt(m_part[:, :, 3], neg[:, 1, :], m_part[:, :, 2], ALU.subtract, (t,))

            t_parts = None

            def max_rows(b):
                q = q_stack[b % 2]
                bk = work.next()
                rows = bk.ap[0:4, 0:PAIRS * QC // 2].bitcast(BF16)
                for p in range(PAIRS):
                    t2 = PE.put(transposed(rows[:, p * QC:(p + 1) * QC], m_part[:, p, :], ident_b[0:QC, 0:QC]),
                                (t_parts,) + tuple(bk.free))
                t = cp(q.ap[ROWS:ROWS + 4, :], rows, (t2,))
                bk.free = (t,)
                q.ready = tuple(q.ready) + (t,)

            def transposed(o, i, idn):
                return lambda e: e.transpose(o, i, idn)

            def exponentials(b, k):
                nonlocal s_free
                q, ks, s = q_stack[b % 2], k_stack[b % 2], p_ring.next()
                for p in range(PAIRS):
                    t = mm(psum[0:KN, p // 4, (p % 4) * QC:(p % 4 + 1) * QC], ks.ap[:, p, k * KN:(k + 1) * KN],
                           q.ap[:, p * QC:(p + 1) * QC], after=tuple(s_free) + tuple(q.ready) + tuple(ks.ready))
                t = act(s.ap[:, :, :], psum[0:KN, 0:2, 0:HALF], ACT.Exp, after=(t,) + tuple(s.free))
                s_free = (t,)
                s.ready = (t,)
                if k == KT - 1:
                    q.free, ks.free = (t,), (t,)
                return s

            def weigh(b, k, s):
                nonlocal acc_done
                v = ctx_v[b % 2]
                for p in range(PAIRS):
                    w = s.ap[:, p // 4, (p % 4) * QC:(p % 4 + 1) * QC]
                    acc_done = PE.put(accumulating(acc(p), w, v.ap[:, k, :], k == 0 and p % 3 == 0, k == KT - 1),
                                      tuple(s.ready) + tuple(v.ready) + (tuple(acc_free) if k == 0 else ()))
                s.free = (acc_done,)
                if k == KT - 1:
                    v.free = (acc_done,)

            def accumulating(o, w, v, first, last):
                return lambda e: e.matmul(o, w, v, start=first, stop=last, skip_group_check=True)

            acc_done = None

            def normalise(b):
                nonlocal acc_free
                t1 = recip(inv[:, 0:6].rearrange("p (g i) -> p g i", g=2),
                           psum[0:QC, 2:4, 0:387].rearrange("p g (i c) -> p g i c", c=129)[:, :, :, 128], (acc_done,))
                t1 = recip(inv[:, 6:8], psum[0:QC, 4, 0:258].rearrange("p (i c) -> p i c", c=129)[:, :, 128], (acc_done,))
                toks = []
                for p in range(PAIRS):
                    o, i = w_slot.ap[:, p, :], acc(p)[:, 0:128]
                    after = (t1,) + tuple(w_slot.free)
                    if p < 3:
                        toks.append(act(o, i, ACT.Copy, scale=inv[:, p:p + 1], after=after))
                    else:
                        toks.append(ts(o, i, inv[:, p:p + 1], None, ALU.mult, after=after))
                acc_free = w_slot.ready = tuple(toks)

            def turn(b):
                if b % 2 == 0:
                    u_r.next()
                u = u_r.slots[u_r.n % len(u_r.slots)]
                outs = []
                for g in range(2):
                    bk = work.next()
                    for i in range(4):
                        t = tr(bk.ap[:, i * QC:(i + 1) * QC], w_slot.ap[:, 4 * g + i, :],
                               tuple(w_slot.ready) + tuple(bk.free))
                    e = cp(u.ap[:, 8 * g:8 * g + 8, (b % 2) * S:(b % 2 + 1) * S],
                           bk.ap[:, 0:4 * QC].rearrange("p (h q) -> p h q", q=S), (t,) + tuple(u.free),
                           lane=(SC, DVE)[g])
                    bk.free = (e,)
                    outs.append(e)
                w_slot.free = (t,)
                u.ready = tuple(outs) if b % 2 == 0 else tuple(u.ready) + tuple(outs)

            fetch_v(0)
            finish(split_queries(1, (rope_done["q", 0],)))
            stack_queries(1)
            for p in range(PAIRS):
                t = row_max(0, p)
            max_parts(t)
            max_rows(0)
            weights = None
            open_steps = []
            beside = side(work)
            for b in range(B + 1):
                for k in range(KT if b < B else 3):
                    if b < B:
                        if k == 0 and 0 < b < B - 1:
                            stack_keys(b + 1)
                            stack_queries(b + 1)
                        made = exponentials(b, k)
                    open_steps = [g for g in open_steps if next(g, "end") != "end"]
                    if b + 2 < B and k in KEY_STEPS:
                        open_steps.append(key_chunk(b + 2, KEY_STEPS.index(k), w_key, work,
                                                    pause=1 if k == KEY_STEPS[0] else 0))
                        next(open_steps[-1])
                    if b + 1 < B and k == KT - 1:
                        max_rows(b + 1)
                    if weights is not None:
                        weigh(*weights)
                    weights = (b, k, made) if b < B else None
                    if b > 0:
                        if k == 0:
                            normalise(b - 1)
                        if k == 1:
                            turn(b - 1)
                        if k == 2 and b % 2 == 0:
                            project_pair(b // 2 - 1, u_r.slots[u_r.n % len(u_r.slots)], table, dst, work.next(), None)
                    if k == 1 and b + 1 < B:
                        fetch_v(b + 1)
                    if k == 9 and b + 3 < B:
                        fetch_t(b + 3)
                    if b + 1 < B:
                        for p in MAX_STEPS.get(k, ()):
                            t_max = row_max(b + 1, p)
                            if p == PAIRS - 1:
                                max_parts(t_max)
                    if b + 2 < B and k == 3:
                        open_steps.append(split_queries(b + 2, (rope_done["q", (b + 2) // BH],)))
                        next(open_steps[-1])
                    if k in SIDE_STEPS:
                        next(beside, None)
                    if b == BH and k == 3:
                        halves_done[0] += 1
            finish(beside)

        def cross_buffers(st, arena, pt_tiles, t_banks):
            w = pt_tiles * 128
            pw = L if pt_tiles == KT else L + S
            return dict(
                p_ring=Ring([Slot(arena[:, i * pw:(i + 1) * pw]) for i in range(2)]),
                pt_ring=Ring([Slot(arena[0:KN, 2 * pw + i * w:2 * pw + (i + 1) * w].rearrange(
                    "p (k r) -> p k r", k=pt_tiles)) for i in range(2)]),
                stat_ring=Ring([Slot(sb(st, f"cross_stat{i}", [128, 4])) for i in range(4)]),
                w_ring=Ring([Slot(sb(st, f"cross_w{i}", [128, 128])[:, :]) for i in range(2)]),
                u_ring=Ring([Slot(sb(st, f"cross_u{i}", [128, H, 2 * S])[:, :, :]) for i in range(2)]),
                t_ring=Ring([bank[i] for i in t_banks]),
            )

        def streamed(st, name, shape, source):
            slots = [Slot(sb(st, f"{name}{i}", shape), arrival(f"{name}{i}_arrived")) for i in range(2)]

            def fetch(b):
                s = slots[b % 2]
                s.ready = (load(s.ap[:, :] if len(shape) == 2 else s.ap[:, :, :], source(b), s.arrival,
                                tuple(s.free) + tuple(s.ready)),)

            return slots, fetch

        if FIRST == 0 or FIRST <= 2 <= LAST:
            with ExitStack() as st:
                w = sb(st, "adaln_w", [128, 2 * NORMS * 128])[:, :]
                bcol = sb(st, "adaln_b", [128, 2 * NORMS])[:, :]
                load(w, dr["adaln_w"], a_w)
                t_w = load(bcol, dr["adaln_b"], a_w)
                gbv = gb[:, :, :, :].rearrange("p n k b -> p (n k) b")
                for g in range(2):
                    for k in range(NORMS):
                        n = NORMS * g + k
                        t = mm(psum[:, g, k * B:(k + 1) * B], w[:, n * 128:(n + 1) * 128], cond, after=[t_w])
                    t = tt(gbv[:, NORMS * g:NORMS * (g + 1), :], psum[:, g, 0:NORMS * B].rearrange("p (n b) -> p n b", b=B),
                           spread(bcol[:, NORMS * g:NORMS * (g + 1)], B), ALU.add, [t, t_w])
                t = ts(gb[:, :, 0, :], gb[:, :, 0, :], 1.0, None, ALU.add, after=[t])
            fence()

        def adaln(n):
            return gb[:, n, 0, :], gb[:, n, 1, :]

        if FIRST <= 0 <= LAST:
            layernorm(x, z)
            with ExitStack() as st:
                cos = sb(st, "rope_cos", [128, L])[:, :]
                sin = sb(st, "rope_sin", [128, L])[:, :]
                block_diag = sb(st, "head_of_feature", [128, H])[:, :]
                w_self = sb(st, "l0_w_self", [128, 2, 128])
                w_cross = sb(st, "l0_w_cross", [128, 2, 128])
                w_up = sb(st, "l0_w_up", [128, 4, 128])
                w_down = sb(st, "l0_w_down", [128, 4, 128])
                bias = sb(st, "l0_bias", [128, NL, 5])
                heads = Slot(sb(st, "l0_heads", [128, 2, 4, 128]), arrival("l0_heads_arrived"))
                fold = Slot(sb(st, "l0_fold", [128, H, 128])[:, :, :])
                parity = sb(st, "head_parity", [128, 2])[:, :]
                mask_rows = sb(st, "ctx_mask_rows", [B, L], BF16)[:, :]
                src_mask = sb(st, "src_mask", [128, T], BF16)[:, :]
                a_self, a_cross, a_mlp = (arrival(f"l0_{n}_arrived") for n in ("self", "cross", "mlp"))
                q_rot = sb(st, "l0_q", [128, T])[:, :]
                k_rot = sb(st, "l0_k", [128, T])[:, :]
                load(cos, dr["rope_cos"], a_w)
                load(sin, dr["rope_sin"], a_w)
                load(block_diag, dr["head_of_feature"], a_w)
                load(parity, dr["head_parity"], a_w)
                with ExitStack() as s2:
                    src_mask8 = sb(s2, "src_mask8", [128, T], U8)[:, :]
                    ctx_mask8 = sb(s2, "ctx_mask8", [B, L], U8)[:, :]
                    load(ctx_mask8, dr["ctx_mask"], a_w)
                    load(bias[:, :, :], dr["l0_bias"], a_w)
                    t_c = load(src_mask8, dr["src_mask"].partition_broadcast(128), a_w)
                    ts(src_mask, src_mask8, LOW, None, ALU.mult, after=[t_c], lane=PL)
                    t_m = ts(mask_rows, ctx_mask8, LOW, None, ALU.mult, after=[t_c], lane=PL)
                    for lane in (PE, DVE, SC, PL, SY):
                        lane.wait([t_c, t_m])

                def fetch_self(i):
                    a_self.ready = load(w_self[:, :, :], dr["l0_w"][i][:, 0:2, :], a_self, again(a_self))

                def fetch_cross(i):
                    a_cross.ready = load(w_cross[:, :, :], dr["l0_w"][i][:, 2:4, :], a_cross, again(a_cross))

                def fetch_mlp(i):
                    load(w_up[:, :, :], dr["l0_w"][i][:, 4:8, :], a_mlp, again(a_mlp))
                    a_mlp.ready = load(w_down[:, :, :], dr["l0_f2"][i], a_mlp)

                def fetch_heads(i, k):
                    heads.ready = (load(heads.ap[:, :, :, :], dr["l0_heads"][i, k], heads.arrival,
                                        tuple(heads.free) + tuple(heads.ready)),)

                def fold_steps(work, fold_free):
                    done = ()
                    for g in range(4):
                        bk, t = work.next(), None
                        for r in range(4):
                            w = heads.ap[32 * r:32 * r + D // H, :, g, :]
                            t = mm(bk.ap[:, r * 128:(r + 1) * 128], w[:, 0, :], w[:, 1, :],
                                   after=tuple(bk.free) + tuple(heads.ready) + ((t,) if t else ()))
                        heads.free = (t,)
                        t = cp(fold.ap[:, 4 * g:4 * g + 4, :], bk.ap.rearrange("p (h d) -> p h d", h=4),
                               (t,) + tuple(fold_free), lane=(DVE, SC)[g % 2])
                        bk.free = (t,)
                        done += (t,)
                        fold.ready = done
                        yield

                G4 = HALF // QC
                by_token = lambda a: a.rearrange("p (b s) -> p b s", s=S)

                def norm_steps(c, n, work):
                    after = now()
                    yield
                    src, dst, d, q = (halves(a)[c] for a in (z, xn, dev, sq))
                    scale, shift = (g[:, c * BH:(c + 1) * BH] for g in adaln(n))
                    bk = work.next()
                    t = mm(bk.ap[:, 0:HALF], mean_w, src, after=after + list(bk.free))
                    t_d = tt(d, src, bk.ap[:, 0:HALF], ALU.subtract, after + [t])
                    bk.free = (t_d,)
                    t_q = act(q, d, ACT.Square, after=after + [t_d])
                    yield
                    bk, std = work.next(), stats[0:QC, 2 * G4 * c:2 * G4 * (c + 1)]
                    for g in range(G4):
                        t = mm(bk.ap[0:QC, g:g + 1], q[:, g * QC:(g + 1) * QC], mean_w[:, 0:1],
                               after=after + [t_q] + list(bk.free))
                    t = act(std[:, 0:G4], bk.ap[0:QC, 0:G4], ACT.Sqrt, bias=eps_col[0:QC, :], after=[t])
                    bk.free = (t,)
                    t_r = recip(std[:, G4:2 * G4], std[:, 0:G4], [t])
                    yield
                    bk = work.next()
                    for g in range(G4):
                        t = mm(bk.ap[:, g * QC:(g + 1) * QC], std[:, G4 + g:G4 + g + 1].broadcast_to([QC, 128]),
                               ident[0:QC, 0:QC], after=[t_r] + list(bk.free))
                    t = tt(dst, d, bk.ap[:, 0:HALF], ALU.mult, [t] + after)
                    bk.free = (t,)
                    v = by_token(dst)
                    t = tt(v, v, spread(scale, S), ALU.mult, [t])
                    norm_done[c] = tt(v, v, spread(shift, S), ALU.add, [t])
                    yield

                norm_done, rope_done = [None, None], {}

                def rope_steps(c, name, dst, w, t_w, scale, work):
                    after = now()
                    yield
                    bk = work.next()
                    t = mm(bk.ap[:, 0:HALF], w, halves(xn)[c], after=after + [norm_done[c], t_w()] + list(bk.free))
                    cs, sn = (a[:, 0:S].unsqueeze(1).broadcast_to([128, BH, S]) for a in (cos, sin))
                    o, other = halves(dst)[c], halves(dev)[c]
                    t_o = shuffle(other, bk.ap[:, 0:HALF], OTHER_HALF, after + [t])
                    t = stt(by_token(o), by_token(bk.ap[:, 0:HALF]), scale, cs, ALU.mult, ALU.mult, after + [t])
                    bk.free = (t,)
                    t_o = stt(by_token(other), by_token(other), scale, sn, ALU.mult, ALU.mult, [t_o])
                    rope_done[name, c] = tt(o, o, other, ALU.add, [t, t_o])
                    yield

                def mlp_steps(c, i, work):
                    after = now() + [norm_done[c]]
                    yield
                    hidden = halves(dev) + halves(sq)
                    ready = []
                    for f in range(4):
                        bk = work.next()
                        t = mm(bk.ap[:, 0:HALF], w_up[:, f, :], halves(xn)[c],
                               after=after + [a_mlp.ready] + list(bk.free))
                        t = act(hidden[f], bk.ap[:, 0:HALF], ACT.Gelu, bias=bias[:, i, f:f + 1], after=after + [t])
                        bk.free = (t,)
                        ready.append(t)
                        if f == 1:
                            yield
                    yield
                    bk = work.next()
                    for f in range(4):
                        t = mm(bk.ap[:, 0:HALF], w_down[:, f, :], hidden[f], f == 0, f == 3, ready + list(bk.free))
                    zc = halves(z)[c]
                    t = stt(zc, bk.ap[:, 0:HALF], bias[:, i, 4:5], zc, ALU.add, ALU.add, [t])
                    bk.free = (t,)
                    yield

                q_scale = float(np.float32(1.0) / np.float32(np.sqrt(8.0)))

                def before_self(c, i, work):
                    yield from norm_steps(c, 3 * i, work)
                    yield from rope_steps(c, "q", q_rot, w_self[:, 0, :], lambda: a_self.ready, q_scale, work)
                    yield from rope_steps(c, "k", k_rot, w_self[:, 1, :], lambda: a_self.ready, 1.0, work)

                def before_cross(c, i, work):
                    yield from norm_steps(c, 3 * i + 1, work)
                    yield from rope_steps(c, "q", q_rot, w_cross[:, 0, :], lambda: a_cross.ready, q_scale, work)

                def after_cross(c, i, work):
                    yield from norm_steps(c, 3 * i + 2, work)
                    yield from mlp_steps(c, i, work)
                    if i + 1 < NL:
                        yield from before_self(c, i + 1, work)

                def block_queries(ring):
                    def get(b):
                        s = ring.next()
                        q = q_rot[:, b * S:(b + 1) * S].unsqueeze(1).broadcast_to([128, H, S])
                        t = tt(s.ap, q, spread(block_diag, S), ALU.mult, (rope_done["q", b // BH],) + tuple(s.free),
                               lane=PL)
                        return s.ap.rearrange("p h q -> p (h q)"), (t, rope_done["k", b // BH]), s
                    return get

                shared = split_keys(st, q_rot, cos, sin, parity, mask_rows)
                fetch_t, key_chunk, stack_keys, split_queries, stack_queries = shared[2:7]

                def self_side(i, folding):
                    work = Ring(bank[6:8])
                    keys = []
                    second = after_cross(1, i - 1, work) if i else iter(())
                    first = before_cross(0, i, work)

                    def beside(k):
                        next(folding, None)
                        if k < 7:
                            next(second, None)
                            next(second, None)
                        if k == 6:
                            finish(second)
                            finish(folding)
                            fetch_heads(i, 1)
                        keys[:] = [g for g in keys if next(g, "end") != "end"]
                        if k in (9, 18):
                            stack_keys(k // 9 - 1)
                        if k < 18 and k % 3 == 0:
                            keys.append(key_chunk(k // 9, k // 3 % 3, w_cross[:, 1, :], work, t_w=a_cross.ready))
                            next(keys[-1])
                        if k == 7:
                            fetch_t(2)
                        if k > BH + 3:
                            next(first, None)
                        if k == B + 2:
                            finish(first)
                            finish(split_queries(0, (rope_done["q", 0],)))
                            stack_queries(0)
                    return beside

                def cross_side(i):
                    def steps(work):
                        yield from fold_steps(work, now())
                        if i + 1 < NL:
                            fetch_heads(i + 1, 0)
                        yield from before_cross(1, i, work)
                        while halves_done[0] <= i:
                            yield
                        yield from after_cross(0, i, work)
                    return steps

                halves_done = [0]
                fetch_self(0)
                fetch_heads(0, 0)
                start = Ring(bank[0:8])
                for bk in bank:
                    bk.free = tuple(now())
                for c in range(2):
                    finish(before_self(c, 0, start))
                fence()
                for i in range(NL):
                    fetch_cross(i)
                    fetch_t(0)
                    fetch_t(1)
                    with ExitStack() as s2:
                        qd_r = Ring([Slot(sb(s2, f"l0_qd{j}", [128, H, S])[:, :, :]) for j in range(2)])
                        self_attention(s2, block_queries(qd_r), k_rot, xn, fold, z, key_mask=src_mask,
                                       beside=self_side(i, fold_steps(Ring(bank[6:8]), now())))
                    fence()
                    fetch_mlp(i)
                    if i + 1 < NL:
                        fetch_self(i + 1)
                    with ExitStack() as s2:
                        split_cross_attention(s2, shared, w_cross[:, 1, :], fold, z, cross_side(i), rope_done,
                                              halves_done)
                    fence()
                for bk in bank:
                    bk.free = tuple(now())
                finish(after_cross(1, NL - 1, start))
            tt(x, x, z, ALU.add, now())
            fence()

        def experts(st, items, gates, extra=None):
            u_ring, g_ring = Ring(bank[2:6]), Ring(bank[6:8])
            h_ring = Ring([Slot(sb(st, f"hidden{i}", [128, 2, HALF])) for i in range(3)])
            r_ring = Ring([Slot(sb(st, f"rectified{i}", [128, 2, HALF])) for i in range(2)])
            gs_ring = Ring([Slot(sb(st, f"gate_spread{i}", [128, HALF])[:, :]) for i in range(4)])
            start = tuple(now())
            for bk in bank:
                bk.free = start
            spread_gate = {}
            n_down = [sum(len(it["downs"]) for it in items if it["c"] == c) for c in range(2)]
            done = [0, 0]
            last = [None, None]
            kept = {}

            def up(i):
                it = items[i]
                c = it["c"]
                toks, banks = [], []
                for w in it["ups"]:
                    bk = u_ring.next()
                    toks.append(mm(bk.ap[:, 0:HALF], w, halves(xn)[c], after=bk.free))
                    banks.append(bk)
                g, key = None, (it["gate"], c)
                if it["gate"] is not None:
                    if key not in spread_gate:
                        lhsT, rhs = gates(it["gate"], c)
                        bk, s = g_ring.next(), gs_ring.next()
                        t = mm(bk.ap[:, 0:HALF], lhsT, rhs, after=bk.free)
                        t = cp(s.ap, bk.ap[:, 0:HALF], (t,) + tuple(s.free), lane=SC)
                        bk.free, s.ready = (t,), (t,)
                        spread_gate[key] = s
                    g = spread_gate[key]
                h = h_ring.next()
                h.ready = it["activate"](banks, toks, g, h, r_ring.next())
                kept[i] = h

            def down(i):
                it, h = items[i], kept.pop(i)
                c = it["c"]
                for k, w in enumerate(it["downs"]):
                    done[c] += 1
                    t = mm(bank[c].ap[:, 0:HALF], w, h.ap[:, k, :], done[c] == 1,
                           done[c] == n_down[c] and extra is None, tuple(h.ready) + tuple(bank[c].free), signal=True)
                h.free = (t,)
                last[c] = t

            for i in range(len(items) + 2):
                if i < len(items):
                    up(i)
                if i >= 2:
                    down(i - 2)
            for c in range(2):
                t = last[c]
                if extra is not None:
                    t = mm(bank[c].ap[:, 0:HALF], extra[0], halves(extra[1])[c], False, True)
                last[c] = t
            return last

        def rank_first(first, src, scratch, cols, n, after):
            mx, cand = scratch
            t = red(mx, src, ALU.max, after=after)
            t = tt(cand, src, spread(mx, n), ALU.is_equal, [t])
            down_count = cols.unsqueeze(1).broadcast_to([128, TT, n])
            t = tt(cand, cand, down_count, ALU.mult, [t])
            t = red(mx, cand, ALU.max, after=[t])
            return tt(first, cand, spread(mx, n), ALU.is_equal, [t])

        if FIRST <= 1 <= LAST:
            E, G, TOPG = 64, 8, 4
            with ExitStack() as st:
                up_w = sb(st, "moe_up", [128, E * 64])[:, :]
                down_w = sb(st, "moe_down", [128, E // 2, 128])[:, :, :]
                sh_up = sb(st, "moe_shared_up", [128, 256])[:, :]
                sh_down = sb(st, "moe_shared_down", [128, 2, 128])[:, :, :]
                rw = sb(st, "moe_router", [128, E])[:, :]
                rb = sb(st, "moe_router_bias", [128, E])[:, :]
                lower = sb(st, "moe_lower_group", [128, G, G])[:, :, :]
                load(rw, dr["moe_router"], a_w2)
                load(rb, dr["moe_bias"].partition_broadcast(128), a_w2)
                t_r = load(lower, dr["moe_lower"].rearrange("a b -> (a b)").partition_broadcast(128).rearrange(
                    "p (a b) -> p a b", a=G), a_w2)
                load(up_w, dr["moe_up"], a_w)
                load(down_w, dr["moe_down"], a_w)
                load(sh_up, dr["moe_shared_up"], a_w)
                t_w = load(sh_down, dr["moe_shared_down"], a_w)
                grid = lambda name, *shape: sb(st, name, [128, TT, *shape])
                score = grid("moe_score", E)[:, :, :]
                sfc = grid("moe_biased", E)[:, :, :]
                top = grid("moe_group_top", G, 8)
                gs = grid("moe_group_score", G)[:, :, :]
                cmp_, eq = grid("moe_cmp", G, G)[:, :, :, :], grid("moe_eq", G, G)[:, :, :, :]
                keep = grid("moe_group_keep", G)[:, :, :]
                m8 = grid("moe_top8", 8)
                rep = grid("moe_replaced", E)
                tot = sb(st, "moe_total", [128, 2, TT])
                wide = sb(st, "moe_expert_rows", [E, E * 64])[:, :]
                cp(wide.rearrange("p (e i) -> p e i", e=E), spread(ident[0:E, 0:E], 64), lane=DVE)
                combT = sb(st, "moe_combine_rows", [E, T])[:, :]
                layernorm(x, xn)
                t = to_tokens(xn, rw, E, 7, now() + [t_r])
                t = act(score, psum[:, 7, 0:TT * E].rearrange("p (t e) -> p t e", t=TT), ACT.Sigmoid, after=[t])
                t = tt(sfc, score, rb.unsqueeze(1).broadcast_to([128, TT, E]), ALU.add, [t, t_r])
                for i in range(TT):
                    for g in range(G):
                        t1 = max8(top[:, i, g, :], sfc[:, i, g * 8:g * 8 + 8], [t])
                t = tt(gs, top[:, :, :, 0], top[:, :, :, 1], ALU.add, [t1])
                other = gs.unsqueeze(2).broadcast_to([128, TT, G, G])
                mine = gs.unsqueeze(3).broadcast_to([128, TT, G, G])
                t1 = tt(cmp_, other, mine, ALU.is_gt, [t])
                t2 = tt(eq, other, mine, ALU.is_equal, [t])
                for i in range(TT):
                    t3 = tt(eq[:, i, :, :], eq[:, i, :, :], lower, ALU.mult, [t2])
                t = tt(cmp_, cmp_, eq, ALU.add, [t1, t3])
                t = red(gs, cmp_, ALU.add, after=[t])
                t = ts(keep, gs, float(TOPG), None, ALU.is_lt, after=[t])
                sfg = sfc.rearrange("p t (g k) -> p (t g) k", g=G)
                t = tt(sfg, sfg, spread(keep.rearrange("p t g -> p (t g)"), E // G), ALU.mult, [t])
                for i in range(TT):
                    t1 = max8(m8[:, i, :], sfc[:, i, :], [t])
                    t1 = replace8(rep[:, i, :], m8[:, i, :], sfc[:, i, :], [t1])
                t = tt(sfc, rep[:, :, :], sfc, ALU.is_lt, [t1])
                t = tt(sfc, sfc, score, ALU.mult, [t])
                t = red(tot[:, 0, :], sfc, ALU.add, after=[t])
                t = ts(tot[:, 0, :], tot[:, 0, :], 1e-20, None, ALU.add, after=[t])
                t = recip(tot[:, 1, :], tot[:, 0, :], [t])
                t = tt(sfc, sfc, spread(tot[:, 1, :], E), ALU.mult, [t])
                t = ts(sfc, sfc, 2.5, None, ALU.mult, after=[t])
                to_rows(sfc, E, combT, [t])
                for lane in (PE,):
                    lane.wait([t_w])

                def relu2(banks, toks, g, h, r):
                    t = act(r.ap[:, 0, :], banks[0].ap[:, 0:HALF], ACT.Relu, after=(toks[0],) + tuple(r.free))
                    banks[0].free = (t,)
                    if g is None:
                        t = tt(h.ap[:, 0, :], r.ap[:, 0, :], r.ap[:, 0, :], ALU.mult, (t,) + tuple(h.free))
                    else:
                        t = tt(r.ap[:, 1, :], r.ap[:, 0, :], g.ap, ALU.mult, (t,) + tuple(g.ready))
                        g.free = (t,)
                        t = tt(h.ap[:, 0, :], r.ap[:, 1, :], r.ap[:, 0, :], ALU.mult, (t,) + tuple(h.free))
                    r.free = (t,)
                    return (t,)

                items = [dict(c=c, ups=[up_w[:, p * 128:(p + 1) * 128]], downs=[down_w[:, p, :]], gate=p, activate=relu2)
                         for p in range(E // 2) for c in range(2)]
                items += [dict(c=c, ups=[sh_up[:, p * 128:(p + 1) * 128]], downs=[sh_down[:, p, :]], gate=None,
                               activate=relu2) for p in range(2) for c in range(2)]
                last = experts(st, items, lambda p, c: (wide[:, p * 128:(p + 1) * 128], halves(combT)[c]))
                for c in range(2):
                    tt(halves(x)[c], bank[c].ap[:, 0:HALF], halves(x)[c], ALU.add, [last[c]])
            fence()

        HD1 = 64

        def head_buffers(st):
            return [sb(st, f"by_head{i}", [HD1, H, 128])[:, :, :] for i in range(4)]

        def fetch_heads_of(names, bufs, arr):
            after = again(arr)
            for name, buf in zip(names, bufs):
                t = load(buf, dr[name], arr, after)
            return t

        def fold_tables(bufs, tables, arrived):
            for k, table in enumerate(tables):
                fold_heads(bufs[2 * k], bufs[2 * k + 1], table, now() + [arrived])

        def pair_queries(slots, fold, src, ring):
            chunk_ = scale_queries(fold, src, ring, now())

            def chunk(pair, g):
                s = slots[pair % 2]
                t = chunk_(pair, s, g)
                s.ready = (t,) if g == 0 else s.ready + (t,)

            def get(b):
                s = slots[(b // 2) % 2]
                return s.ap[:, b % 2, :, :].rearrange("p h q -> p (h q)"), s.ready, s
            return chunk, get

        if FIRST <= 2 <= LAST:
            with ExitStack() as st:
                bo = sb(st, "l1_bias", [128, 2 + 8 + 1])
                a_h = arrival("l1_heads_arrived")
                by_head = head_buffers(st)
                t_h = fetch_heads_of(["l1_q1", "l1_k1", "l1_v1", "l1_o1"], by_head, a_h)
                t_b = load(bo[:, :], dr["l1_bias"], a_w)
                w1 = sb(st, "l1_ff1", [128, 8 * 128])[:, :]
                w2 = sb(st, "l1_ff2", [128, 4, 128])[:, :, :]
                load(w1, dr["l1_ff1"], a_w)
                t_w = load(w2, dr["l1_ff2"], a_w)
                layernorm(x, z)
                for lane in (PE, DVE, SC):
                    lane.wait([t_w])
                q_fold = sb(st, "l1_q_fold", [128, H, 128])[:, :, :]
                o_fold = sb(st, "l1_o_fold", [128, H, 128])[:, :, :]
                q_slots = [Slot(sb(st, f"l1_q{i}", [128, 2, H, S])) for i in range(2)]
                for s in q_slots:
                    s.scale = 1.0 / np.sqrt(HD1)
                with ExitStack() as s2:
                    fold_tables(by_head, [q_fold, o_fold], t_h)
                    t_h = fetch_heads_of(["l1_q2", "l1_k2", "l1_v2", "l1_o2"], by_head, a_h)
                    layernorm(z, xn, per_batch=adaln(3 * NL))
                    chunk, get = pair_queries(q_slots, q_fold, xn, Ring([bank[6]]))

                    def query(b):
                        if b % 2 == 0:
                            for g in range(4):
                                chunk(b // 2, g)
                        return get(b)
                    self_attention(s2, query, xn, xn, Slot(o_fold), z, bias_col=bo[:, 0:1])
                fence()
                with ExitStack() as s2:
                    fold_tables(by_head, [q_fold, o_fold], t_h)
                    layernorm(z, xn, per_batch=adaln(3 * NL + 1))
                    arena = sb(s2, "l1_arena", [128, 2 * L + 2 * KT * 128])[:, :]
                    bufs = cross_buffers(s2, arena, KT, (3, 4, 5))
                    for bk in bank:
                        bk.free = tuple(now())
                    for s in q_slots:
                        s.free = tuple(now())
                    ctx_t, fetch_t = streamed(s2, "ctx_t", [128, L], lambda b: dr["ctxT"][b])
                    ctx_v, fetch_v = streamed(s2, "ctx_v", [KN, KT, 128], lambda b: dr["ctxV"][b])
                    chunk, get = pair_queries(q_slots, q_fold, xn, bufs["t_ring"])
                    fetch_t(0)
                    fetch_v(0)
                    for g in range(4):
                        chunk(0, g)
                    part = [sb(s2, f"stat_part{i}", [KN, KT, 6]) for i in range(2)]
                    both = sb(s2, "stat_mean_var", [KN, B, KT, 2])
                    part_read = {}

                    def statistics(b, r):
                        if r == R - 1:
                            return
                        s = ctx_v[b % 2]
                        for k in (2 * r, 2 * r + 1):
                            t = bn_stats(part[b % 2][:, k, :], s.ap[:, k, :],
                                         tuple(s.ready) + ((part_read[b - 2],) if b >= 2 else ()))
                        stats_read[b] = t
                        for k in (2 * r, 2 * r + 1):
                            t = bn_aggr(both[:, b, k, :], part[b % 2][:, k, :], [t])
                        part_read[b] = t

                    stats_read, v_read = {}, [()]

                    def hooks(b, r):
                        if b > 0 and r == 0:
                            v_read[0] = (stats_read[b - 1],)
                        statistics(b, r)
                        if r == 1 and b + 1 < B:
                            fetch_t(b + 1)
                            s = ctx_v[(b + 1) % 2]
                            s.free = tuple(s.free) + tuple(v_read[0])
                            fetch_v(b + 1)
                        if b % 2 == 1 and b + 1 < B and 1 <= r <= 4:
                            chunk(b // 2 + 1, r - 1)

                    cross_attention(bufs, [500] * 3, hooks, get,
                                    lambda b: (ctx_t[b % 2].ap, ctx_t[b % 2].ready, ctx_t[b % 2]),
                                    lambda b: (ctx_v[b % 2].ap, ctx_v[b % 2].ready, ctx_v[b % 2]),
                                    o_fold, z, bias_col=bo[:, 1:2])
                    t = act(c_rstd[:, :, :], both[:, :, :, 1], ACT.Sqrt, bias=eps_col[0:KN, :], after=now())
                    recip(c_rstd[:, :, :], c_rstd[:, :, :], [t])
                    cp(c_mean[:, :, :], both[:, :, :, 0], now())
                fence()
                with ExitStack() as s2:
                    layernorm(z, xn, per_batch=adaln(3 * NL + 2))
                    hid = sb(s2, "l1_hidden", [128, 4, T])
                    gate = sb(s2, "l1_gate", [128, 4, T])
                    after = now()
                    ready, freed = [], []
                    for f in range(4):
                        bks = (0, 1, 2, 3) if f % 2 == 0 else (4, 5, 6, 7)
                        aft = after + freed[-2:] if f < 2 else after + freed[2 * (f - 2):2 * (f - 1)]
                        tg = linear([(w1[:, (4 + f) * 128:(5 + f) * 128], xn)], bks[0:2], aft)
                        ta = linear([(w1[:, f * 128:(f + 1) * 128], xn)], bks[2:4], aft)
                        for c in range(2):
                            g = halves(gate[:, f, :])[c]
                            t = act(g, psum[:, bks[c], 0:HALF], ACT.Gelu, bias=bo[:, 6 + f:7 + f], after=[tg[c]] + after)
                            t = stt(halves(hid[:, f, :])[c], psum[:, bks[2 + c], 0:HALF], bo[:, 2 + f:3 + f], g, ALU.add,
                                    ALU.mult, [t, ta[c]])
                            freed.append(t)
                    t = linear([(w2[:, f, :], hid[:, f, :]) for f in range(4)], (0, 1), now())
                    for c in range(2):
                        stt(halves(z)[c], psum[:, c, 0:HALF], bo[:, 10:11], halves(z)[c], ALU.add, ALU.add, [t[c]])
            tt(x, x, z, ALU.add, now())
            fence()

        if FIRST <= 3 <= LAST:
            E, CAP = 8, T // 8
            with ExitStack() as st:
                up_w = sb(st, "ec_up", [128, E * 256])[:, :]
                down_w = sb(st, "ec_down", [128, E * 2, 128])[:, :, :]
                wg = sb(st, "ec_gate_w", [128, E])[:, :]
                down_count = sb(st, "ec_index_down", [128, E])[:, :]
                load(wg, dr["ec_gate"], a_w2)
                t_r = load(down_count, dr["index_down"].partition_broadcast(128), a_w2)
                load(up_w, dr["ec_up"], a_w)
                t_w = load(down_w, dr["ec_down"], a_w)
                grid = lambda name, *shape: sb(st, name, [128, TT, *shape])
                probs, sel_t, val, cand, onehot = (grid(f"ec_{n}", E)[:, :, :] for n in
                                                   ("probs", "chosen", "value", "candidate", "expert"))
                tok = sb(st, "ec_token", [128, 3, TT])
                rows = [sb(st, f"ec_rows{i}", [E, T])[:, :] for i in range(2)]
                m8 = sb(st, "ec_top8", [E, 8])[:, :]
                gate_rows = sb(st, "ec_gate_rows", [E, T])[:, :]
                layernorm(x, xn)
                t = to_tokens(xn, wg, E, 7, now() + [t_r])
                lg = psum[:, 7, 0:TT * E].rearrange("p (t e) -> p t e", t=TT)
                t1 = red(tok[:, 0, :], lg, ALU.max, after=[t])
                t = tt(probs, lg, spread(tok[:, 0, :], E), ALU.subtract, [t1])
                t = act(probs, probs, ACT.Exp, after=[t])
                t = red(tok[:, 0, :], probs, ALU.add, after=[t])
                t = recip(tok[:, 1, :], tok[:, 0, :], [t])
                t = tt(probs, probs, spread(tok[:, 1, :], E), ALU.mult, [t])
                t = to_rows(probs, E, rows[0], [t])
                src = rows[0]
                orig = sb(st, "ec_rows_kept", [E, T])[:, :]
                t = [cp(orig, rows[0], t)]
                for k in range(CAP // 8):
                    t = [max8(m8, src, t)]
                    d = rows[(k + 1) % 2]
                    t = [replace8(d, m8, src, t)]
                    src = d
                t = tt(orig, src, orig, ALU.not_equal, t)
                for i in range(TT):
                    t1 = tr(psum[:, 6, i * E:(i + 1) * E], orig[:, i * 128:(i + 1) * 128], [t])
                t = cp(sel_t, psum[:, 6, 0:TT * E].rearrange("p (t e) -> p t e", t=TT), [t1])
                t1 = red(tok[:, 2, :], sel_t, ALU.max, after=[t])
                t = ts(val, sel_t, -LOW, LOW, ALU.mult, ALU.add, after=[t])
                t = tt(val, val, spread(tok[:, 2, :], E), ALU.mult, [t, t1])
                t = tt(val, val, probs, ALU.add, [t])
                t = rank_first(onehot, val, (tok[:, 0, :], cand), down_count, E, [t])
                t = tt(onehot, onehot, probs, ALU.mult, [t])
                to_rows(onehot, E, gate_rows, [t])
                PE.wait([t_w])

                def gelu_gated(banks, toks, g, h, r):
                    outs = []
                    for k in range(2):
                        t = act(r.ap[:, k, :], banks[k].ap[:, 0:HALF], ACT.Gelu, after=(toks[k],) + tuple(r.free))
                        banks[k].free = (t,)
                        t = tt(h.ap[:, k, :], r.ap[:, k, :], g.ap, ALU.mult, (t,) + tuple(h.free) + tuple(g.ready))
                        outs.append(t)
                    g.free, r.free = (t,), (t,)
                    return tuple(outs)

                items = [dict(c=c, ups=[up_w[:, (2 * e + f) * 128:(2 * e + f + 1) * 128] for f in range(2)],
                              downs=[down_w[:, 2 * e + f, :] for f in range(2)], gate=e, activate=gelu_gated)
                         for e in range(E) for c in range(2)]
                last = experts(st, items, lambda g, c: (ident[0:E, g:g + 1].broadcast_to([E, 128]),
                                                        halves(gate_rows)[c]))
                for c in range(2):
                    tt(halves(x)[c], bank[c].ap[:, 0:HALF], halves(x)[c], ALU.add, [last[c]])
            fence()

        if LAST >= 4 and 3 <= FIRST <= 6:
            with ExitStack() as st:
                slots, fetch = streamed(st, "ctx_v", [KN, KT, 128], lambda b: dr["ctxV"][b])
                part = [sb(st, f"stat_part{i}", [KN, KT, 6]) for i in range(2)]
                both = sb(st, "stat_mean_var", [KN, B, KT, 2])
                fetch(0)
                for b in range(B):
                    if b + 1 < B:
                        fetch(b + 1)
                    s = slots[b % 2]
                    for k in range(KT):
                        t = bn_stats(part[b % 2][:, k, :], s.ap[:, k, :],
                                     tuple(s.ready) + ((t,) if b >= 2 and k == 0 else ()))
                    s.free = (t,)
                    for k in range(KT):
                        t = bn_aggr(both[:, b, k, :], part[b % 2][:, k, :], [t])
                t = act(c_rstd[:, :, :], both[:, :, :, 1], ACT.Sqrt, bias=eps_col[0:KN, :], after=[t])
                t = recip(c_rstd[:, :, :], c_rstd[:, :, :], [t])
                cp(c_mean[:, :, :], both[:, :, :, 0], [t])
            fence()

        def normalise_context(b, buf, w_row, b_row, after, lane=PL, tiles=(0, KT)):
            lo, hi = tiles
            for k in range(lo, hi):
                t = ts(buf[:, k, :], buf[:, k, :], c_mean[:, b, k:k + 1], c_rstd[:, b, k:k + 1], ALU.subtract, ALU.mult,
                       after=after)
            part = buf[:, lo:hi, :]
            t = tt(part, part, w_row.unsqueeze(1).broadcast_to([KN, hi - lo, 128]), ALU.mult, [t], lane=lane)
            return tt(part, part, b_row.unsqueeze(1).broadcast_to([KN, hi - lo, 128]), ALU.add, [t], lane=PL)

        if FIRST <= 4 <= LAST:
            with ExitStack() as st:
                aff = sb(st, "l2_affine", [128, 2])
                w_row = sb(st, "l2_ctx_w", [KN, 128])[:, :]
                b_row = sb(st, "l2_ctx_b", [KN, 128])[:, :]
                cond1 = sb(st, "cond_plus_1", [128, B])[:, :]
                a_h = arrival("l2_heads_arrived")
                load(aff[:, :], dr["l2_affine"], a_w)
                load(w_row, dr["l2_ln1_w"].partition_broadcast(KN), a_w)
                t_w = load(b_row, dr["l2_ln1_b"].partition_broadcast(KN), a_w)
                DVE.wait([t_w])
                PL.wait([t_w])
                ts(cond1, cond, 1.0, None, ALU.add)
                q_fold = sb(st, "l2_q_fold", [128, H, 128])[:, :, :]
                o_fold = sb(st, "l2_o_fold", [128, H, 128])[:, :, :]
                with ExitStack() as s3:
                    by_head = head_buffers(s3)
                    t_h = fetch_heads_of(["l2_q", "l2_k", "l2_v", "l2_o"], by_head, a_h)
                    layernorm(x, xn)
                    fold_tables(by_head, [q_fold, o_fold], t_h)
                layernorm(xn, xn, per_feature=(aff[:, 0:1], aff[:, 1:2]))
                v = xn.rearrange("p (b s) -> p b s", s=S)
                t = tt(v, v, spread(cond1, S), ALU.mult, now())
                t = tt(v, v, spread(cond, S), ALU.add, [t])
                lat = sb(st, "l2_latents", [S, B, 128])[:, :, :]
                for g in range(4):
                    for k in range(4):
                        t1 = tr(psum[0:S, g, k * 128:(k + 1) * 128], xn[:, (4 * g + k) * S:(4 * g + k + 1) * S], [t])
                    cp(lat[:, 4 * g:4 * g + 4, :], psum[0:S, g, :].rearrange("p (k d) -> p k d", k=4), [t1])
                fence()
                arena = sb(st, "l2_arena", [128, 2 * (L + S) + 2 * (KT + 1) * 128])[:, :]
                bufs = cross_buffers(st, arena, KT + 1, (4, 5))
                q_slots = [Slot(sb(st, f"l2_q{i}", [128, 2, H, S])) for i in range(2)]
                for s in q_slots:
                    s.scale = 1.0 / np.sqrt(HD1)
                for bk in bank:
                    bk.free = tuple(now())
                ctx_v, fetch_v = streamed(st, "ctx_v", [KN, KT, 128], lambda b: dr["ctxV"][b])
                k_slots = [Slot(sb(st, f"l2_keys{i}", [128, L + S])[:, :]) for i in range(2)]
                chunk, get = pair_queries(q_slots, q_fold, xn, bufs["t_ring"])

                def norm(b, c):
                    s = ctx_v[b % 2]
                    s.ready = (normalise_context(b, s.ap[:, :, :], w_row, b_row, s.ready,
                                                 tiles=(4 * c, 4 * c + 4)),)

                def key_chunk(b, c):
                    s, k_ = ctx_v[b % 2], k_slots[b % 2]
                    bk = bufs["t_ring"].next()
                    for k in range(4):
                        t = tr(bk.ap[:, k * KN:(k + 1) * KN], s.ap[:, 4 * c + k, :], tuple(s.ready) + tuple(bk.free))
                    e = cp(k_.ap[:, c * 500:(c + 1) * 500], bk.ap[:, 0:500], (t,) + tuple(k_.free), lane=(SC, DVE, SC)[c])
                    bk.free = (e,)
                    if c == 0:
                        k_.ready = (e, cp(k_.ap[:, L:L + S], xn[:, b * S:(b + 1) * S], tuple(k_.free), lane=PL))
                    else:
                        k_.ready += (e,)

                fetch_v(0)
                for c in range(3):
                    norm(0, c)
                    key_chunk(0, c)
                for g in range(4):
                    chunk(0, g)

                def hooks(b, r):
                    if b + 1 < B:
                        if r == 1:
                            fetch_v(b + 1)
                        if r in (4, 5, 6):
                            key_chunk(b + 1, r - 4)
                        if r in (2, 3, 4):
                            norm(b + 1, r - 2)
                        if b % 2 == 1 and r < 4:
                            chunk(b // 2 + 1, r)

                cross_attention(bufs, [(L + S) // 4] * 4, hooks, get,
                                lambda b: (k_slots[b % 2].ap, k_slots[b % 2].ready, k_slots[b % 2]),
                                lambda b: (ctx_v[b % 2].ap, ctx_v[b % 2].ready, ctx_v[b % 2]),
                                o_fold, x, own_values=lat)
            fence()

        if FIRST <= 5 <= LAST:
            E = 8
            with ExitStack() as st:
                w1 = sb(st, "sm_w1", [128, E * 512])[:, :]
                w3 = sb(st, "sm_w3", [128, E * 512])[:, :]
                w2 = sb(st, "sm_w2", [128, E * 4, 128])[:, :, :]
                wg = sb(st, "sm_gate_w", [128, E])[:, :]
                down_count = sb(st, "sm_index_down", [128, E])[:, :]
                load(wg, dr["sm_gate"], a_w2)
                t_r = load(down_count, dr["index_down"].partition_broadcast(128), a_w2)
                load(w1, dr["sm_w1"], a_w)
                load(w3, dr["sm_w3"], a_w)
                t_w = load(w2, dr["sm_w2"], a_w)
                grid = lambda name: sb(st, name, [128, TT, E])[:, :, :]
                sco, mag, fac, cand, hot, s2_, ex, gate = (grid(f"sm_{n}") for n in (
                    "scores", "magnitude", "factor", "candidate", "onehot", "rest", "exp", "gate"))
                mx, mx2, sm_, inv = (sb(st, f"sm_token_{n}", [128, TT])[:, :] for n in ("max", "tmp", "sum", "inv"))
                gate_rows = sb(st, "sm_gate_rows", [E, T])[:, :]
                layernorm(x, xn)
                t = to_tokens(xn, wg, E, 7, now() + [t_r])
                t = cp(sco, psum[:, 7, 0:TT * E].rearrange("p (t e) -> p t e", t=TT), [t])
                t = act(mag, sco, ACT.Abs, after=[t])
                src = sco
                for k in range(2):
                    t = red(mx, src, ALU.max, after=[t])
                    t = rank_first(hot, src, (mx2, cand), down_count, E, [t])
                    t = tt(fac, mag, spread(mx, E), ALU.max, [t])
                    t = ts(fac, fac, 0.02, None, ALU.mult, after=[t])
                    t = tt(ex, spread(mx, E), sco, ALU.subtract, [t])
                    t = tt(fac, ex, fac, ALU.is_gt, [t])
                    t = ts(fac, fac, -1.0, 1.0, ALU.mult, ALU.add, after=[t])
                    t = tt(ex, src, spread(mx, E), ALU.subtract, [t])
                    t = act(ex, ex, ACT.Exp, after=[t])
                    t = tt(ex, ex, fac, ALU.mult, [t])
                    t = red(sm_, ex, ALU.add, after=[t])
                    t = recip(inv, sm_, [t])
                    if k == 0:
                        t = tt(gate, hot, spread(inv, E), ALU.mult, [t])
                        t = stt(s2_, hot, LOW, sco, ALU.mult, ALU.add, [t])
                        src = s2_
                    else:
                        t = tt(hot, hot, spread(inv, E), ALU.mult, [t])
                        t = tt(gate, gate, hot, ALU.add, [t])
                to_rows(gate, E, gate_rows, [t])
                PE.wait([t_w])

                def silu_gated(banks, toks, g, h, r):
                    t = act(r.ap[:, 0, :], banks[0].ap[:, 0:HALF], ACT.Silu, after=(toks[0],) + tuple(r.free))
                    banks[0].free = (t,)
                    t = tt(r.ap[:, 1, :], r.ap[:, 0, :], banks[1].ap[:, 0:HALF], ALU.mult, (t, toks[1]))
                    banks[1].free = (t,)
                    t = tt(h.ap[:, 0, :], r.ap[:, 1, :], g.ap, ALU.mult, (t,) + tuple(h.free) + tuple(g.ready))
                    g.free, r.free = (t,), (t,)
                    return (t,)

                items = [dict(c=c, ups=[w1[:, (4 * e + f) * 128:(4 * e + f + 1) * 128],
                                        w3[:, (4 * e + f) * 128:(4 * e + f + 1) * 128]],
                              downs=[w2[:, 4 * e + f, :]], gate=e, activate=silu_gated)
                         for e in range(E) for c in range(2) for f in range(4)]
                last = experts(st, items, lambda g, c: (ident[0:E, g:g + 1].broadcast_to([E, 128]),
                                                        halves(gate_rows)[c]))
                for c in range(2):
                    tt(halves(x)[c], bank[c].ap[:, 0:HALF], halves(x)[c], ALU.add, [last[c]])
            fence()

        if FIRST <= 6 <= LAST:
            with ExitStack() as st:
                xin = sb(st, "slot_context", [KN, B, KT, 129])
                wts = sb(st, "slot_w", [128, 6, 128])
                colv = sb(st, "slot_cols", [128, 14])
                w_row = sb(st, "slot_ctx_w", [KN, 128])[:, :]
                b_row = sb(st, "slot_ctx_b", [KN, 128])[:, :]
                load(wts[:, :, :], dr["slot_w"], a_w)
                load(colv[:, :], dr["slot_cols"], a_w)
                load(w_row, dr["slot_lnkv_g"].partition_broadcast(KN), a_w)
                t_w = load(b_row, dr["slot_lnkv_b"].partition_broadcast(KN), a_w)
                for lane in (PE, DVE, SC, PL):
                    lane.wait([t_w])
                cq = {n: colv[:, i:i + 1] for i, n in enumerate((
                    "mu", "logsig", "lnq_g", "lnq_b", "lnm_g", "lnm_b", "lnp_g", "lnp_b", "bk", "bv", "bq", "bu", "b1",
                    "b2"))}
                wk_t, wq, wv, wu, w1, w2 = (wts[:, i, :] for i in range(6))
                sig = sb(st, "slot_sigma", [128, 1])[:, :]
                bk_wide = cq["bk"].broadcast_to([128, 128])
                t_ones = memset(xin[:, :, :, 128:129], 1.0)
                PE.wait([t_ones])
                act(sig, cq["logsig"], ACT.Exp)
                ring4 = [arrival(f"slot_ctx{i}_arrived") for i in range(4)]
                ready, landed = {}, {}
                for b in range(B):
                    a = ring4[b % 4]
                    landed[b] = load(xin[:, b, :, 0:128], dr["ctxV"][b], a, [(a, a.count)] if a.count else [])

                def norm_ctx(b):
                    ready[b] = normalise_context(b, xin[:, b, :, 0:128], w_row, b_row, [landed[b]], lane=DVE)

                for b in range(3):
                    norm_ctx(b)
                layernorm(x, z, per_feature=(sig, cq["mu"]))
                big = lambda n: sb(st, f"slot_{n}", [128, T])[:, :]
                qT, q2, cbk, upd = big("q"), big("q_folded"), big("bk_q"), big("update")
                x_t = [Slot(sb(st, f"slot_ctxT{i}", [128, L])[:, :]) for i in range(2)]
                at_ = [Slot(sb(st, f"slot_attn{i}", [KN, KT, S])[:, :, :]) for i in range(4)]
                stat = [sb(st, f"slot_stat{i}", [KN, 3, KT]) for i in range(4)]
                rden = [sb(st, f"slot_rden{i}", [S, 1])[:, :] for i in range(2)]
                normed = Ring([Slot(sb(st, f"slot_normed{i}", [S, 128])[:, :]) for i in range(2)])
                root = float(np.sqrt(np.float32(D)))

                def dense(dst, w, src, ready, banks, bias, plus=None, func=None):
                    done = []
                    for c in range(2):
                        o, i = halves(dst)[c], psum[:, banks[c], 0:HALF]
                        t = mm(i, w, halves(src)[c], after=ready[c])
                        if func is not None:
                            t = act(o, i, func, bias=bias, after=[t] + ready[c])
                        elif plus is not None:
                            t = stt(o, i, bias, halves(plus)[c], ALU.add, ALU.add, [t] + ready[c])
                        elif bias is not None:
                            t = ts(o, i, bias, None, ALU.add, after=[t] + ready[c])
                        else:
                            t = cp(o, i, [t] + ready[c], lane=(DVE, SC)[c])
                        done.append(ready[c] + [t])
                    return done

                for it in range(3):
                    before = now()
                    t = layernorm(z, xn, per_feature=(cq["lnq_g"], cq["lnq_b"]))
                    t = dense(qT, wq, xn, [before + [t[0]], before + [t[1]]], (5, 6), cq["bq"])
                    dense(q2, wk_t, qT, t, (7, 0), None)
                    dense(cbk, bk_wide, qT, t, (1, 2), None)
                    start = tuple(now())
                    for bk in bank:
                        bk.free = start
                    updated = {}

                    def turn_ctx(b):
                        s = x_t[b % 2]
                        toks = []
                        for g in range(3):
                            bk = bank[g]
                            for k in range(4):
                                t = tr(bk.ap[:, k * KN:(k + 1) * KN], xin[:, b, 4 * g + k, 0:128], tuple(bk.free) + (ready[b],))
                            e = cp(s.ap[:, g * 500:(g + 1) * 500], bk.ap[:, 0:500], (t,) + tuple(s.free),
                                   lane=(SC, DVE, SC)[g])
                            bk.free = (e,)
                            toks.append(e)
                        s.ready = tuple(toks)

                    def slot_scores(b):
                        s, a, sp = x_t[b % 2], at_[b % 4], stat[b % 4]
                        for k in range(KT):
                            bk = bank[3 + k // 6]
                            t = mm(bk.ap[0:KN, (k % 6) * S:(k % 6 + 1) * S], s.ap[:, k * KN:(k + 1) * KN],
                                   q2[:, b * S:(b + 1) * S], after=tuple(s.ready) + tuple(bk.free))
                        s.free = (t,)
                        lg = psum[0:KN, 3:5, 0:6 * S].rearrange("p c (k s) -> p c k s", s=S)
                        av = a.ap.rearrange("p (c k) s -> p c k s", c=2)
                        cb = cbk[0:KN, b * S:(b + 1) * S].unsqueeze(1).unsqueeze(1).broadcast_to([KN, 2, 6, S])
                        t = tt(av, lg, cb, ALU.add, (t,) + tuple(a.free))
                        bank[3].free = bank[4].free = (t,)
                        t = red(sp[:, 0, :], a.ap, ALU.max, after=(t,))
                        t = tt(a.ap, a.ap, spread(sp[:, 0, :], S), ALU.subtract, (t,))
                        a.ready = (act(a.ap, a.ap, ACT.Exp, scale=root, after=(t,)),)

                    def slot_normalise(b):
                        a, sp = at_[b % 4], stat[b % 4]
                        t = red(sp[:, 1, :], a.ap, ALU.add, after=a.ready)
                        t = recip(sp[:, 2, :], sp[:, 1, :], (t,))
                        t = tt(a.ap, a.ap, spread(sp[:, 2, :], S), ALU.mult, (t,))
                        t = ts(a.ap, a.ap, 1e-8, None, ALU.add, after=(t,))
                        a.ready = (t,)

                    def slot_update(b):
                        a = at_[b % 4]
                        for k in range(KT):
                            t = mm(bank[5].ap[0:S, 0:129], a.ap[:, k, :], xin[:, b, k, :], k == 0, k == KT - 1,
                                   tuple(a.ready) + tuple(bank[5].free))
                        a.free = (t,)
                        w, r = normed.next(), rden[b % 2]
                        t = recip(r, bank[5].ap[0:S, 128:129], (t,) + tuple(w.free))
                        t = ts(w.ap, bank[5].ap[0:S, 0:128], r, None, ALU.mult, after=(t,))
                        bank[5].free = w.ready = (t,)
                        updated[b] = w

                    def turn_update(b):
                        w = updated.pop(b)
                        t = tr(bank[6].ap[:, 0:S], w.ap, tuple(w.ready) + tuple(bank[6].free))
                        w.free = (t,)
                        bank[6].free = (cp(upd[:, b * S:(b + 1) * S], bank[6].ap[:, 0:S], (t,), lane=SC),)

                    for i in range(B + 4):
                        if i < B:
                            turn_ctx(i)
                        if it == 0 and 3 <= i + 3 < B:
                            norm_ctx(i + 3)
                        if 1 <= i <= B:
                            slot_scores(i - 1)
                        if i >= 4:
                            turn_update(i - 4)
                        if 3 <= i < B + 3:
                            slot_update(i - 3)
                        if 2 <= i <= B + 1:
                            slot_normalise(i - 2)
                    t = dense(qT, wv, upd, [now(), now()], (5, 6), cq["bv"])
                    dense(z, wu, qT, t, (7, 0), cq["bu"], plus=z)
                    before = now()
                    t = layernorm(z, xn, per_feature=(cq["lnm_g"], cq["lnm_b"]))
                    t = dense(qT, w1, xn, [before + [t[0]], before + [t[1]]], (5, 6), cq["b1"], func=ACT.Gelu)
                    dense(z, w2, qT, t, (7, 0), cq["b2"], plus=z)
                    v = z.rearrange("p (b s) -> p b s", s=S)
                    tt(v, v, spread(cond, S), ALU.add, now())
                    layernorm(z, z, per_feature=(cq["lnp_g"], cq["lnp_b"]))
                tt(x, x, z, ALU.add, now())
            fence()

        if FIRST <= 7 <= LAST:
            DEPTH, LEAVES = 4, 16
            NODES = LEAVES - 1
            with ExitStack() as st:
                w1 = sb(st, "fff_w1", [128, 3, LEAVES * 64])
                w2 = sb(st, "fff_w2", [128, 3, LEAVES // 2, 128])
                b1 = sb(st, "fff_b1", [128, 3, LEAVES // 2])
                b2 = sb(st, "fff_b2", [LEAVES, 3, 128])
                nw = sb(st, "fff_node_w", [128, 3 * NODES])[:, :]
                nb = sb(st, "fff_node_b", [128, 3 * NODES])[:, :]
                load(nw, dr["fff_node_w"], a_w2)
                t_r = load(nb, dr["fff_node_b"].partition_broadcast(128), a_w2)
                load(w1[:, :, :], dr["fff_w1"], a_w)
                load(w2[:, :, :, :], dr["fff_w2"], a_w)
                load(b1[:, :, :], dr["fff_b1"], a_w)
                t_w = load(b2[:, :, :], dr["fff_b2"], a_w)
                layernorm(x, xn)
                bit = sb(st, "fff_bit", [128, TT, 3 * NODES])
                path = [sb(st, f"fff_path{d}", [128, TT, 3, 2 ** d]) for d in range(DEPTH + 1)]
                t = to_tokens(xn, nw, 3 * NODES, 7, now() + [t_r])
                t = tt(bit[:, :, :], psum[:, 7, 0:TT * 3 * NODES].rearrange("p (t n) -> p t n", t=TT),
                       nb.unsqueeze(1).broadcast_to([128, TT, 3 * NODES]), ALU.add, [t])
                t = ts(bit[:, :, :], bit[:, :, :], 0.0, None, ALU.is_ge, after=[t])
                t0 = memset(path[0][:, :, :, :], 1.0, lane=DVE)
                bits = bit[:, :, :].rearrange("p t (j n) -> p t j n", j=3)
                t = [t, t0]
                for d in range(DEPTH):
                    w = 2 ** d
                    here = bits[:, :, :, w - 1:2 * w - 1]
                    nxt = path[d + 1][:, :, :, :].rearrange("p t j (n k) -> p t j n k", k=2)
                    for j in range(3):
                        t1 = tt(nxt[:, :, j, :, 1], path[d][:, :, j, :], here[:, :, j, :], ALU.mult, t)
                    for j in range(3):
                        t2 = tt(nxt[:, :, j, :, 0], path[d][:, :, j, :], nxt[:, :, j, :, 1], ALU.subtract, [t1])
                    t = [t2]
                wide = sb(st, "fff_leaf_cols", [LEAVES, LEAVES * 64])[:, :]
                cp(wide.rearrange("p (e i) -> p e i", e=LEAVES), spread(ident[0:LEAVES, 0:LEAVES], 64))
                rows = [sb(st, f"fff_leaf_rows{j}", [LEAVES, T])[:, :] for j in range(3)]
                for j in range(3):
                    t = to_rows(path[DEPTH][:, :, j, :], LEAVES, rows[j], now())
                PE.wait([t_w])
                SC.wait([t_w])
                res = [sb(st, f"fff_{n}", [128, T])[:, :] for n in "qkv"]
                for j in range(3):
                    with ExitStack() as s2:
                        def relu_gated(p):
                            def f(banks, toks, g, h, r):
                                t = act(r.ap[:, 0, :], banks[0].ap[:, 0:HALF], ACT.Relu, bias=b1[:, j, p:p + 1],
                                        after=(toks[0],) + tuple(r.free))
                                banks[0].free = (t,)
                                t = tt(h.ap[:, 0, :], r.ap[:, 0, :], g.ap, ALU.mult, (t,) + tuple(h.free) + tuple(g.ready))
                                g.free, r.free = (t,), (t,)
                                return (t,)
                            return f
                        items = [dict(c=c, ups=[w1[:, j, p * 128:(p + 1) * 128]], downs=[w2[:, j, p, :]], gate=p,
                                      activate=relu_gated(p)) for p in range(LEAVES // 2) for c in range(2)]
                        last = experts(s2, items, lambda p, c: (wide[:, p * 128:(p + 1) * 128],
                                                                halves(rows[j])[c]), extra=(b2[:, j, :], rows[j]))
                        for c in range(2):
                            cp(halves(res[j])[c], bank[c].ap[:, 0:HALF], [last[c]])
                    fence()
                q, k_, v_ = res
                p = sb(st, "fff_p", [S, B, S])[:, :, :]
                pt = sb(st, "fff_pt", [S, B, S])[:, :, :]
                vt = sb(st, "fff_v_tokens", [S, B, 128])[:, :, :]
                sst = sb(st, "fff_stat", [S, 3, B])
                for b in range(B):
                    c = slice(b * S, (b + 1) * S)
                    t = mm(psum[0:S, b // 8, (b % 8) * S:(b % 8 + 1) * S], q[:, c], k_[:, c])
                for b in range(B):
                    t1 = tr(psum[0:S, 4 + b // 4, (b % 4) * 128:(b % 4 + 1) * 128], v_[:, b * S:(b + 1) * S])
                sv = psum[0:S, 0:2, 0:HALF].rearrange("p c (b s) -> p c b s", s=S)
                t = red(sst[:, 0, :].rearrange("p (c b) -> p c b", c=2), sv, ALU.max, after=[t])
                for c in range(2):
                    t = tt(p[:, 8 * c:8 * c + 8, :], sv[:, c, :, :], spread(sst[:, 0, 8 * c:8 * c + 8], S), ALU.subtract, [t])
                t = act(p, p, ACT.Exp, scale=float(1.0 / np.sqrt(np.float32(D))), after=[t])
                t = red(sst[:, 1, :], p, ALU.add, after=[t])
                t = recip(sst[:, 2, :], sst[:, 1, :], [t])
                t = tt(p, p, spread(sst[:, 2, :], S), ALU.mult, [t])
                for b in range(B):
                    t2 = tr(psum[0:S, 2 + b // 8, (b % 8) * S:(b % 8 + 1) * S], p[:, b, :], [t])
                e1 = [cp(pt[:, 8 * c:8 * c + 8, :], psum[0:S, 2 + c, 0:HALF].rearrange("p (b s) -> p b s", s=S), [t2])
                      for c in range(2)]
                e1 += [cp(vt[:, 4 * g:4 * g + 4, :], psum[0:S, 4 + g, :].rearrange("p (b d) -> p b d", b=4), [t1], lane=SC)
                       for g in range(4)]
                for b in range(B):
                    t = mm(psum[:, b // 8, (b % 8) * S:(b % 8 + 1) * S], vt[:, b, :], pt[:, b, :], after=e1)
                for c in range(2):
                    tt(halves(x)[c], psum[:, c, 0:HALF], halves(x)[c], ALU.add, [t])
            fence()

        t = load(out, x, a_out, now())
        SY.wait([t])

        block = ctx.enter_context(nc.Block())

        @block.sync
        def _(e):
            SY.run(e)

        @block.tensor
        def _(e):
            PE.run(e)

        @block.vector
        def _(e):
            DVE.run(e)

        @block.scalar
        def _(e):
            SC.run(e)

        @block.gpsimd
        def _(e):
            PL.run(e)


PAIR_ORDER = np.arange(D).reshape(H // 2, 2, 2, D // H // 2).transpose(1, 3, 2, 0).reshape(D)


def rope_tables():
    half = D // H // 2
    inv = (1.0 / 10000.0 ** (np.arange(half, dtype=np.float32) / np.float32(half))).astype(np.float32)
    ang = np.arange(L, dtype=np.float32)[:, None] * inv
    c, s = np.cos(ang).T, np.sin(ang).T
    return (np.ascontiguousarray(np.tile(np.concatenate([c, c]), (H, 1))[PAIR_ORDER], dtype=np.float32),
            np.ascontiguousarray(np.tile(np.concatenate([-s, s]), (H, 1))[PAIR_ORDER], dtype=np.float32))


def layout(v):
    c = np.ascontiguousarray
    a = {}
    a["xT"] = c(v["x"].reshape(T, D).T)
    a["condT"] = c(v["cond_1024"].T)
    ctx = v["ctx_1024"]
    a["ctxT"] = c(ctx.transpose(0, 2, 1))
    a["ctxV"] = c(ctx.reshape(B, KT, KN, D).transpose(0, 2, 1, 3))
    a["src_mask"] = c(v["mask_BxS_bf0"]).reshape(T)
    a["ctx_mask"] = c(v["mask_BxS2_bf0"])
    ws, bs = [], []
    for i in range(NL):
        for n in ("n1", "n2", "n3"):
            ws.append(v[f"L0_xcond_{n}_w"][i].T)
            bs.append(v[f"L0_xcond_{n}_b"][i])
    for n in ("norm1", "norm2", "norm3"):
        ws.append(v[f"L1_xcond_{n}_w"])
        bs.append(v[f"L1_xcond_{n}_b"])
    a["adaln_w"] = c(np.concatenate(ws, axis=1))
    a["adaln_b"] = c(np.stack(bs).reshape(2 * NORMS, 128).T)
    a["rope_cos"], a["rope_sin"] = rope_tables()
    a["head_of_feature"] = (PAIR_ORDER[:, None] // 8 == np.arange(H)[None, :]).astype(np.float32)
    a["head_parity"] = ((PAIR_ORDER[:, None] // 8) % 2 == np.arange(2)[None, :]).astype(np.float32)
    lw, f2, hd, lb = [], [], [], []
    for i in range(NL):
        q, k, vv = (v["L0_xcond_qkv_w"][i][j * D:(j + 1) * D] for j in range(3))
        cq, ck = v["L0_xcond_cq_w"][i], v["L0_xcond_ck_w"][i]
        rows = [w[PAIR_ORDER] for w in (q, k, cq, ck)] + [v["L0_xcond_f1_w"][i]]
        lw.append(np.concatenate(rows).T.reshape(D, 8, D))
        f2.append(v["L0_xcond_f2_w"][i].T.reshape(4, 128, D).transpose(1, 0, 2))
        by_head = lambda m: np.pad(m.reshape(4, 4, 8, D).transpose(1, 2, 0, 3),
                                   ((0, 0), (0, 24), (0, 0), (0, 0))).reshape(128, 4, D)
        hd.append(np.stack([np.stack([by_head(m) for m in pair], axis=1) for pair in (
            (vv, v["L0_xcond_so_w"][i].T), (v["L0_xcond_cv_w"][i], v["L0_xcond_co_w"][i].T))]))
        lb.append(np.concatenate([v["L0_xcond_f1_b"][i], v["L0_xcond_f2_b"][i]]).reshape(5, 128).T)
    a["l0_w"], a["l0_f2"], a["l0_heads"] = c(np.stack(lw)), c(np.stack(f2)), c(np.stack(hd))
    a["l0_bias"] = c(np.stack(lb, axis=1))
    a["moe_router"] = c(v["L0_ffn_router_w"].T)
    a["moe_bias"] = c(v["L0_ffn_correction_bias"])
    a["moe_lower"] = (np.arange(8)[None, :] < np.arange(8)[:, None]).astype(np.float32)
    a["moe_up"] = c(v["L0_ffn_up_w"].transpose(1, 0, 2).reshape(D, -1))
    a["moe_down"] = c(v["L0_ffn_down_w"].reshape(32, 128, D).transpose(1, 0, 2))
    a["moe_shared_up"] = c(v["L0_ffn_shared_up_w"])
    a["moe_shared_down"] = c(v["L0_ffn_shared_down_w"].reshape(2, 128, D).transpose(1, 0, 2))
    head64 = lambda m: c(m.reshape(H, 64, D).transpose(1, 0, 2))
    for n in (1, 2):
        for k in "qkv":
            a[f"l1_{k}{n}"] = head64(v[f"L1_xcond_attn{n}_w{k}"].T)
        a[f"l1_o{n}"] = head64(v[f"L1_xcond_attn{n}_wo"])
    a["l1_ff1"] = c(v["L1_xcond_ff_w1"])
    a["l1_ff2"] = c(v["L1_xcond_ff_w2"].reshape(4, 128, D).transpose(1, 0, 2))
    a["l1_bias"] = c(np.concatenate([v["L1_xcond_attn1_bo"], v["L1_xcond_attn2_bo"], v["L1_xcond_ff_b1"],
                                     v["L1_xcond_ff_b2"]]).reshape(11, 128).T)
    a["ec_gate"] = c(v["L1_ffn_Wg"])
    a["ec_up"] = c(v["L1_ffn_W1"].transpose(1, 0, 2).reshape(D, -1))
    a["ec_down"] = c(v["L1_ffn_W2"].reshape(16, 128, D).transpose(1, 0, 2))
    a["index_down"] = np.arange(8, 0, -1).astype(np.float32)
    a["l2_affine"] = c(np.stack([v["L2_xcond_ln2_w"], v["L2_xcond_ln2_b"]], axis=1))
    a["l2_ln1_w"], a["l2_ln1_b"] = c(v["L2_xcond_ln1_w"]), c(v["L2_xcond_ln1_b"])
    a["l2_q"] = head64(v["L2_xcond_Wq"])
    a["l2_k"], a["l2_v"] = head64(v["L2_xcond_Wkv"][:H * 64]), head64(v["L2_xcond_Wkv"][H * 64:])
    a["l2_o"] = head64(v["L2_xcond_Wo"].T)
    a["sm_gate"] = c(v["L2_ffn_gate_w"].T)
    for k in ("w1", "w3"):
        a[f"sm_{k}"] = c(v[f"L2_ffn_{k}"].transpose(2, 0, 1).reshape(D, -1))
    a["sm_w2"] = c(v["L2_ffn_w2"].transpose(0, 2, 1).reshape(32, 128, D).transpose(1, 0, 2))
    w = {k: v[f"L3_xcond_{k}"] for k in ("wk", "wq", "wv", "wu", "w1", "w2")}
    a["slot_w"] = c(np.stack([w["wk"].T] + [w[k] for k in ("wq", "wv", "wu", "w1", "w2")], axis=1))
    a["slot_cols"] = c(np.stack([v[f"L3_xcond_{k}"].reshape(D) for k in (
        "q_mu", "q_logsig", "lnq_g", "lnq_b", "lnm_g", "lnm_b", "lnp_g", "lnp_b", "bk", "bv", "bq", "bu", "b1",
        "b2")], axis=1))
    a["slot_lnkv_g"], a["slot_lnkv_b"] = c(v["L3_xcond_lnkv_g"]), c(v["L3_xcond_lnkv_b"])
    three = lambda k: [v[f"L3_ffn_{j}_{k}"] for j in "qkv"]
    a["fff_node_w"] = c(np.concatenate(three("node_w")).T)
    a["fff_node_b"] = c(np.concatenate(three("node_b")))
    a["fff_w1"] = c(np.stack([m.transpose(1, 0, 2).reshape(D, -1) for m in three("w1")], axis=1))
    a["fff_w2"] = c(np.stack([m.reshape(8, 128, D).transpose(1, 0, 2) for m in three("w2")], axis=1))
    a["fff_b1"] = c(np.stack([m.reshape(8, 128).T for m in three("b1")], axis=1))
    a["fff_b2"] = c(np.stack(three("b2"), axis=1))
    return a


def kernel(**inputs):
    import concourse.bacc as bacc
    from concourse.bass_utils import run_bass_kernel_spmd

    arrays = layout({k: np.asarray(a) for k, a in inputs.items()})
    nc = bacc.Bacc("TRN2", target_bir_lowering=False, num_devices=1)
    dr = {n: nc.dram_tensor(f"in_{n}", a.shape, mybir.dt.from_np(a.dtype), kind="ExternalInput").ap()
          for n, a in arrays.items()}
    out = nc.dram_tensor("out_0", (D, T), F32, kind="ExternalOutput").ap()
    program(nc, dr, out)
    r = run_bass_kernel_spmd(nc, [{f"in_{n}": a for n, a in arrays.items()}], core_ids=[0])
    return np.ascontiguousarray(r.results[0]["out_0"].T).reshape(B, S, D)
```
